# Optimizing a Trainium2 kernel written in Bass

```python
import numpy as np
import jax
import jax.numpy as jnp

def _softmax(x, axis=-1):
    return jax.nn.softmax(x, axis=axis)

def _gelu(x):
    return jax.nn.gelu(x, approximate=True)

def _silu(x):
    return jax.nn.silu(x)

def _sigmoid(x):
    return jax.nn.sigmoid(x)

def _layernorm(x, axis=-1, eps=1e-05):
    m = jnp.mean(x, axis=axis, keepdims=True)
    v = jnp.var(x, axis=axis, keepdims=True)
    return (x - m) / jnp.sqrt(v + eps)

def _scatter_add(tgt, idx, src, axis=0):
    return tgt.at[idx].add(src)

def _segment_sum(src, seg, n):
    return jax.ops.segment_sum(src, seg, n)
kernel_name = 'mk_conv_attn_hybrid_d2_conv_nchw128_r2_bd0cf8'

def setup_inputs(seed: int=0):
    np.random.seed(seed)
    _w = jnp.asarray

    def _rec_inputs():
        import jax
        import jax.numpy as jnp
        _gk = jax.random.key(seed)
        x = -0.0002023 + 1 * jax.random.normal(jax.random.fold_in(_gk, 1), (16, 64, 56, 56), jnp.float32)
        return x
    x = _rec_inputs()

    def _L0_conv_setup():
        import math
        import jax, jax.numpy as jnp
        import numpy as np
        from jax import lax
        N, C, H, W = (16, 64, 56, 56)

        def _conv(x, w, padding, dilation=(1, 1), groups=1):
            return lax.conv_general_dilated(x, w, window_strides=(1, 1), padding=[(padding[0], padding[0]), (padding[1], padding[1])], rhs_dilation=dilation, dimension_numbers=('NCHW', 'OIHW', 'NCHW'), feature_group_count=groups)
        key = jax.random.key(seed)
        ks = jax.random.split(key, 6)
        x = jax.random.normal(ks[0], (N, C, H, W), jnp.float32)
        w2 = jax.random.normal(ks[1], (C, C, 1, 3), jnp.float32) * 0.05
        p6w = jax.random.normal(ks[2], (1, C, 7, 1), jnp.float32) * 0.02
        w7 = jax.random.normal(ks[3], (C, 1, 1, 5), jnp.float32) * 0.05
        w8 = jax.random.normal(ks[4], (C, 1, 5, 5), jnp.float32) * 0.05
        p9w = jax.random.normal(ks[5], (1, 1, 7, C), jnp.float32) * 0.02
        return {'x': x, 'w2': w2, 'p6w': p6w, 'w7': w7, 'w8': w8, 'p9w': p9w}
    _L0_conv_all = _L0_conv_setup()
    _L0_conv_in = {k: v for k, v in _L0_conv_all.items() if k in ('w2', 'p6w', 'w7', 'w8', 'p9w')}
    del _L0_conv_all

    def _L1_attn_setup():
        import jax, jax.numpy as jnp
        import numpy as np
        B, S, D, H = (4, 2048, 64, 16)
        DH = D * H
        key = jax.random.key(seed)
        ks = jax.random.split(key, 10)
        sc = lambda fan: 1.0 / np.sqrt(fan)
        return {'x': jax.random.normal(ks[0], (B, S, D), jnp.float32), 'mask': jnp.ones((B, S), jnp.bool_), 'wq_w': jax.random.normal(ks[1], (DH, D), jnp.float32) * sc(D), 'wq_b': jax.random.normal(ks[2], (DH,), jnp.float32) * 0.01, 'wk_w': jax.random.normal(ks[3], (DH, D), jnp.float32) * sc(D), 'wk_b': jax.random.normal(ks[4], (DH,), jnp.float32) * 0.01, 'wv_w': jax.random.normal(ks[5], (DH, D), jnp.float32) * sc(D), 'wv_b': jax.random.normal(ks[6], (DH,), jnp.float32) * 0.01, 'dense_w': jax.random.normal(ks[7], (D, DH), jnp.float32) * sc(DH), 'dense_b': jax.random.normal(ks[8], (D,), jnp.float32) * 0.01}
    _L1_attn_all = _L1_attn_setup()
    _L1_attn_in = {k: v for k, v in _L1_attn_all.items() if k in ('mask', 'wq_w', 'wq_b', 'wk_w', 'wk_b', 'wv_w', 'wv_b', 'dense_w', 'dense_b')}
    del _L1_attn_all

    def _L1_ffn_setup():
        import jax, jax.numpy as jnp
        import numpy as np
        B, S, D, E, H, O, K = (256, 1024, 64, 32, 256, 64, 8)
        key = jax.random.key(seed)
        k0, k1, k2, k3 = jax.random.split(key, 4)
        x = jax.random.normal(k0, (B, S, D), dtype=jnp.float32)
        gate_w = jax.random.normal(k1, (E, D), dtype=jnp.float32) * (1.0 / np.sqrt(D))
        gate_b = jnp.zeros((E,), dtype=jnp.float32)
        weight1 = jax.random.uniform(k2, (E, D + 1, H), dtype=jnp.float32, minval=-1.0, maxval=1.0) * (1.0 / np.sqrt(D + 1))
        weight2 = jax.random.uniform(k3, (E, H + 1, O), dtype=jnp.float32, minval=-1.0, maxval=1.0) * (1.0 / np.sqrt(H + 1))
        return {'x': x, 'gate_w': gate_w, 'gate_b': gate_b, 'weight1': weight1, 'weight2': weight2}
    _L1_ffn_all = _L1_ffn_setup()
    _L1_ffn_in = {k: v for k, v in _L1_ffn_all.items() if k in ('gate_w', 'gate_b', 'weight1', 'weight2')}
    del _L1_ffn_all
    return {'x': x, 'L0_conv_w2': _L0_conv_in['w2'], 'L0_conv_p6w': _L0_conv_in['p6w'], 'L0_conv_w7': _L0_conv_in['w7'], 'L0_conv_w8': _L0_conv_in['w8'], 'L0_conv_p9w': _L0_conv_in['p9w'], 'L1_attn_mask': _L1_attn_in['mask'], 'L1_attn_wq_w': _L1_attn_in['wq_w'], 'L1_attn_wq_b': _L1_attn_in['wq_b'], 'L1_attn_wk_w': _L1_attn_in['wk_w'], 'L1_attn_wk_b': _L1_attn_in['wk_b'], 'L1_attn_wv_w': _L1_attn_in['wv_w'], 'L1_attn_wv_b': _L1_attn_in['wv_b'], 'L1_attn_dense_w': _L1_attn_in['dense_w'], 'L1_attn_dense_b': _L1_attn_in['dense_b'], 'L1_ffn_gate_w': _L1_ffn_in['gate_w'], 'L1_ffn_gate_b': _L1_ffn_in['gate_b'], 'L1_ffn_weight1': _L1_ffn_in['weight1'], 'L1_ffn_weight2': _L1_ffn_in['weight2']}

def reference(x, L0_conv_w2, L0_conv_p6w, L0_conv_w7, L0_conv_w8, L0_conv_p9w, L1_attn_mask, L1_attn_wq_w, L1_attn_wq_b, L1_attn_wk_w, L1_attn_wk_b, L1_attn_wv_w, L1_attn_wv_b, L1_attn_dense_w, L1_attn_dense_b, L1_ffn_gate_w, L1_ffn_gate_b, L1_ffn_weight1, L1_ffn_weight2):
    import jax
    import jax.numpy as jnp

    def _L0_conv_ref(x, w2, p6w, w7, w8, p9w):
        import math
        import jax, jax.numpy as jnp
        import numpy as np
        from jax import lax
        N, C, H, W = (16, 64, 56, 56)

        def _conv(x, w, padding, dilation=(1, 1), groups=1):
            return lax.conv_general_dilated(x, w, window_strides=(1, 1), padding=[(padding[0], padding[0]), (padding[1], padding[1])], rhs_dilation=dilation, dimension_numbers=('NCHW', 'OIHW', 'NCHW'), feature_group_count=groups)
        n, c, h, w = x.shape
        xp = jnp.pad(x, ((0, 0), (0, 0), (0, 0), (6, 6)))
        t1 = jnp.stack([xp[..., 2 * k:2 * k + w] for k in range(7)], axis=2)
        t2 = _conv(x, w2, (0, 1))
        t3 = jnp.einsum('nakhw,nbhw->nakb', t1, x) / math.sqrt(h * w)
        t2p = jnp.pad(t2, ((0, 0), (0, 0), (3, 3), (0, 0)))
        t4 = jnp.stack([t2p[:, :, k:k + h, :] for k in range(7)], axis=2)
        t6 = p6w * t3
        t7 = _conv(t2, w7, (0, 2), groups=c)
        t8 = _conv(x, w8, (4, 4), dilation=(2, 2), groups=c)
        t9 = p9w * t6
        t10 = jnp.einsum('nakb,nakhw->nbhw', t9, t4) / math.sqrt(c * 7)
        t11 = t10 - t7
        t12 = t8 - t11
        return t12

    def _L1_attn_ref(x, mask, wq_w, wq_b, wk_w, wk_b, wv_w, wv_b, dense_w, dense_b):
        import jax, jax.numpy as jnp
        import numpy as np
        B, S, D, H = (4, 2048, 64, 16)
        DH = D * H
        b, s, d = x.shape
        h = wq_w.shape[0] // d
        q = (x @ wq_w.T + wq_b).reshape(b, s, h, d)
        k = (x @ wk_w.T + wk_b).reshape(b, s, h, d)
        v = (x @ wv_w.T + wv_b).reshape(b, s, h, d)
        q = jax.nn.elu(q) + 1.0
        k = jax.nn.elu(k) + 1.0
        pos = 1.57 * jnp.arange(s, dtype=x.dtype) / s
        cos = jnp.cos(pos)[None, :, None, None]
        sin = jnp.sin(pos)[None, :, None, None]
        q_cos, q_sin = (q * cos, q * sin)
        k_cos, k_sin = (k * cos, k * sin)
        kv_cos = jnp.einsum('bshx,bshz->bhxz', k_cos, v)
        kv_sin = jnp.einsum('bshx,bshz->bhxz', k_sin, v)
        qkv = jnp.einsum('bshx,bhxz->bshz', q_cos, kv_cos) + jnp.einsum('bshx,bhxz->bshz', q_sin, kv_sin)
        denom = 1.0 / (jnp.einsum('bshd,bhd->bsh', q_cos, k_cos.sum(axis=1)) + jnp.einsum('bshd,bhd->bsh', q_sin, k_sin.sum(axis=1)) + 1e-05)
        o = qkv * denom[..., None]
        concat = o.reshape(b, s, h * d)
        return concat @ dense_w.T + dense_b

    def _L1_ffn_ref(x, gate_w, gate_b, weight1, weight2):
        import jax, jax.numpy as jnp
        import numpy as np
        B, S, D, E, H, O, K = (256, 1024, 64, 32, 256, 64, 8)
        Bn, Sn, Dn = x.shape
        logits = jnp.einsum('bsd,ed->bse', x, gate_w) + gate_b
        probs = jax.nn.softmax(logits, axis=1)
        vals, idx = jax.lax.top_k(probs.transpose(0, 2, 1), K)
        topv = vals.transpose(0, 2, 1)
        topi = idx.transpose(0, 2, 1)
        flat_idx = topi.reshape(Bn, K * E)
        gathered = jnp.take_along_axis(x, flat_idx[:, :, None], axis=1)
        gathered = gathered.reshape(Bn, K, E, Dn)
        pooled = jnp.einsum('bked,bke->bed', gathered, topv)
        ones = jnp.ones((E, Bn, 1), dtype=x.dtype)
        h = jnp.concatenate([pooled.transpose(1, 0, 2), ones], axis=-1)
        h = jax.nn.gelu(jnp.einsum('ebd,edh->ebh', h, weight1), approximate=False)
        h = jnp.concatenate([h, ones], axis=-1)
        out = jnp.einsum('ebh,eho->ebo', h, weight2)
        out = out.transpose(1, 0, 2)
        weighted = jnp.einsum('beo,bke->bkeo', out, topv).reshape(Bn, K * E, O)
        outputs = jnp.zeros((Bn, Sn, O), dtype=x.dtype)
        outputs = outputs.at[jnp.arange(Bn)[:, None], flat_idx].add(weighted)
        return outputs

    def _gn(v, G=32, eps=1e-05):
        B_, C_, H_, W_ = v.shape
        g = v.reshape(B_, G, C_ // G, H_, W_)
        m = jnp.mean(g, axis=(2, 3, 4), keepdims=True)
        s = jnp.var(g, axis=(2, 3, 4), keepdims=True)
        return ((g - m) / jnp.sqrt(s + eps)).reshape(v.shape)

    def _ln_c(v, eps=1e-06):
        m = jnp.mean(v, axis=1, keepdims=True)
        s = jnp.var(v, axis=1, keepdims=True)
        return (v - m) / jnp.sqrt(s + eps)

    def _ln_t(v, eps=1e-05):
        m = jnp.mean(v, axis=-1, keepdims=True)
        s = jnp.var(v, axis=-1, keepdims=True)
        return (v - m) / jnp.sqrt(s + eps)

    def _to_tokens(v):
        B_, C_, H_, W_ = v.shape
        return v.reshape(B_, C_, H_ * W_).transpose(0, 2, 1)

    def _from_tokens(t, like):
        B_, C_, H_, W_ = like.shape
        return t.transpose(0, 2, 1).reshape(B_, C_, H_, W_)
    x = x + _L0_conv_ref(_gn(x), L0_conv_w2, L0_conv_p6w, L0_conv_w7, L0_conv_w8, L0_conv_p9w)
    t = _to_tokens(x)
    t = t + _L1_attn_ref(_ln_t(t), L1_attn_mask, L1_attn_wq_w, L1_attn_wq_b, L1_attn_wk_w, L1_attn_wk_b, L1_attn_wv_w, L1_attn_wv_b, L1_attn_dense_w, L1_attn_dense_b)
    t = t + _L1_ffn_ref(_ln_t(t), L1_ffn_gate_w, L1_ffn_gate_b, L1_ffn_weight1, L1_ffn_weight2)
    x = _from_tokens(t, x)
    return x

_drawn_inputs = setup_inputs


def setup_inputs(seed=0):
    import zlib

    import numpy as np

    out = dict(_drawn_inputs(seed))
    spreads = {'L1_ffn_gate_b': (0.0, 2.0)}
    factors = {'L0_conv_p6w': 8.0,
     'L0_conv_p9w': 8.0,
     'L1_attn_wq_w': 8.0,
     'L1_attn_wq_b': 200.0,
     'L1_attn_wk_w': 4.785,
     'L1_attn_wk_b': 200.0,
     'L1_attn_wv_w': 2.706,
     'L1_attn_wv_b': 5.893,
     'L1_attn_dense_b': 6.16,
     'L1_ffn_gate_w': 8.0,
     'L1_ffn_weight1': 8.0,
     'L1_ffn_weight2': 8.0}
    for name, (base, spread) in spreads.items():
        noise = np.random.default_rng([zlib.crc32(name.encode()), seed]).standard_normal(out[name].shape)
        drawn = base * np.exp(spread * noise) if base else spread * noise
        out[name] = jnp.asarray(drawn.astype(out[name].dtype))
    for name, factor in factors.items():
        out[name] = (out[name] * factor).astype(out[name].dtype)
    return out
```

```python
import concourse.bass as bass
from concourse import mybir
from contextlib import ExitStack

F32, F16, BF16 = mybir.dt.float32, mybir.dt.float16, mybir.dt.bfloat16
ALU = mybir.AluOpType
ACT = mybir.ActivationFunctionType
AX = mybir.AxisListType

P = 128
IMAGES, C, H, W = 16, 64, 56, 56
S = H * W
PAIRS = IMAGES // 2
HEADS = 16
FEAT = HEADS * C
NCHUNK = FEAT // P
ROWS = 8
PIX = ROWS * W
NPIX = S // PIX
TILES = (S + P - 1) // P
LAST = S - (TILES - 1) * P
GROUP = 8
GROUPS = [(g, min(GROUP, TILES - g)) for g in range(0, TILES, GROUP)]
SUB = PIX // 4
STEPS = 2 * NPIX
EXPERTS, HIDDEN = 32, 256
PADH, PITCH = H + 8, W + 6
GSIZE = 4 + PADH * PITCH + 8
PADH2, PADW2 = H + 6, W + 4
SPLIT = PITCH // 2
COLS = SPLIT + 6
HALFP = 2 * H
COLGROUPS = [(g, min(GROUP, COLS - g)) for g in range(0, COLS, GROUP)]
DROWS = C + HEADS
LN_EPS, GN_EPS, DEN_EPS = 1e-5, 1e-5, 1e-5


def tile_rows(t):
    return LAST if t == TILES - 1 else P


class Signal:

    def __init__(self, sem, per_pair, setup=0, unit=1):
        self.sem, self.per, self.setup, self.unit = sem, per_pair, setup, unit

    def first(self, n):
        return self.sem, n * self.unit

    def at(self, pair, n):
        return self.sem, pair * (self.per * self.unit) + (self.setup + n) * self.unit

    def after(self, n):
        return self.sem, (self.setup + PAIRS * self.per + n) * self.unit


def program(nc, x, w2, p6w, w7, w8, p9w, wq_w, wq_b, wk_w, wk_b, wv_w, wv_b, dense_w, dense_b,
            gate_w, gate_b, weight1, weight2, ident_c, avg_c, mask_c, cst_c, cs_c,
            out, t_keep, w_keep, o_keep):
    ctx = ExitStack()
    with ctx:
        ctx.enter_context(nc.allow_non_contiguous_dma(reason="small weights"))

        def sb(name, shape, dtype=F32):
            return ctx.enter_context(nc.sbuf_tensor(name, shape, dtype))

        def signal(name, per_pair=0, setup=0, unit=1):
            return Signal(ctx.enter_context(nc.semaphore(name)), per_pair, setup, unit)

        arena = sb("arena", [P, S + GSIZE + PADH2 * PADW2 + COLS * P])
        at0 = 0

        def carve(n):
            nonlocal at0
            at0 += n
            return arena[:, at0 - n:at0]

        X = carve(S)
        G = carve(GSIZE)

        def g_window(row, col, rows):
            at = 4 + row * PITCH + col
            return G[:, at:at + rows * PITCH].rearrange("p (h w) -> p h w", w=PITCH)[:, :, 0:W]

        T2 = carve(PADH2 * PADW2).rearrange("p (h w) -> p h w", w=PADW2)
        cols_flat = carve(COLS * P)
        UCOL = cols_flat.rearrange("p (j c) -> p j c", c=P)
        E = cols_flat[:, 0:2 * FEAT].rearrange("p (b f) -> p b f", b=2)
        KT = cols_flat[:, 2 * FEAT:4 * FEAT].rearrange("p (b f) -> p b f", b=2)
        EW = cols_flat[0:C, 0:S]

        Y = sb("Y", [P, S])
        R1 = sb("R1", [P, NCHUNK * PIX])
        R2 = sb("R2", [P, NCHUNK * PIX])
        YT = R1[:, 0:TILES * P].rearrange("p (t c) -> p t c", c=P)
        YG = R1[:, 0:TILES * P].rearrange("p (g c) -> p g c", c=C)
        SQ = R2[:, 0:TILES * P].rearrange("p (g c) -> p g c", c=C)
        UHL = R2[:, 0:TILES * P].bitcast(F16).rearrange("p (g s c) -> p g s c", s=2, c=C)
        Q = [r[:, :].rearrange("p (c n) -> p c n", n=PIX) for r in (R1, R2)]
        LG = R2[0:C, 0:S]
        plane = sb("plane", [P, S])
        UTS = [plane[:, i * S // 2:(i + 1) * S // 2].bitcast(F16) for i in range(2)]
        U2 = plane[:, :]
        small = sb("small", [P, 4 * FEAT + 2 * NCHUNK * DROWS])
        AT = [small[:, i * FEAT:(i + 1) * FEAT] for i in range(2)]
        MW = [small[:, (2 + i) * FEAT:(3 + i) * FEAT].rearrange("p (c o) -> p c o", o=P) for i in range(2)]
        KKF = [small[:, 4 * FEAT + i * NCHUNK * DROWS:4 * FEAT + (i + 1) * NCHUNK * DROWS] for i in range(2)]
        KK = [k.rearrange("p (c m) -> p c m", m=DROWS) for k in KKF]
        L2 = small[0:C, 0:S]
        WT = small[:, S + 32:S + 32 + TILES * C].rearrange("p (t e) -> p t e", e=C)
        EQ = sb("EQ", [P, 2, PIX])

        WKH, WKL, WQH, WQL = (sb(n, [P, FEAT], F16) for n in ("WKH", "WKL", "WQH", "WQL"))
        BD = sb("BD", [P, HEADS, P + 2])
        D8 = sb("D8", [P, 25, P])
        D7 = sb("D7", [P, 5, P])
        W2T = sb("W2T", [P, 3, P])
        P9T = sb("P9T", [P, 7, P])
        L10 = sb("L10", [P, 7, P])
        SELB = sb("SELB", [P, 4, HEADS, C], BF16)
        CST = sb("CST", [P, S])
        CS = sb("CS", [P, TILES, 2])
        IDN = sb("IDN", [P, P])
        IDH = sb("IDH", [P, P], F16)
        AVG = sb("AVG", [P, P])
        SEL = sb("SEL", [P, 2, HEADS])
        FOLD = sb("FOLD", [P, C])
        GWT = sb("GWT", [P, C])
        UA = sb("UA", [P, 2, 2, C])
        DS = sb("DS", [DROWS, PIX])
        OS = sb("OS", [P, PIX])
        RR = sb("RR", [P, 2, SUB])
        RS3 = sb("RS3", [P, 3, SUB], BF16)
        PT = sb("PT", [C + 1, EXPERTS, IMAGES])
        P6 = sb("P6", [P, 7])
        W8C = sb("W8C", [P, 25])
        W7C = sb("W7C", [P, 5])
        DBC = sb("DBC", [P, 1])
        GBC = sb("GBC", [C, 1])
        EPS = sb("EPS", [P, 1])
        NEG1 = sb("NEG1", [P, 1])
        BS = sb("BS", [P, NPIX, 6])
        MV = sb("MV", [P, 8])
        ST = sb("ST", [P, 4, 2 * TILES])
        MX = sb("MX", [C, 12])

        ps = {a: ctx.enter_context(nc.psum_tensor(f"ps_{a}", [P, 512 * (2 if a in "ABC" else 1)], F32))
              for a in "ABCDE"}

        turn = [0]

        def misc():
            turn[0] += 1
            return "ABC"[turn[0] % 3]

        setup_uses = [(k, misc()) for k in ("wk", "wq", "wd", "vd", "w2", "gw")]
        pair_uses = [("gmean", misc()), ("gvar", misc())]
        pair_uses += [(("t2", n), misc()) for n in range(NPIX)]
        pair_uses += [(("ucol", g), misc()) for g in range(len(COLGROUPS))]
        pair_uses += [("t3", "D"), ("t3t", misc())]
        pair_uses += [(("conv", n), misc()) for n in range(NPIX)]
        pair_uses += [(("yt", g), misc()) for g in range(len(GROUPS))]
        pair_uses += [(("uts", i, g), misc()) for i in range(2) for g in range(len(GROUPS))]
        for i in range(2):
            pair_uses += [(("kp", i, t), "AB"[t % 2]) for t in range(TILES)]
            pair_uses += [(("kv", 0, 0), "C")] if i == 0 else [(("kv", 1, 0), "D"), (("kv", 1, 1), "E")]
        pair_uses += [(("m", i, g), misc()) for i in range(2) for g in range(2)]
        for s in range(STEPS):
            pair_uses += [(("qp", s, cc), "AB"[cc % 2]) for cc in range(4)]
            pair_uses += [(("den", s), "E"), (("dsum", s), "C")]
            pair_uses += [(("rb", s, cc), "C") for cc in range(4)] + [(("out", s), "D"), (("fold", s), "C")]
        pair_uses += [(("yt2", g), misc()) for g in range(len(GROUPS))]
        pair_uses += [(("u2", g), misc()) for g in range(len(GROUPS))]
        pair_uses += [(("lg", n), misc()) for n in range(NPIX)]
        pair_uses += [(("wt", g), misc()) for g in range(2)] + [("pool", "D")]
        final_uses = [("hid", "A")] + [(("eo", g), "BC"[g % 2]) for g in range(2)]
        final_uses += [(("add", q, n), "ABC"[(q * NPIX + n) % 3]) for q in range(PAIRS) for n in range(NPIX)]
        order = {}
        totals = {}
        for phase, uses in (("setup", setup_uses), ("pair", pair_uses), ("final", final_uses)):
            count = dict.fromkeys("ABCDE", 0)
            for key, a in uses:
                count[a] += 1
                order[key] = (a, phase, count[a])
            totals[phase] = count
        filled_s = {a: signal(f"ps_{a}_filled", totals["pair"][a], totals["setup"][a]) for a in "ABCDE"}
        emptied_s = {a: signal(f"ps_{a}_emptied", totals["pair"][a], totals["setup"][a] + (a in "DE"))
                     for a in "ABCDE"}

        def value(signals, key, pair, less):
            a, phase, n = order[key]
            sig = signals[a]
            if phase == "setup":
                return sig.first(n - less)
            return sig.at(pair, n - less) if phase == "pair" else sig.after(n - less)

        def room(key, pair=None):
            return value(emptied_s, key, pair, 1)

        def filled(key, pair=None):
            return value(filled_s, key, pair, 0)

        def emptied(key, pair=None):
            return value(emptied_s, key, pair, 0)

        def last_uses(which, keys, pair=None):
            return list({order[k][0]: which(k, pair) for k in keys}.values())

        def products_done(k, pair):
            i, t = divmod(k, TILES)
            if t == TILES - 1:
                return filled(("kv", i, i), pair)
            return kv_used.at(pair, k + 1 - i)

        def passed(eng):
            eng.sem_inc(waits_passed.sem, 1)

        def area(key):
            return ps[order[key][0]]

        def fill(key):
            return filled_s[order[key][0]].sem, 1

        def empty(key):
            return emptied_s[order[key][0]].sem, 1

        loaded = signal("loaded", setup=1, unit=16 * 27)
        zeroed = signal("zeroed", setup=1)
        vstep = signal("vstep", per_pair=VSTEPS, setup=VSETUP)
        prepared = signal("prepared", setup=4)
        x_loaded = signal("x_loaded", 1, unit=16)
        stats = signal("stats", NPIX)
        gn_sums = signal("gn_sums", 1)
        g_ready = signal("g_ready", 1)
        centred1 = signal("centred1", 1, setup=1)
        centred2 = signal("centred2", 1)
        squared = signal("squared", 2)
        sums = signal("sums", 2)
        std = signal("std", 2)
        un_ready = signal("un_ready", 2)
        u_high = signal("u_high", 1)
        u_split = signal("u_split", 1)
        ua_ready = signal("ua_ready", 2 * TILES)
        e_ready = signal("e_ready", 2 * TILES)
        kv_used = signal("kv_used", 2 * (TILES - 1))
        eq_ready = signal("eq_ready", 4 * STEPS)
        gstep = signal("gstep", 3 * STEPS)
        split_ready = signal("split_ready", STEPS)
        t_stored = signal("t_stored", 1, setup=1, unit=16)
        lmax_ready = signal("lmax_ready", 1)
        l2_ready = signal("l2_ready", 1)
        exp_ready = signal("exp_ready", 2)
        w_ready = signal("w_ready", 1)
        w_stored = signal("w_stored", 1, unit=16)
        experts_loaded = signal("experts_loaded", unit=16 * 3)
        o_stored = signal("o_stored", unit=16)
        waits_passed = signal("waits_passed")
        ones_ready = signal("ones_ready")
        od_zeroed = signal("od_zeroed")
        od_loaded = signal("od_loaded", unit=32)
        last_t = [signal(f"last_t{b}", unit=16) for b in range(2)]
        last_w = [signal(f"last_w{b}", unit=16) for b in range(2)]
        last_out = [signal(f"last_out{b}", unit=16) for b in range(2)]

        x_v = x.rearrange("n c h w -> (n c) (h w)")
        out_v = out.rearrange("n c h w -> (n c) (h w)")

        WNAT = {n: v[:, 0:NCHUNK * P].rearrange("p (c s d) -> p c s d", s=2, d=C)
                for n, v in (("k", R1), ("q", R2), ("v", plane))}
        WB = {n: v[:, NCHUNK * P:NCHUNK * P + NCHUNK] for n, v in (("k", R1), ("q", R2), ("v", plane))}
        DN = Y[0:C, 0:FEAT]
        W2N = Y[:, FEAT:FEAT + 3 * C].rearrange("p (i k) -> p i k", k=3)
        W2B = Y[:, 1216:1216 + 3 * P].rearrange("p (k s i) -> p k s i", k=3, s=2)
        GWB = Y[0:C, 1600:1600 + P]
        P9N = Y[:, 1728:1728 + 7 * C].rearrange("p (k b) -> p k b", k=7)
        MASK = Y[:, 2176:2176 + P]
        WDT = Y[:, 2304:2304 + NCHUNK * C].rearrange("p (c o) -> p c o", o=C)

        n1, n2 = EXPERTS * HIDDEN, 2 * EXPERTS * C
        W1S = arena[0:C + 1, 0:n1].rearrange("p (e h) -> p e h", h=HIDDEN)
        W2S = arena[:, n1:n1 + n2].rearrange("p (a e o) -> p a e o", a=2, o=C)
        B2S = arena[0:1, n1 + n2:n1 + n2 + EXPERTS * C].rearrange("p (e o) -> p e o", o=C)
        HID = R1[:, 0:2 * EXPERTS * IMAGES].rearrange("p (a e b) -> p a e b", a=2, b=IMAGES)
        EO = R2[0:IMAGES, 0:EXPERTS * C].rearrange("p (e o) -> p e o", o=C)
        ONES = R2[0:1, EXPERTS * C:EXPERTS * C + IMAGES]
        OD = small[0:C, 0:PAIRS * P].rearrange("p (q o) -> p q o", o=P)
        LT = [Y[:, :], arena[:, 0:S]]
        LW = [plane[0:C, :], CST[0:C, :]]

        block = ctx.enter_context(nc.Block())

        @block.sync
        def _(sp):
            loads = [(IDN[:], ident_c), (AVG[:], avg_c), (MASK, mask_c), (CST[:], cst_c), (CS[:], cs_c)]
            for n, w, b in (("k", wk_w, wk_b), ("q", wq_w, wq_b), ("v", wv_w, wv_b)):
                loads += [(WNAT[n][:, :, 0, :], w.rearrange("(c p) d -> p c d", p=P)),
                          (WB[n], b.rearrange("(c p) -> p c", p=P))]
            loads += [(DN, dense_w)]
            for i in range(2):
                half = slice(i * C, (i + 1) * C)
                loads += [(W2N[half], w2.rearrange("o i a k -> o i (a k)")),
                          (P6[half], p6w.rearrange("a c k b -> c (a k b)")),
                          (W8C[half], w8.rearrange("c a k l -> c (a k l)")),
                          (W7C[half], w7.rearrange("c a b k -> c (a b k)")),
                          (DBC[half], dense_b.rearrange("(c a) -> c a", a=1)),
                          (GBC[i * EXPERTS:(i + 1) * EXPERTS], gate_b.rearrange("(e a) -> e a", a=1))]
            loads += [(P9N, bass.AP(p9w.tensor, p9w.offset, [[0, P], [C, 7], [1, C]]))]
            sp.sem_inc(t_stored.sem, 16)
            for dst, src in loads:
                sp.dma_start(dst, src).then_inc(loaded.sem, 16)
            sp.wait_ge(*zeroed.first(1))
            for i in range(2):
                sp.dma_start(GWB[i * EXPERTS:(i + 1) * EXPERTS, i * C:(i + 1) * C],
                             gate_w).then_inc(loaded.sem, 16)
            assert len(loads) + 2 == loaded.unit // 16, len(loads)
            with sp.Fori(0, PAIRS) as pair:
                sp.wait_ge(*centred1.at(pair, 0))
                sp.dma_start(X, x_v[bass.ds(pair * P, P), :]).then_inc(x_loaded.sem, 16)
                sp.wait_ge(*emptied(("fold", STEPS - 1), pair))
                sp.dma_start(t_keep[bass.ds(pair * P, P), :], Y[:, :]).then_inc(t_stored.sem, 16)
                sp.wait_ge(*w_ready.at(pair, 1))
                sp.dma_start(w_keep[bass.ds(pair * C, C), :], EW).then_inc(w_stored.sem, 16)

            sp.wait_ge(*w_stored.after(0))
            sp.wait_ge(*emptied("pool", PAIRS - 1))
            sp.dma_start(W1S, weight1.rearrange("e d h -> d e h")).then_inc(experts_loaded.sem, 16)
            for a in range(2):
                sp.dma_start(W2S[:, a], weight2[:, a * P:(a + 1) * P, :].rearrange("e h o -> h e o"))\
                    .then_inc(experts_loaded.sem, 16)
            sp.dma_start(B2S, weight2[:, HIDDEN:HIDDEN + 1, :].rearrange("e a o -> a e o"))\
                .then_inc(o_stored.sem, 16)
            for w in last_uses(emptied, [("eo", 0), ("eo", 1)]):
                sp.wait_ge(*w)
            sp.dma_start(o_keep, EO).then_inc(o_stored.sem, 16)
            sp.wait_ge(*o_stored.after(2))
            sp.wait_ge(*od_zeroed.after(1))
            o_v = o_keep.rearrange("(q i) e o -> i e q o", i=2)
            for i in range(2):
                sp.dma_start(OD[i * EXPERTS:(i + 1) * EXPERTS, :, i * C:(i + 1) * C],
                             o_v[i]).then_inc(od_loaded.sem, 16)
            for q in range(PAIRS):
                b = q % 2
                if q >= 2:
                    sp.wait_ge(*last_out[b].after(q // 2))
                    for w in last_uses(filled, [("add", q - 2, n) for n in range(NPIX)]):
                        sp.wait_ge(*w)
                else:
                    sp.wait_ge(*emptied("hid"))
                sp.wait_ge(*t_stored.after(0))
                sp.dma_start(LT[b], t_keep[q * P:(q + 1) * P, :]).then_inc(last_t[b].sem, 16)
                sp.dma_start(LW[b], w_keep[q * C:(q + 1) * C, :]).then_inc(last_w[b].sem, 16)
                if q >= 1:
                    for w in last_uses(emptied, [("add", q - 1, n) for n in range(NPIX)]):
                        sp.wait_ge(*w)
                    sp.dma_start(out_v[(q - 1) * P:q * P, :], LT[1 - b]).then_inc(last_out[1 - b].sem, 16)
            for w in last_uses(emptied, [("add", PAIRS - 1, n) for n in range(NPIX)]):
                sp.wait_ge(*w)
            sp.dma_start(out_v[(PAIRS - 1) * P:, :], LT[1]).then_inc(last_out[1].sem, 16)
            for b in range(2):
                sp.wait_ge(*last_out[b].after(PAIRS // 2))

        @block.gpsimd
        def _(pool):
            pool.memset(arena[:, :], 0.0)
            pool.memset(small[:, :], 0.0)
            pool.memset(BD[:, :, :], 0.0)
            pool.memset(W2B, 0.0)
            pool.memset(GWB, 0.0)
            pool.memset(PT[:, :, :], 1.0)
            pool.memset(EPS[:, :], GN_EPS)
            pool.memset(NEG1[:, :], -1.0).then_inc(zeroed.sem, 1)
            pool.wait_ge(*loaded.first(1))
            with pool.Fori(0, PAIRS) as pair:
                pool.wait_ge(*un_ready.at(pair, 1))
                for i in range(2):
                    for t in range(TILES):
                        k = i * TILES + t
                        if k >= 2:
                            pool.wait_ge(*products_done(k - 2, pair))
                        r = tile_rows(t)
                        pool.tensor_tensor(
                            out=UA[0:r, k % 2], op=ALU.mult,
                            in0=YG[0:r, 2 * t + i:2 * t + i + 1, :].broadcast_to([r, 2, C]),
                            in1=CS[0:r, t, :].unsqueeze(2).broadcast_to([r, 2, C]),
                        ).then_inc(ua_ready.sem, 1)
                for s in range(STEPS):
                    pool.wait_ge(*emptied(("dsum", s), pair))
                    if s >= 1:
                        pool.wait_ge(*filled(("rb", s - 1, 3), pair))
                    passed(pool)
                    pool.tensor_copy(RS3[:, 0], RR[:, 0]).then_inc(gstep.sem, 1)
                    pool.wait_ge(*gstep.at(pair, 3 * s + 1))
                    pool.tensor_tensor(out=RR[:, 1], in0=RR[:, 0], in1=RS3[:, 0], op=ALU.subtract)\
                        .then_inc(gstep.sem, 1)
                    pool.wait_ge(*gstep.at(pair, 3 * s + 2))
                    passed(pool)
                    pool.tensor_copy(RS3[:, 1], RR[:, 1]).then_inc(gstep.sem, 1)
                    pool.wait_ge(*gstep.at(pair, 3 * s + 3))
                    pool.tensor_tensor(out=RS3[:, 2], in0=RR[:, 1], in1=RS3[:, 1], op=ALU.subtract)\
                        .then_inc(split_ready.sem, 1)
            pool.wait_ge(*emptied("pool", PAIRS - 1))
            pool.memset(OD, 0.0).then_inc(od_zeroed.sem, 1)

        @block.scalar
        def _(act):
            act.wait_ge(*zeroed.first(1))
            act.wait_ge(*loaded.first(1))
            with act.Fori(0, PAIRS) as pair:
                act.wait_ge(*filled("gvar", pair))
                act.activation(MV[:, 6:7], area("gvar")[:, 0:1], ACT.Sqrt, bias=EPS[:, 0:1])\
                    .then_inc(*empty("gvar"))
                for n in range(NPIX):
                    act.wait_ge(*filled(("t2", n), pair))
                    act.activation(T2[:, 3 + n * ROWS:3 + (n + 1) * ROWS, 2:2 + W],
                                   area(("t2", n))[:, 0:PIX].rearrange("p (h w) -> p h w", w=W),
                                   ACT.Copy).then_inc(*empty(("t2", n)))
                for g, (j, m) in enumerate(COLGROUPS):
                    act.wait_ge(*filled(("ucol", g), pair))
                    act.activation(UCOL[0:HALFP, j:j + m, :],
                                   area(("ucol", g))[0:HALFP, 0:m * P].rearrange("p (j c) -> p j c", c=P),
                                   ACT.Copy).then_inc(*empty(("ucol", g)))

                def layer_norm(which, uses, centred):
                    for g, (t, m) in enumerate(GROUPS):
                        act.wait_ge(*filled((uses, g), pair))
                        r = P if m > 1 else LAST
                        act.activation(YT[0:r, t:t + m, :],
                                       area((uses, g))[0:r, 0:m * P].rearrange("p (t c) -> p t c", c=P),
                                       ACT.Copy).then_inc(*empty((uses, g)))
                    act.wait_ge(*centred.at(pair, 1))
                    act.activation(SQ, YG, ACT.Square).then_inc(squared.sem, 1)
                    act.wait_ge(*sums.at(pair, which))
                    act.activation(ST[:, 2, :], ST[:, 1, :], ACT.Sqrt, scale=1.0 / C, bias=EPS[:, 0:1])\
                        .then_inc(std.sem, 1)

                layer_norm(1, "yt", centred1)
                act.wait_ge(*un_ready.at(pair, 1))
                act.activation(UHL[:, :, 0, :], YG, ACT.Copy).then_inc(u_high.sem, 1)
                for i in range(2):
                    for g, (t, m) in enumerate(GROUPS):
                        key = ("uts", i, g)
                        n = m * P if m > 1 else LAST
                        act.wait_ge(*filled(key, pair))
                        act.activation(UTS[i][:, t * P:t * P + n], area(key)[:, 0:512].bitcast(F16)[:, 0:n],
                                       ACT.Copy).then_inc(*empty(key))
                for i in range(2):
                    for t in range(TILES):
                        k, r = i * TILES + t, tile_rows(t)
                        act.wait_ge(*filled(("kp", i, t), pair))
                        if k >= 2:
                            act.wait_ge(*emptied(("kp", *divmod(k - 2, TILES)), pair))
                        act.activation(E[0:r, k % 2], area(("kp", i, t))[0:r, :], ACT.Exp,
                                       bias=NEG1[0:r, 0:1]).then_inc(e_ready.sem, 1)
                    for b in range(1 + i):
                        key = ("kv", i, b)
                        wide = FEAT // (1 + i)
                        act.wait_ge(*filled(key, pair))
                        act.activation(AT[i][:, b * wide:(b + 1) * wide], area(key)[:, 0:wide], ACT.Copy)\
                            .then_inc(*empty(key))
                for s in range(STEPS):
                    for cc in range(4):
                        n = 4 * s + cc
                        key = ("qp", s, cc)
                        act.wait_ge(*filled(key, pair))
                        if n >= 1:
                            act.wait_ge(*emptied(("qp", *divmod(n - 1, 4)), pair))
                        act.activation(EQ[:, :, :], area(key)[:, :].rearrange("p (c n) -> p c n", c=2)[:, :, 0:PIX],
                                       ACT.Exp, bias=NEG1[:, 0:1]).then_inc(eq_ready.sem, 1)
                layer_norm(2, "yt2", centred2)
                for g, (t, m) in enumerate(GROUPS):
                    n = m * P if m > 1 else LAST
                    act.wait_ge(*filled(("u2", g), pair))
                    act.activation(U2[:, t * P:t * P + n], area(("u2", g))[:, 0:n], ACT.Copy)\
                        .then_inc(*empty(("u2", g)))
                for n in range(NPIX):
                    act.wait_ge(*filled(("lg", n), pair))
                    act.activation(LG[:, n * PIX:(n + 1) * PIX], area(("lg", n))[0:C, 0:PIX], ACT.Identity,
                                   bias=GBC[:, 0:1]).then_inc(*empty(("lg", n)))
                act.wait_ge(*lmax_ready.at(pair, 1))
                act.activation(EW, LG, ACT.Exp, bias=MX[:, 8:9], accum_out=MX[:, 9:10])\
                    .then_inc(exp_ready.sem, 1)
                act.wait_ge(*l2_ready.at(pair, 1))
                act.activation(L2, L2, ACT.Exp, bias=MX[:, 8:9]).then_inc(exp_ready.sem, 1)
                for g in range(2):
                    act.wait_ge(*filled(("wt", g), pair))
                    m = 16 if g == 0 else TILES - 16
                    act.activation(WT[:, 16 * g:16 * g + m, :],
                                   area(("wt", g))[:, 0:m * C].rearrange("p (t e) -> p t e", e=C), ACT.Copy)\
                        .then_inc(*empty(("wt", g)))
            act.wait_ge(*filled("hid"))
            act.activation(HID, area("hid")[:, :].rearrange("p (a e b) -> p a e b", a=2, b=IMAGES), ACT.Gelu)\
                .then_inc(*empty("hid"))

        @block.vector
        def _(dve):
            links = [0]
            now = [vstep.first]

            def link(ins):
                links[0] += 1
                ins.then_inc(vstep.sem, 1)
                dve.wait_ge(*now[0](links[0]))

            for s in (centred1, emptied_s["D"], emptied_s["E"]):
                dve.sem_inc(s.sem, 1)
            dve.wait_ge(*zeroed.first(1))
            dve.wait_ge(*loaded.first(1))
            for n, one in (("k", 1.0), ("q", 1.0), ("v", 0.0)):
                w = WNAT[n]
                link(dve.tensor_copy(ST[:, 0, 0:NCHUNK], w[:, :, 0, C - 1]))
                link(dve.tensor_tensor(out=w[:, :, 0, :], in0=w[:, :, 0, :], op=ALU.subtract,
                                       in1=ST[:, 0, 0:NCHUNK].unsqueeze(2).broadcast_to([P, NCHUNK, C])))
                link(dve.tensor_scalar(w[:, :, 0, C - 1], WB[n], one, None, ALU.add))
                dve.tensor_copy(w[:, :, 1, :], w[:, :, 0, :]).then_inc(prepared.sem, 1)
            for k in range(3):
                for i in range(2):
                    half = slice(i * C, (i + 1) * C)
                    link(dve.tensor_copy(W2B[half, k, i, :], W2N[half, :, k]))
            dve.tensor_copy(IDH[:, :], IDN[:, :]).then_inc(prepared.sem, 1)
            for d, w, m in ((D8, W8C, 25), (D7, W7C, 5)):
                link(dve.tensor_tensor(out=d[:, :, :], op=ALU.mult,
                                       in0=IDN[:, :].unsqueeze(1).broadcast_to([P, m, P]),
                                       in1=w[:, :].unsqueeze(2).broadcast_to([P, m, P])))
            for k in range(7):
                link(dve.tensor_tensor(out=P9T[:, k, :].rearrange("p (s b) -> p s b", s=2), op=ALU.mult,
                                       in0=MASK.rearrange("p (s b) -> p s b", s=2),
                                       in1=P9N[:, k, :].unsqueeze(1).broadcast_to([P, 2, C])))
            for j in range(4):
                link(dve.tensor_copy(SELB[:, j], IDN[:, 32 * j:32 * j + HEADS].unsqueeze(2)
                                     .broadcast_to([P, HEADS, C])))
            for d in range(2):
                link(dve.tensor_tensor(out=SEL[:, d, :], in0=IDN[:, 0:HEADS], in1=IDN[:, C:C + HEADS],
                                       op=ALU.add))
            link(dve.tensor_tensor(out=FOLD[:, :], in0=IDN[:, 0:C], in1=IDN[:, C:P], op=ALU.add))
            link(dve.tensor_copy(BD[:, :, P], IDN[:, C - 1:C].broadcast_to([P, HEADS])))
            link(dve.tensor_copy(BD[:, :, P + 1], IDN[:, P - 1:P].broadcast_to([P, HEADS])))
            for n, hi, lo in (("wk", WKH, WKL), ("wq", WQH, WQL)):
                dve.wait_ge(*filled(n))
                link(dve.tensor_copy(hi[:, :], area(n)[:, :]))
                dve.tensor_tensor(out=lo[:, :], in0=area(n)[:, :], in1=hi[:, :], op=ALU.subtract)\
                    .then_inc(*empty(n))
            dve.wait_ge(*filled("wd"))
            dve.tensor_copy(WDT, area("wd")[:, 0:NCHUNK * C].rearrange("p (c o) -> p c o", o=C))\
                .then_inc(*empty("wd"))
            dve.wait_ge(*filled("vd"))
            for s in range(2):
                vd = area("vd")[:, s * 512:(s + 1) * 512].rearrange("p (h o) -> p h o", o=C)
                link(dve.tensor_copy(BD[0:C, s:HEADS:2, 0:C], vd[0:C]))
                ins = dve.tensor_copy(BD[C:P, s:HEADS:2, C:P], vd[C:P])
            ins.then_inc(*empty("vd"))
            dve.wait_ge(*filled("w2"))
            dve.tensor_copy(W2T[:, :, :], area("w2")[:, 0:3 * P].rearrange("p (k o) -> p k o", k=3))\
                .then_inc(*empty("w2"))
            dve.wait_ge(*filled("gw"))
            link(dve.tensor_copy(GWT[:, :], area("gw")[:, 0:C]))
            link(dve.memset(R1[:, :], 0.0))
            dve.memset(R2[:, :], 0.0).then_inc(*empty("gw"))
            assert links[0] == VSETUP, links[0]

            with dve.Fori(0, PAIRS) as pair:
                links[0] = 0
                now[0] = lambda n: vstep.at(pair, n)
                dve.wait_ge(*emptied_s[order["gw"][0]].first(order["gw"][2]))

                dve.wait_ge(*x_loaded.at(pair, 1))
                for n in range(NPIX):
                    dve.bn_stats(out=BS[:, n, :], in_=X[:, n * PIX:(n + 1) * PIX]).then_inc(stats.sem, 1)
                dve.wait_ge(*stats.at(pair, NPIX))
                passed(dve)
                dve.bn_aggr(out=MV[:, 0:2], in_=BS[:, :, :]).then_inc(gn_sums.sem, 1)
                dve.wait_ge(*filled("gmean", pair))
                link(dve.tensor_copy(MV[:, 2:3], area("gmean")[:, 0:1]))
                link(dve.tensor_tensor(out=MV[:, 3:4], in0=MV[:, 0:1], in1=MV[:, 2:3], op=ALU.subtract))
                link(dve.tensor_tensor(out=MV[:, 4:5], in0=MV[:, 3:4], in1=MV[:, 3:4], op=ALU.mult))
                dve.tensor_tensor(out=MV[:, 5:6], in0=MV[:, 4:5], in1=MV[:, 1:2], op=ALU.add)\
                    .then_inc(*empty("gmean"))
                dve.wait_ge(*emptied("gvar", pair))
                link(dve.reciprocal(MV[:, 7:8], MV[:, 6:7]))
                dve.tensor_scalar(g_window(4, 0, H), X.rearrange("p (h w) -> p h w", w=W),
                                  MV[:, 2:3], MV[:, 7:8], ALU.subtract, ALU.mult).then_inc(g_ready.sem, 1)

                dve.wait_ge(*filled("t3", pair))
                t3 = area("t3")[:, :].rearrange("p (i c) -> p i c", i=4)
                link(dve.tensor_copy(OS[:, 0:3 * P], area("t3")[:, P:4 * P]))
                for i in range(4):
                    k = 3 - i
                    link(dve.scalar_tensor_tensor(out=L10[:, k, :], in0=t3[:, i, :], scalar=P6[:, k:k + 1],
                                                  in1=P9T[:, k, :], op0=ALU.mult, op1=ALU.mult))
                dve.tensor_tensor(out=L10[:, 3, :], in0=L10[:, 3, :], in1=D7[:, 2, :], op=ALU.add)\
                    .then_inc(*empty("t3"))
                dve.wait_ge(*filled("t3t", pair))
                for i in range(1, 4):
                    k = 3 + i
                    ins = dve.scalar_tensor_tensor(
                        out=L10[:, k, :], in0=area("t3t")[:, (i - 1) * P:i * P], scalar=P6[:, k:k + 1],
                        in1=P9T[:, k, :], op0=ALU.mult, op1=ALU.mult)
                    if i < 3:
                        link(ins)
                ins.then_inc(*empty("t3t"))

                dve.wait_ge(*t_stored.at(pair, 0))
                for n in range(NPIX):
                    dve.wait_ge(*filled(("conv", n), pair))
                    cut = slice(n * PIX, (n + 1) * PIX)
                    dve.tensor_tensor(out=Y[:, cut], in0=area(("conv", n))[:, 0:PIX], in1=X[:, cut],
                                      op=ALU.add).then_inc(*empty(("conv", n)))

                def layer_norm(which, uses, centred):
                    for w in last_uses(emptied, [(uses, g) for g in range(len(GROUPS))], pair):
                        dve.wait_ge(*w)
                    wide = [P, 2 * TILES, C]
                    link(dve.tensor_reduce(out=ST[:, 0, :], in_=YG, axis=AX.X, op=ALU.add))
                    link(dve.tensor_scalar(ST[:, 3, :], ST[:, 0, :], 1.0 / C, None, ALU.mult))
                    dve.tensor_tensor(out=YG, in0=YG, in1=ST[:, 3, :].unsqueeze(2).broadcast_to(wide),
                                      op=ALU.subtract).then_inc(centred.sem, 1)
                    dve.wait_ge(*squared.at(pair, which))
                    dve.tensor_reduce(out=ST[:, 1, :], in_=SQ, axis=AX.X, op=ALU.add).then_inc(sums.sem, 1)
                    dve.wait_ge(*std.at(pair, which))
                    link(dve.reciprocal(ST[:, 3, :], ST[:, 2, :]))
                    return dve.tensor_tensor(out=YG, in0=YG, op=ALU.mult,
                                             in1=ST[:, 3, :].unsqueeze(2).broadcast_to(wide))

                link(layer_norm(1, "yt", centred1))
                dve.memset(YG[:, :, C - 1:C], 1.0).then_inc(un_ready.sem, 1)
                dve.wait_ge(*u_high.at(pair, 1))
                dve.tensor_tensor(out=UHL[:, :, 1, :], in0=YG, in1=UHL[:, :, 0, :], op=ALU.subtract)\
                    .then_inc(u_split.sem, 1)

                for i in range(2):
                    for t in range(TILES):
                        k, r = i * TILES + t, tile_rows(t)
                        key = ("kp", i, t)
                        dve.wait_ge(*e_ready.at(pair, k + 1))
                        if k >= 2:
                            dve.wait_ge(*products_done(k - 2, pair))
                        dve.scalar_tensor_tensor(out=KT[0:r, k % 2], in0=E[0:r, k % 2], scalar=1.0,
                                                 in1=area(key)[0:r, :], op0=ALU.min, op1=ALU.max)\
                            .then_inc(*empty(key))
                for i in range(2):
                    for g in range(2):
                        key = ("m", i, g)
                        dve.wait_ge(*filled(key, pair))
                        m = area(key)[:, :].rearrange("p (c n) -> p c n", n=256)
                        dve.tensor_copy(MW[i][:, 4 * g:4 * g + 4, :], m[:, :, 0:P])
                        for hh in range(2):
                            for cs in range(2):
                                half = slice(hh * C, (hh + 1) * C)
                                first = 4 * g * (DROWS + 2) + cs * C + hh
                                ins = dve.tensor_copy(
                                    KKF[i][half, first:first + 3 * (DROWS + 2) + 1:DROWS + 2], m[half, :, P + cs])
                        ins.then_inc(*empty(key))
                def q_features(s, cc):
                    n, key = 4 * s + cc, ("qp", s, cc)
                    dve.wait_ge(*eq_ready.at(pair, n + 1))
                    if s >= 2 and cc == 0:
                        dve.wait_ge(*filled(("out", s - 2), pair))
                    dve.scalar_tensor_tensor(
                        out=Q[s % 2][:, 2 * cc:2 * cc + 2, :], in0=EQ[:, :, :], scalar=1.0,
                        in1=area(key)[:, :].rearrange("p (c n) -> p c n", c=2)[:, :, 0:PIX],
                        op0=ALU.min, op1=ALU.max).then_inc(*empty(key))

                def denominators(s):
                    n = s % NPIX
                    dve.wait_ge(*filled(("den", s), pair))
                    if s >= 1:
                        dve.wait_ge(*filled(("dsum", s - 1), pair))
                    dve.tensor_tensor(out=DS[:, :], in0=area(("den", s))[0:DROWS, 0:PIX],
                                      in1=CST[0:DROWS, n * PIX:(n + 1) * PIX], op=ALU.mult)\
                        .then_inc(*empty(("den", s)))
                    dve.wait_ge(*filled(("dsum", s), pair))
                    if s >= 1:
                        dve.wait_ge(*split_ready.at(pair, s))
                    link(dve.tensor_scalar(RR[:, 0], area(("dsum", s))[:, 0:SUB], DEN_EPS, None, ALU.add))
                    dve.reciprocal(RR[:, 0], RR[:, 0]).then_inc(*empty(("dsum", s)))

                def scale(s, cc):
                    key = ("rb", s, cc)
                    q = Q[s % 2][:, 2 * cc:2 * cc + 2, :]
                    dve.wait_ge(*filled(key, pair))
                    dve.tensor_tensor(out=q, in0=q, op=ALU.mult,
                                      in1=area(key)[:, :].rearrange("p (c n) -> p c n", c=2)[:, :, 0:PIX])\
                        .then_inc(*empty(key))

                def residual(s):
                    i, n = divmod(s, NPIX)
                    cut, half = slice(n * PIX, (n + 1) * PIX), slice(i * C, (i + 1) * C)
                    dve.wait_ge(*filled(("out", s), pair))
                    if s >= 1:
                        dve.wait_ge(*filled(("fold", s - 1), pair))
                    dve.tensor_tensor(out=OS[:, :], in0=area(("out", s))[:, 0:PIX], in1=CST[:, cut],
                                      op=ALU.mult).then_inc(*empty(("out", s)))
                    dve.wait_ge(*filled(("fold", s), pair))
                    dve.scalar_tensor_tensor(out=Y[half, cut], in0=area(("fold", s))[half, 0:PIX],
                                             scalar=DBC[half, 0:1], in1=Y[half, cut], op0=ALU.add, op1=ALU.add)\
                        .then_inc(*empty(("fold", s)))

                for s in range(STEPS + 1):
                    for cc in range(4):
                        if s < STEPS:
                            q_features(s, cc)
                        if s >= 1:
                            scale(s - 1, cc)
                    if s >= 1:
                        residual(s - 1)
                    if s < STEPS:
                        denominators(s)

                layer_norm(2, "yt2", centred2).then_inc(un_ready.sem, 1)

                for w in last_uses(emptied, [("lg", n) for n in range(NPIX)], pair):
                    dve.wait_ge(*w)
                passed(dve)
                link(dve.max(out=MX[:, 0:8], in_=LG))
                dve.tensor_scalar(MX[:, 8:9], MX[:, 0:1], -1.0, None, ALU.mult).then_inc(lmax_ready.sem, 1)
                dve.match_replace(out=L2, in_to_replace=MX[:, 0:8], in_values=LG, imm_value=LOW)\
                    .then_inc(l2_ready.sem, 1)
                dve.wait_ge(*exp_ready.at(pair, 2))
                link(dve.tensor_tensor(out=EW, in0=EW, in1=L2, op=ALU.subtract))
                link(dve.reciprocal(MX[:, 10:11], MX[:, 9:10]))
                dve.tensor_scalar(EW, EW, MX[:, 10:11], None, ALU.mult).then_inc(w_ready.sem, 1)
                dve.wait_ge(*filled("pool", pair))
                for i in range(2):
                    ins = dve.tensor_copy(
                        PT[0:C, :, bass.ds(2 * pair + i, 1)].rearrange("p e a -> p (e a)"),
                        area("pool")[i * C:(i + 1) * C, i * EXPERTS:(i + 1) * EXPERTS])
                ins.then_inc(*empty("pool"))
                assert links[0] == VSTEPS, links[0]

            now[0] = vstep.after
            links[0] = 0
            dve.memset(ONES, 1.0).then_inc(ones_ready.sem, 1)
            for g in range(2):
                dve.wait_ge(*filled(("eo", g)))
                dve.tensor_copy(EO[:, 16 * g:16 * g + 16, :],
                                area(("eo", g))[0:IMAGES, :].rearrange("p (e o) -> p e o", o=C))\
                    .then_inc(*empty(("eo", g)))
            for q in range(PAIRS):
                b = q % 2
                dve.wait_ge(*last_t[b].after(q // 2 + 1))
                for n in range(NPIX):
                    key, cut = ("add", q, n), slice(n * PIX, (n + 1) * PIX)
                    dve.wait_ge(*filled(key))
                    dve.tensor_tensor(out=LT[b][:, cut], in0=area(key)[:, 0:PIX], in1=LT[b][:, cut],
                                      op=ALU.add).then_inc(*empty(key))

        @block.tensor
        def _(pe):
            pe.wait_ge(*zeroed.first(1))
            pe.wait_ge(*loaded.first(1))
            for m, (n, w) in enumerate((("wk", "k"), ("wq", "q"))):
                pe.wait_ge(*prepared.first(m + 1))
                for c in range(NCHUNK):
                    ins = pe.transpose(area(n)[:, c * P:(c + 1) * P],
                                       WNAT[w][:, c].rearrange("p s d -> p (s d)"), IDN[:, :])
                ins.then_inc(*fill(n))
            for c in range(NCHUNK):
                ins = pe.transpose(area("wd")[:, c * C:(c + 1) * C], DN[:, c * P:(c + 1) * P], IDN[0:C, 0:C])
            ins.then_inc(*fill("wd"))
            pe.wait_ge(*prepared.first(4))
            pe.wait_ge(*emptied_s[order["wd"][0]].first(order["wd"][2]))
            pe.wait_ge(*room("vd"))
            for h in range(HEADS):
                c, half = h // 2, slice(h % 2 * C, (h % 2 + 1) * C)
                at = h % 2 * 512 + c * C
                ins = pe.matmul(area("vd")[:, at:at + C],
                                WNAT["v"][half, c].rearrange("p s d -> p (s d)"), WDT[half, c, :],
                                start=True, stop=True)
            ins.then_inc(*fill("vd"))
            pe.wait_ge(*room("w2"))
            for k in range(3):
                ins = pe.transpose(area("w2")[:, k * P:(k + 1) * P],
                                   W2B[:, k].rearrange("p s i -> p (s i)"), IDN[:, :])
            ins.then_inc(*fill("w2"))
            pe.wait_ge(*room("gw"))
            pe.transpose(area("gw")[:, 0:C], GWB, IDN[0:C, 0:C]).then_inc(*fill("gw"))
            pe.wait_ge(*emptied_s[order["gw"][0]].first(order["gw"][2]))

            with pe.Fori(0, PAIRS) as pair:
                for m, key in enumerate(("gmean", "gvar")):
                    pe.wait_ge(*(gn_sums.at(pair, 1) if m == 0 else emptied("gmean", pair)))
                    pe.wait_ge(*room(key, pair))
                    pe.matmul(area(key)[:, 0:1], AVG[:, :], MV[:, 5 * m:5 * m + 1], start=True, stop=True)\
                        .then_inc(*fill(key))
                pe.wait_ge(*g_ready.at(pair, 1))
                for n in range(NPIX):
                    key = ("t2", n)
                    pe.wait_ge(*room(key, pair))
                    for k in range(3):
                        ins = pe.matmul(area(key)[:, 0:PIX], W2T[:, k, :],
                                        g_window(4 + n * ROWS, k - 1, ROWS),
                                        start=k == 0, stop=k == 2)
                    ins.then_inc(*fill(key))
                for g, (j, m) in enumerate(COLGROUPS):
                    key = ("ucol", g)
                    pe.wait_ge(*room(key, pair))
                    for a in range(m):
                        at = 4 + 4 * PITCH + j + a
                        ins = pe.transpose(area(key)[0:HALFP, a * P:(a + 1) * P],
                                           G[:, at:at + (HALFP - 1) * SPLIT + 1:SPLIT], IDN[:, :])
                    ins.then_inc(*fill(key))
                for w in last_uses(emptied, [("ucol", g) for g in range(len(COLGROUPS))], pair):
                    pe.wait_ge(*w)
                pe.wait_ge(*room("t3", pair))
                for j in range(SPLIT):
                    ins = pe.matmul(area("t3")[:, :], UCOL[0:HALFP, j, :], UCOL[0:HALFP, j:j + 7:2, :],
                                    start=j == 0, stop=j == SPLIT - 1)
                ins.then_inc(*fill("t3"))
                pe.wait_ge(*emptied("t3", pair))
                pe.wait_ge(*room("t3t", pair))
                for i in range(3):
                    ins = pe.transpose(area("t3t")[:, i * P:(i + 1) * P], OS[:, i * P:(i + 1) * P], IDN[:, :])
                ins.then_inc(*fill("t3t"))
                for n in range(NPIX):
                    key, row = ("conv", n), n * ROWS
                    pe.wait_ge(*room(key, pair))
                    acc = area(key)[:, 0:PIX]
                    for k in range(25):
                        r, c = row + 2 * (k // 5), 2 * (k % 5) - 4
                        pe.matmul(acc, D8[:, k, :], g_window(r, c, ROWS), start=k == 0, stop=False)
                    if n == 0:
                        pe.wait_ge(*emptied("t3t", pair))
                        for w in last_uses(emptied, [("t2", m) for m in range(NPIX)], pair):
                            pe.wait_ge(*w)
                    for k in (0, 1, 3, 4):
                        pe.matmul(acc, D7[:, k, :], T2[:, row + 3:row + 3 + ROWS, k:k + W],
                                  start=False, stop=False)
                    for k in range(7):
                        ins = pe.matmul(acc, L10[:, k, :], T2[:, row + k:row + k + ROWS, 2:2 + W],
                                        start=False, stop=k == 6)
                    ins.then_inc(*fill(key))

                def to_tokens(uses):
                    for g, (t, m) in enumerate(GROUPS):
                        key = (uses, g)
                        pe.wait_ge(*room(key, pair))
                        passed(pe)
                        for a in range(m):
                            r = tile_rows(t + a)
                            at = (t + a) * P
                            ins = pe.transpose(area(key)[0:r, a * P:(a + 1) * P], Y[:, at:at + r], IDN[:, :])
                        ins.then_inc(*fill(key))

                for w in last_uses(emptied, [("conv", n) for n in range(NPIX)], pair):
                    pe.wait_ge(*w)
                to_tokens("yt")
                pe.wait_ge(*u_split.at(pair, 1))
                for i in range(2):
                    for g, (t, m) in enumerate(GROUPS):
                        key = ("uts", i, g)
                        pe.wait_ge(*room(key, pair))
                        passed(pe)
                        half = area(key)[:, 0:512].bitcast(F16)
                        for a in range(m):
                            r = tile_rows(t + a)
                            ins = pe.transpose(half[:, a * P:a * P + r],
                                               UHL[0:r, 2 * (t + a) + i].rearrange("p s c -> p (s c)"),
                                               IDH[0:r, 0:r])
                        ins.then_inc(*fill(key))

                def k_project(i, t):
                    key, r = ("kp", i, t), tile_rows(t)
                    pe.wait_ge(*room(key, pair))
                    for n in range(2):
                        cut = slice(n * 512, (n + 1) * 512)
                        for m, w in enumerate((WKH, WKL)):
                            ins = pe.matmul(area(key)[0:r, cut], UTS[i][:, t * P:t * P + r], w[:, cut],
                                            start=m == 0, stop=m == 1)
                    ins.then_inc(*fill(key))

                def k_products(i, t):
                    k, r = i * TILES + t, tile_rows(t)
                    if t == 0:
                        for b in range(1 + i):
                            pe.wait_ge(*room(("kv", i, b), pair))
                    pe.wait_ge(*emptied(("kp", i, t), pair))
                    pe.wait_ge(*ua_ready.at(pair, k + 1))
                    for n in range(2):
                        dst = area(("kv", 0, 0))[:, n * 512:(n + 1) * 512] if i == 0 \
                            else area(("kv", 1, n))[:, :]
                        ins = pe.matmul(dst, UA[0:r, k % 2].rearrange("p s c -> p (s c)"),
                                        KT[0:r, k % 2, n * 512:(n + 1) * 512],
                                        start=t == 0, stop=t == TILES - 1)
                        if t == TILES - 1 and (i or n):
                            ins.then_inc(*fill(("kv", i, n if i else 0)))
                    if t < TILES - 1:
                        ins.then_inc(kv_used.sem, 1)

                for w in last_uses(emptied, [("uts", i, g) for i in range(2) for g in range(len(GROUPS))], pair):
                    pe.wait_ge(*w)
                for i in range(2):
                    for t in range(TILES + 1):
                        if t < TILES:
                            k_project(i, t)
                        if t >= 1:
                            k_products(i, t - 1)
                for i in range(2):
                    for b in range(1 + i):
                        pe.wait_ge(*emptied(("kv", i, b), pair))
                    for g in range(2):
                        key = ("m", i, g)
                        pe.wait_ge(*room(key, pair))
                        for h in range(8 * g, 8 * g + 8):
                            c = h // 2 % 4
                            half = slice(h % 2 * C, (h % 2 + 1) * C)
                            ins = pe.matmul(area(key)[half, c * 256:c * 256 + P + 2],
                                            AT[i][:, h * C:(h + 1) * C], BD[:, h, :], start=True, stop=True)
                        ins.then_inc(*fill(key))

                def q_project(s, cc):
                    i, n = divmod(s, NPIX)
                    key = ("qp", s, cc)
                    pe.wait_ge(*room(key, pair))
                    for a in range(2):
                        c = 2 * cc + a
                        for m, w in enumerate((WQH, WQL)):
                            ins = pe.matmul(area(key)[:, a * 512:a * 512 + PIX], w[:, c * P:(c + 1) * P],
                                            UTS[i][:, n * PIX:(n + 1) * PIX], start=m == 0, stop=m == 1)
                    ins.then_inc(*fill(key))

                def q_denominators(s, cc):
                    i = s // NPIX
                    if cc == 0:
                        pe.wait_ge(*room(("den", s), pair))
                        if s % NPIX == 0:
                            for w in last_uses(emptied, [("m", i, 0), ("m", i, 1)], pair):
                                pe.wait_ge(*w)
                    pe.wait_ge(*emptied(("qp", s, cc), pair))
                    for c in (2 * cc, 2 * cc + 1):
                        ins = pe.matmul(area(("den", s))[0:DROWS, 0:PIX], KK[i][:, c, :], Q[s % 2][:, c, :],
                                        start=c == 0, stop=c == NCHUNK - 1)
                    if cc == 3:
                        ins.then_inc(*fill(("den", s)))

                def q_sums(s):
                    key = ("dsum", s)
                    pe.wait_ge(*emptied(("den", s), pair))
                    pe.wait_ge(*room(key, pair))
                    for j in range(4):
                        ins = pe.matmul(area(key)[32 * j:32 * j + 32, 0:SUB],
                                        SEL[0:DROWS, :, :].rearrange("p d h -> p (d h)"),
                                        DS[:, j * SUB:(j + 1) * SUB], start=True, stop=True)
                    ins.then_inc(*fill(key))

                def q_broadcast(s, cc):
                    key = ("rb", s, cc)
                    pe.wait_ge(*split_ready.at(pair, s + 1))
                    pe.wait_ge(*room(key, pair))
                    for a in range(2):
                        c = 2 * cc + a
                        for j in range(4):
                            for m in range(3):
                                ins = pe.matmul(
                                    area(key)[:, a * 512 + j * SUB:a * 512 + (j + 1) * SUB],
                                    SELB[:, j, 2 * c:2 * c + 2, :].rearrange("p h c -> p (h c)"),
                                    RS3[:, m, :], start=m == 0, stop=m == 2)
                    ins.then_inc(*fill(key))
                    if cc == 3:
                        ins

                def q_output(s, cc):
                    i = s // NPIX
                    key = ("out", s)
                    if cc == 0:
                        pe.wait_ge(*room(key, pair))
                    pe.wait_ge(*emptied(("rb", s, cc), pair))
                    for c in (2 * cc, 2 * cc + 1):
                        ins = pe.matmul(area(key)[:, 0:PIX], MW[i][:, c, :], Q[s % 2][:, c, :],
                                        start=c == 0, stop=c == NCHUNK - 1)
                    if cc == 3:
                        ins.then_inc(*fill(key))

                def q_fold(s):
                    i = s // NPIX
                    key = ("fold", s)
                    pe.wait_ge(*emptied(("out", s), pair))
                    pe.wait_ge(*room(key, pair))
                    pe.matmul(area(key)[i * C:(i + 1) * C, 0:PIX], FOLD[:, :], OS[:, :],
                              start=True, stop=True).then_inc(*fill(key))

                for s in range(STEPS + 1):
                    for cc in range(5):
                        if s < STEPS and cc < 4:
                            q_project(s, cc)
                        if s >= 1 and cc < 4:
                            q_broadcast(s - 1, cc)
                        if s < STEPS and cc >= 1:
                            q_denominators(s, cc - 1)
                        if s >= 1 and cc >= 1:
                            q_output(s - 1, cc - 1)
                    if s >= 1:
                        q_fold(s - 1)
                    if s < STEPS:
                        q_sums(s)

                pe.wait_ge(*emptied(("fold", STEPS - 1), pair))
                to_tokens("yt2")
                pe.wait_ge(*un_ready.at(pair, 2))
                for g, (t, m) in enumerate(GROUPS):
                    key = ("u2", g)
                    pe.wait_ge(*room(key, pair))
                    passed(pe)
                    for a in range(m):
                        r = tile_rows(t + a)
                        ins = pe.transpose(area(key)[:, a * P:a * P + r], YT[0:r, t + a, :], IDN[0:r, 0:r])
                    ins.then_inc(*fill(key))
                for w in last_uses(emptied, [("u2", g) for g in range(len(GROUPS))], pair):
                    pe.wait_ge(*w)
                for n in range(NPIX):
                    key = ("lg", n)
                    pe.wait_ge(*room(key, pair))
                    pe.matmul(area(key)[0:C, 0:PIX], GWT[:, :], U2[:, n * PIX:(n + 1) * PIX],
                              start=True, stop=True).then_inc(*fill(key))
                pe.wait_ge(*w_ready.at(pair, 1))
                for g in range(2):
                    key = ("wt", g)
                    pe.wait_ge(*room(key, pair))
                    passed(pe)
                    for t in range(16 * g, min(16 * g + 16, TILES)):
                        r = tile_rows(t)
                        ins = pe.transpose(area(key)[0:r, t % 16 * C:(t % 16 + 1) * C],
                                           EW[:, t * P:t * P + r], IDN[0:C, 0:C])
                    ins.then_inc(*fill(key))
                for w in last_uses(emptied, [("wt", 0), ("wt", 1)], pair):
                    pe.wait_ge(*w)
                pe.wait_ge(*room("pool", pair))
                for t in range(TILES):
                    r = tile_rows(t)
                    ins = pe.matmul(area("pool")[:, 0:C], YT[0:r, t, :], WT[0:r, t, :],
                                    start=t == 0, stop=t == TILES - 1)
                ins.then_inc(*fill("pool"))

            pe.wait_ge(*experts_loaded.after(1))
            pe.wait_ge(*room("hid"))
            pe.wait_ge(*emptied("pool", PAIRS - 1))
            for e in range(EXPERTS):
                for a in range(2):
                    col = (a * EXPERTS + e) * IMAGES
                    ins = pe.matmul(area("hid")[:, col:col + IMAGES], W1S[:, e, a * P:(a + 1) * P],
                                    PT[:, e, :], start=True, stop=True)
            ins.then_inc(*fill("hid"))
            pe.wait_ge(*emptied("hid"))
            pe.wait_ge(*ones_ready.after(1))
            pe.wait_ge(*o_stored.after(1))
            for g in range(2):
                key = ("eo", g)
                pe.wait_ge(*room(key))
                for e in range(16 * g, 16 * g + 16):
                    dst = area(key)[0:IMAGES, e % 16 * C:(e % 16 + 1) * C]
                    for a in range(2):
                        pe.matmul(dst, HID[:, a, e, :], W2S[:, a, e, :], start=a == 0, stop=False)
                    ins = pe.matmul(dst, ONES, B2S[:, e, :], start=False, stop=True)
                ins.then_inc(*fill(key))
            pe.wait_ge(*od_loaded.after(1))
            for q in range(PAIRS):
                pe.wait_ge(*last_w[q % 2].after(q // 2 + 1))
                for n in range(NPIX):
                    key = ("add", q, n)
                    pe.wait_ge(*room(key))
                    pe.matmul(area(key)[:, 0:PIX], OD[:, q, :], LW[q % 2][:, n * PIX:(n + 1) * PIX],
                              start=True, stop=True).then_inc(*fill(key))


VSETUP = 39
VSTEPS = 35
LOW = -3.0e38

_INS = ["x", "L0_conv_w2", "L0_conv_p6w", "L0_conv_w7", "L0_conv_w8", "L0_conv_p9w", "L1_attn_wq_w",
        "L1_attn_wq_b", "L1_attn_wk_w", "L1_attn_wk_b", "L1_attn_wv_w", "L1_attn_wv_b", "L1_attn_dense_w",
        "L1_attn_dense_b", "L1_ffn_gate_w", "L1_ffn_gate_b", "L1_ffn_weight1", "L1_ffn_weight2"]


def shape_constants():
    import numpy as np

    ident = np.eye(P, dtype=np.float32)
    channel = np.arange(P)
    avg = np.where(channel[:, None] // 2 == channel[None, :] // 2, 0.5, 0.0).astype(np.float32)
    mask = np.where(channel[:, None] // C == channel[None, :] // C,
                    -1.0 / (np.sqrt(S) * np.sqrt(7 * C)), 0.0).astype(np.float32)
    pos = (np.float32(1.57) * np.arange(S, dtype=np.float32) / np.float32(S)).astype(np.float32)
    cos, sin = np.cos(pos).astype(np.float32), np.sin(pos).astype(np.float32)
    cst = np.concatenate([np.tile(cos, (C, 1)), np.tile(sin, (C, 1))]).astype(np.float32)
    padded = np.zeros((2, TILES * P), np.float32)
    padded[0, :S], padded[1, :S] = cos, sin
    cs = np.ascontiguousarray(padded.reshape(2, TILES, P).transpose(2, 1, 0))
    return {"ident": ident, "avg": avg, "mask": mask, "cst": cst, "cs": cs}


def kernel(**inputs):
    import numpy as np
    import concourse.bacc as bacc
    from concourse.bass_utils import run_bass_kernel_spmd

    nc = bacc.Bacc("TRN2", target_bir_lowering=False, num_devices=1,
                   dynamic_dma_scratch_size=2048)
    arrays, args = {}, []
    for name in _INS:
        arrays[name] = np.ascontiguousarray(inputs[name])
    arrays.update(shape_constants())
    for name, a in arrays.items():
        args.append(nc.dram_tensor(name, a.shape, mybir.dt.from_np(a.dtype), kind="ExternalInput").ap())
    args.append(nc.dram_tensor("out", (IMAGES, C, H, W), F32, kind="ExternalOutput").ap())
    args.append(nc.dram_tensor("t_keep", (IMAGES * C, S), F32, kind="Internal").ap())
    args.append(nc.dram_tensor("w_keep", (IMAGES * EXPERTS, S), F32, kind="Internal").ap())
    args.append(nc.dram_tensor("o_keep", (IMAGES, EXPERTS, C), F32, kind="Internal").ap())
    program(nc, *args)
    r = run_bass_kernel_spmd(nc, [arrays], core_ids=[0])
    return r.results[0]["out"]
```

```python
import concourse.bass as bass
from concourse import mybir
from contextlib import ExitStack

F32, F16, BF16 = mybir.dt.float32, mybir.dt.float16, mybir.dt.bfloat16
ALU = mybir.AluOpType
ACT = mybir.ActivationFunctionType
AX = mybir.AxisListType

P = 128
IMAGES, C, H, W = 16, 64, 56, 56
S = H * W
PAIRS = IMAGES // 2
HEADS = 16
FEAT = HEADS * C
NCHUNK = FEAT // P
ROWS = 8
PIX = ROWS * W
NPIX = S // PIX
TILES = (S + P - 1) // P
LAST = S - (TILES - 1) * P
GROUP = 2 * PIX // P
GROUPS = [(g, min(GROUP, TILES - g)) for g in range(0, TILES, GROUP)]
NG = len(GROUPS)
SUB = PIX // 2
COLGROUP = 8
STEPS = 2 * NPIX
EXPERTS, HIDDEN = 32, 256
PADH, PITCH = H + 8, W + 6
GSIZE = 4 + PADH * PITCH + 8
PADH2, PADW2 = H + 6, W + 4
SPLIT = PITCH // 2
COLS = SPLIT + 6
HALFP = 2 * H
COLGROUPS = [(g, min(COLGROUP, COLS - g)) for g in range(0, COLS, COLGROUP)]
DROWS = C + HEADS
LATE = 12
GN_STEP = 5
LN2_STEPS = [11, 13, 15, 16]
LN_EPS, GN_EPS, DEN_EPS = 1e-5, 1e-5, 1e-5


def tile_rows(t):
    return LAST if t == TILES - 1 else P


class Signal:

    def __init__(self, sem, per_pair, setup=0, unit=1):
        self.sem, self.per, self.setup, self.unit = sem, per_pair, setup, unit

    def first(self, n):
        return self.sem, n * self.unit

    def at(self, pair, n):
        return self.sem, pair * (self.per * self.unit) + (self.setup + n) * self.unit

    def after(self, n):
        return self.sem, (self.setup + PAIRS * self.per + n) * self.unit


def program(nc, x, w2, p6w, w7, w8, p9w, wq_w, wq_b, wk_w, wk_b, wv_w, wv_b, dense_w, dense_b,
            gate_w, gate_b, weight1, weight2, ident_c, avg_c, mask_c, cst_c, cs_c,
            out, t_keep, w_keep, o_keep):
    ctx = ExitStack()
    with ctx:
        ctx.enter_context(nc.allow_non_contiguous_dma(reason="small weights"))

        def sb(name, shape, dtype=F32):
            return ctx.enter_context(nc.sbuf_tensor(name, shape, dtype))

        def signal(name, per_pair=0, setup=0, unit=1):
            return Signal(ctx.enter_context(nc.semaphore(name)), per_pair, setup, unit)

        arena = sb("arena", [P, S + GSIZE + PADH2 * PADW2])
        X = arena[:, 0:S]
        G = arena[:, S:S + GSIZE]
        def g_window(row, col, rows):
            at = 4 + row * PITCH + col
            return G[:, at:at + rows * PITCH].rearrange("p (h w) -> p h w", w=PITCH)[:, :, 0:W]

        T2 = arena[:, S + GSIZE:].rearrange("p (h w) -> p h w", w=PADW2)

        QSIZE = NCHUNK * PIX
        region = sb("region", [P, COLS * P + 2 * S])
        Q = [region[:, i * QSIZE:(i + 1) * QSIZE].rearrange("p (c n) -> p c n", n=PIX) for i in range(3)]
        UCOL = region[:, 0:COLS * P].rearrange("p (j c) -> p j c", c=P)
        un1 = region[:, 0:TILES * P]
        E = region[:, QSIZE:QSIZE + 2 * FEAT].rearrange("p (b f) -> p b f", b=2)
        KT = region[:, QSIZE + 2 * FEAT:QSIZE + 4 * FEAT].rearrange("p (b f) -> p b f", b=2)
        AT = [region[:, QSIZE + (4 + i) * FEAT:QSIZE + (5 + i) * FEAT] for i in range(2)]
        LG = region[0:C, COLS * P:COLS * P + S]
        WT = region[:, COLS * P:COLS * P + TILES * C].rearrange("p (t e) -> p t e", e=C)
        EW = region[0:C, COLS * P + S:COLS * P + 2 * S]

        Y = sb("Y", [P, S])
        un2 = sb("un2", [P, TILES * P])
        UN = {1: un1.rearrange("p (g c) -> p g c", c=C),
              2: un2[:, :].rearrange("p (g c) -> p g c", c=C)}
        UT = {1: un1.rearrange("p (t c) -> p t c", c=P), 2: un2[:, :].rearrange("p (t c) -> p t c", c=P)}
        SQ = sb("SQ", [P, 2 * GROUP, C])
        UHL = sb("UHL", [P, 2 * GROUP, 2, C], F16)
        plane = sb("plane", [P, S])
        UTS = [plane[:, i * S // 2:(i + 1) * S // 2].bitcast(F16) for i in range(2)]
        U2 = plane[:, :]
        small = sb("small", [P, 2 * FEAT + 2 * NCHUNK * DROWS])
        MW = [small[:, i * FEAT:(1 + i) * FEAT].rearrange("p (c o) -> p c o", o=P) for i in range(2)]
        KKF = [small[:, 2 * FEAT + i * NCHUNK * DROWS:2 * FEAT + (i + 1) * NCHUNK * DROWS] for i in range(2)]
        KK = [k.rearrange("p (c m) -> p c m", m=DROWS) for k in KKF]
        L2 = small[0:C, 0:S]
        EQ = sb("EQ", [P, 2, PIX])

        WKH, WKL, WQH, WQL = (sb(n, [P, FEAT], F16) for n in ("WKH", "WKL", "WQH", "WQL"))
        BD = sb("BD", [P, HEADS, P + 2])
        D8 = sb("D8", [P, 25, P])
        D7 = sb("D7", [P, 5, P])
        W2T = sb("W2T", [P, 3, P])
        P9T = sb("P9T", [P, 7, P])
        L10 = sb("L10", [P, 7, P])
        SELB = sb("SELB", [96, 2, HEADS, C], BF16)
        CST = sb("CST", [P, S])
        CS = sb("CS", [P, TILES, 2])
        IDN = sb("IDN", [P, P])
        IDH = sb("IDH", [P, P], F16)
        AVG = sb("AVG", [P, P])
        SEL = sb("SEL", [P, 2, 3, 2, HEADS])
        FOLD = sb("FOLD", [P, C])
        GWT = sb("GWT", [P, C])
        UA = sb("UA", [P, 2, 2, C])
        DS = sb("DS", [DROWS, PIX])
        OS = sb("OS", [P, PIX])
        RR = sb("RR", [96, 3, SUB])
        RS3 = sb("RS3", [96, SUB], BF16)
        PT = sb("PT", [C + 1, EXPERTS, IMAGES])
        P6 = sb("P6", [P, 7])
        W8C = sb("W8C", [P, 25])
        W7C = sb("W7C", [P, 5])
        DBC = sb("DBC", [P, 1])
        GBC = sb("GBC", [C, 1])
        EPS = sb("EPS", [P, 1])
        NEG1 = sb("NEG1", [P, 1])
        BS = sb("BS", [P, NPIX, 6])
        MV = sb("MV", [P, 8])
        ST = sb("ST", [P, 4, 2 * GROUP])
        MX = sb("MX", [C, 12])

        ps = {a: ctx.enter_context(nc.psum_tensor(f"ps_{a}", [P, 512 * (2 if a in "ABC" else 1)], F32))
              for a in "ABCDE"}

        turn = [0]

        def misc():
            turn[0] += 1
            return "ABC"[turn[0] % 3]

        def front_uses():
            return [(("t2", n), misc()) for n in range(NPIX)]

        def back_uses(routing):
            uses = [(("ucol", g), misc()) for g in range(len(COLGROUPS))]
            uses += [("t3", "D"), ("t3t", misc())]
            for n in range(NPIX):
                if n == NPIX - 1:
                    uses += [(("yt", 2), misc())]
                uses += [(("conv", n), misc())]
                uses += [(("wt", g), misc()) for g in range(2)] if routing and n == 1 else []
                uses += [("pool", "D")] if routing and n == 2 else []
                uses += [(("yt", n // 2 - 1), misc())] if n in (2, 4) else []
                uses += [(("uts", i, n // 2 - 1), misc()) for i in range(2)] if n in (3, 5) else []
            return uses + [(("uts", i, 2), misc()) for i in range(2)] + [(("yt", 3), misc())]

        def pair_uses(last):
            uses = []
            for i in range(2):
                for t in range(TILES):
                    uses += [(("kp", i, t), "AB"[t % 2])]
                    if (i, t) == (0, 0):
                        uses += [(("kv", 0, 0), "C")]
                    if (i, t) == (0, LATE):
                        uses += [(("uts", 0, 3), "D"), (("uts", 1, 3), "E")]
                    if (i, t) == (1, 0):
                        uses += [(("kv", 1, 0), "D"), (("kv", 1, 1), "E")]
            uses += [(("m", i, g), misc()) for i in range(2) for g in range(2)]
            for s in range(STEPS + 3):
                uses += [(("qp", s, cc), "AB"[cc % 2]) for cc in range(4)] if s < STEPS else []
                rb = 2 <= s < STEPS + 2
                uses += [(("rb", s - 2, 0), "C")] if rb else []
                uses += [(("dsum", s - 1), "C")] if 1 <= s <= STEPS else []
                uses += [(("den", s), "E")] if s < STEPS else []
                uses += [(("fold", s - 3), "C")] if s >= 3 else []
                uses += [(("out", s - 2), "D")] if rb else []
                uses += [(("rb", s - 2, cc), "C") for cc in (1, 2, 3)] if rb else []
                uses += [("gmean", "C"), ("gvar", "C")] if s == GN_STEP and not last else []
                uses += [(("yt2", LN2_STEPS.index(s)), "C")] if s in LN2_STEPS else []
            uses += [] if last else front_uses()
            uses += [(("u2", g), misc()) for g in range(NG)]
            uses += [(("lg", n), misc()) for n in range(NPIX)]
            return uses + ([(("wt", g), misc()) for g in range(2)] + [("pool", "D")] if last
                           else back_uses(True))

        final_uses = [("hid", "A")] + [(("eo", g), "BC"[g % 2]) for g in range(2)]
        final_uses += [(("add", q, n), "ABC"[(q * NPIX + n) % 3]) for q in range(PAIRS) for n in range(NPIX)]
        spans = {
            "setup": [(k, misc()) for k in ("wk", "wq", "wd", "vd", "w2", "gw")]
            + [("gmean", misc()), ("gvar", misc())] + front_uses() + back_uses(False),
            "loop": pair_uses(False), "last": pair_uses(True), "final": final_uses}
        order, base = {}, {}
        count = dict.fromkeys("ABCDE", 0)
        for span, uses in spans.items():
            base[span] = dict(count)
            for key, a in uses:
                count[a] += 1
                order[span, key] = (a, count[a] - base[span][a])
            if span == "loop":
                per_pair = {a: count[a] - base[span][a] for a in "ABCDE"}
                count = {a: base[span][a] + (PAIRS - 1) * per_pair[a] for a in "ABCDE"}
        filled_s = {a: signal(f"ps_{a}_filled") for a in "ABCDE"}
        emptied_s = {a: signal(f"ps_{a}_emptied") for a in "ABCDE"}
        spare = {a: int(a in "DE") for a in "ABCDE"}

        class Here:

            def __init__(self, span, pair=0):
                self.span, self.pair = span, pair

            def value(self, a, n):
                if self.span == "loop":
                    return self.pair * per_pair[a] + (base["loop"][a] + n)
                return base[self.span][a] + n

            def area(self, key):
                return ps[order[self.span, key][0]]

            def room(self, key):
                a, n = order[self.span, key]
                return emptied_s[a].sem, self.value(a, n - 1 + spare[a])

            def filled(self, key):
                a, n = order[self.span, key]
                return filled_s[a].sem, self.value(a, n)

            def emptied(self, key):
                a, n = order[self.span, key]
                return emptied_s[a].sem, self.value(a, n + spare[a])

            def all_emptied(self, keys):
                return list({order[self.span, k][0]: self.emptied(k) for k in keys}.values())

            def all_before(self, which="ABC"):
                return [(emptied_s[a].sem, self.value(a, spare[a])) for a in which]

            def fill(self, key):
                return filled_s[order[self.span, key][0]].sem, 1

            def empty(self, key):
                return emptied_s[order[self.span, key][0]].sem, 1

        def products_done(k, here):
            i, t = divmod(k, TILES)
            if t == TILES - 1:
                return here.filled(("kv", i, i))
            return kv_used.at(here.pair, k + 1 - i)

        def passed(eng):
            eng.sem_inc(waits_passed.sem, 1)

        loaded = signal("loaded", setup=1, unit=16 * 27)
        zeroed = signal("zeroed", setup=1)
        vstep = signal("vstep", per_pair=VLOOP, setup=VSETUP)
        prepared = signal("prepared", setup=4)
        x_loaded = signal("x_loaded", 1, unit=16)
        stats = signal("stats", NPIX)
        gn_mean = signal("gn_mean", 1)
        g_ready = signal("g_ready", 1)
        ln1_sums = signal("ln1_sums", NG)
        ln1_std = signal("ln1_std", NG)
        ln2_sums = signal("ln2_sums", NG)
        ln2_std = signal("ln2_std", NG)
        un1_ready = signal("un1_ready", NG)
        un2_ready = signal("un2_ready", NG)
        u_high = signal("u_high", NG)
        u_split = signal("u_split", NG)
        ua_ready = signal("ua_ready", 2 * TILES)
        e_ready = signal("e_ready", 2 * TILES)
        kv_used = signal("kv_used", 2 * (TILES - 1))
        eq_ready = signal("eq_ready", 4 * STEPS)
        recip_ready = signal("recip_ready", STEPS)
        gstep = signal("gstep", 3 * STEPS)
        split_ready = signal("split_ready", STEPS)
        t_stored = signal("t_stored", 1, unit=16)
        lmax_ready = signal("lmax_ready", 1)
        l2_ready = signal("l2_ready", 1)
        exp_ready = signal("exp_ready", 2)
        w_ready = signal("w_ready", 1)
        w_stored = signal("w_stored", 1, setup=1, unit=16)
        w1_loaded = signal("w1_loaded", unit=16)
        w2_loaded = signal("w2_loaded", unit=16 * 3)
        o_stored = signal("o_stored", unit=16)
        waits_passed = signal("waits_passed")
        ones_ready = signal("ones_ready")
        od_zeroed = signal("od_zeroed")
        od_loaded = signal("od_loaded", unit=32)
        last_t = [signal(f"last_t{b}", unit=16) for b in range(2)]
        last_w = [signal(f"last_w{b}", unit=16) for b in range(2)]
        last_out = [signal(f"last_out{b}", unit=16) for b in range(3)]

        x_v = x.rearrange("n c h w -> (n c) (h w)")
        out_v = out.rearrange("n c h w -> (n c) (h w)")

        WNAT = {n: v[:, 0:NCHUNK * P].rearrange("p (c s d) -> p c s d", s=2, d=C)
                for n, v in (("k", un2), ("q", region), ("v", plane))}
        WB = {n: v[:, NCHUNK * P:NCHUNK * P + NCHUNK] for n, v in (("k", un2), ("q", region), ("v", plane))}
        DN = Y[0:C, 0:FEAT]
        W2N = Y[:, FEAT:FEAT + 3 * C].rearrange("p (i k) -> p i k", k=3)
        W2B = Y[:, 1216:1216 + 3 * P].rearrange("p (k s i) -> p k s i", k=3, s=2)
        GWB = Y[0:C, 1600:1600 + P]
        P9N = Y[:, 1728:1728 + 7 * C].rearrange("p (k b) -> p k b", k=7)
        MASK = Y[:, 2176:2176 + P]
        WDT = Y[:, 2304:2304 + NCHUNK * C].rearrange("p (c o) -> p c o", o=C)

        n2 = 2 * EXPERTS * C
        d8 = D8[:, :, :].rearrange("p k c -> p (k c)")
        W1S = arena[0:C + 1, 0:EXPERTS * HIDDEN].rearrange("p (e h) -> p e h", h=HIDDEN)
        W2S = region[:, 0:n2].rearrange("p (a e o) -> p a e o", a=2, o=C)
        B2S = region[0:1, n2:n2 + EXPERTS * C].rearrange("p (e o) -> p e o", o=C)
        HID = d8[:, 0:2 * EXPERTS * IMAGES].rearrange("p (a e b) -> p a e b", a=2, b=IMAGES)
        EO = d8[0:IMAGES, 1024:1024 + EXPERTS * C].rearrange("p (e o) -> p e o", o=C)
        ONES = d8[0:1, 3072:3072 + IMAGES]
        OD = small[0:C, 0:PAIRS * P].rearrange("p (q o) -> p q o", o=P)
        LAST_ORDER = [PAIRS - 1] + list(range(PAIRS - 1))
        LT = [Y[:, :], CST[:, :], un2[:, 0:S]]
        LW = [EW, plane[0:C, :], arena[0:C, 0:S]]

        def last_buffer(k):
            return (0, 0) if k == 0 else (1 + (k - 1) % 2, (k - 1) // 2 + 1)

        block = ctx.enter_context(nc.Block())

        @block.sync
        def _(sp):
            loads = [(IDN[:], ident_c), (AVG[:], avg_c), (MASK, mask_c), (CST[:], cst_c), (CS[:], cs_c)]
            for n, w, b in (("k", wk_w, wk_b), ("q", wq_w, wq_b), ("v", wv_w, wv_b)):
                loads += [(WNAT[n][:, :, 0, :], w.rearrange("(c p) d -> p c d", p=P)),
                          (WB[n], b.rearrange("(c p) -> p c", p=P))]
            loads += [(DN, dense_w)]
            for i in range(2):
                half = slice(i * C, (i + 1) * C)
                loads += [(W2N[half], w2.rearrange("o i a k -> o i (a k)")),
                          (P6[half], p6w.rearrange("a c k b -> c (a k b)")),
                          (W8C[half], w8.rearrange("c a k l -> c (a k l)")),
                          (W7C[half], w7.rearrange("c a b k -> c (a b k)")),
                          (DBC[half], dense_b.rearrange("(c a) -> c a", a=1)),
                          (GBC[i * EXPERTS:(i + 1) * EXPERTS], gate_b.rearrange("(e a) -> e a", a=1))]
            loads += [(P9N, bass.AP(p9w.tensor, p9w.offset, [[0, P], [C, 7], [1, C]]))]
            sp.sem_inc(w_stored.sem, 16)
            for dst, src in loads:
                sp.dma_start(dst, src).then_inc(loaded.sem, 16)
            sp.wait_ge(*zeroed.first(1))
            for i in range(2):
                sp.dma_start(GWB[i * EXPERTS:(i + 1) * EXPERTS, i * C:(i + 1) * C],
                             gate_w).then_inc(loaded.sem, 16)
            assert len(loads) + 2 == loaded.unit // 16, len(loads)
            sp.dma_start(X, x_v[0:P, :]).then_inc(x_loaded.sem, 16)

            def pair_of_images(here):
                pair = here.pair
                for w in here.all_before():
                    sp.wait_ge(*w)
                if here.span == "loop":
                    sp.dma_start(X, x_v[bass.ds((pair + 1) * P, P), :]).then_inc(x_loaded.sem, 16)
                else:
                    sp.dma_start(W1S, weight1.rearrange("e d h -> d e h")).then_inc(w1_loaded.sem, 16)
                sp.wait_ge(*here.emptied(("fold", STEPS - 1)))
                if here.span == "loop":
                    sp.dma_start(t_keep[bass.ds(pair * P, P), :], Y[:, :]).then_inc(t_stored.sem, 16)
                    sp.wait_ge(*w_ready.at(pair, 1))
                    sp.dma_start(w_keep[bass.ds(pair * C, C), :], EW).then_inc(w_stored.sem, 16)

            with sp.Fori(0, PAIRS - 1) as pair:
                pair_of_images(Here("loop", pair))
            pair_of_images(Here("last", PAIRS - 1))

            end = Here("final")

            def last_load(k):
                b, n = last_buffer(k)
                q = LAST_ORDER[k]
                sp.dma_start(LT[b], t_keep[q * P:(q + 1) * P, :]).then_inc(last_t[b - 1].sem, 16)
                if k == 2:
                    sp.wait_ge(*end.emptied("hid"))
                sp.dma_start(LW[b], w_keep[q * C:(q + 1) * C, :]).then_inc(last_w[b - 1].sem, 16)

            sp.wait_ge(*Here("last").emptied("pool"))
            for a in range(2):
                sp.dma_start(W2S[:, a], weight2[:, a * P:(a + 1) * P, :].rearrange("e h o -> h e o"))\
                    .then_inc(w2_loaded.sem, 16)
            sp.dma_start(B2S, weight2[:, HIDDEN:HIDDEN + 1, :].rearrange("e a o -> a e o"))\
                .then_inc(w2_loaded.sem, 16)
            sp.wait_ge(*t_stored.at(PAIRS - 1, 0))
            sp.wait_ge(*w_stored.at(PAIRS - 1, 0))
            last_load(1)
            last_load(2)
            for w in end.all_emptied([("eo", 0), ("eo", 1)]):
                sp.wait_ge(*w)
            sp.dma_start(o_keep, EO).then_inc(o_stored.sem, 16)
            sp.wait_ge(*o_stored.after(1))
            sp.wait_ge(*od_zeroed.after(1))
            o_v = o_keep.rearrange("(q i) e o -> i e q o", i=2)
            for i in range(2):
                sp.dma_start(OD[i * EXPERTS:(i + 1) * EXPERTS, :, i * C:(i + 1) * C],
                             o_v[i]).then_inc(od_loaded.sem, 16)
            for k in range(PAIRS):
                b, n = last_buffer(k)
                q = LAST_ORDER[k]
                for w in end.all_emptied([("add", k, n) for n in range(NPIX)]):
                    sp.wait_ge(*w)
                sp.dma_start(out_v[q * P:(q + 1) * P, :], LT[b]).then_inc(last_out[b].sem, 16)
                if k >= 1 and k + 2 < PAIRS:
                    sp.wait_ge(*last_out[b].after(n))
                    last_load(k + 2)
            for b in range(3):
                sp.wait_ge(*last_out[b].after(sum(last_buffer(k)[0] == b for k in range(PAIRS))))

        @block.gpsimd
        def _(pool):
            pool.memset(arena[:, :], 0.0)
            pool.memset(small[:, :], 0.0)
            pool.memset(region[:, NCHUNK * P + NCHUNK:], 0.0)
            pool.memset(BD[:, :, :], 0.0)
            pool.memset(W2B, 0.0)
            pool.memset(GWB, 0.0)
            pool.memset(SEL[:, :, :, :, :], 0.0)
            pool.memset(PT[:, :, :], 1.0)
            pool.memset(EPS[:, :], GN_EPS)
            pool.memset(NEG1[:, :], -1.0).then_inc(zeroed.sem, 1)
            pool.wait_ge(*loaded.first(1))

            def pair_of_images(here):
                pair = here.pair
                for i in range(2):
                    for t in range(TILES):
                        k = i * TILES + t
                        if i == 0 and t % GROUP == 0:
                            pool.wait_ge(*un1_ready.at(pair, t // GROUP + 1))
                        if k >= 2:
                            pool.wait_ge(*products_done(k - 2, here))
                        r = tile_rows(t)
                        pool.tensor_tensor(
                            out=UA[0:r, k % 2], op=ALU.mult,
                            in0=UN[1][0:r, 2 * t + i:2 * t + i + 1, :].broadcast_to([r, 2, C]),
                            in1=CS[0:r, t, :].unsqueeze(2).broadcast_to([r, 2, C]),
                        ).then_inc(ua_ready.sem, 1)
                for s in range(STEPS):
                    pool.wait_ge(*recip_ready.at(pair, s + 1))
                    if s >= 1:
                        pool.wait_ge(*here.filled(("rb", s - 1, 3)))
                    passed(pool)
                    pool.tensor_copy(RS3[:, :], RR[:, 1]).then_inc(gstep.sem, 1)
                    pool.wait_ge(*gstep.at(pair, 3 * s + 1))
                    pool.tensor_tensor(out=RR[:, 2], in0=RR[:, 1], in1=RS3[:, :],
                                       op=ALU.subtract).then_inc(gstep.sem, 1)
                    pool.wait_ge(*gstep.at(pair, 3 * s + 2))
                    passed(pool)
                    pool.tensor_copy(RS3[32:64, :], RR[32:64, 2])
                    pool.tensor_copy(RS3[64:96, :], RR[64:96, 2]).then_inc(gstep.sem, 1)
                    pool.wait_ge(*gstep.at(pair, 3 * s + 3))
                    pool.tensor_tensor(out=RS3[64:96, :], in0=RR[64:96, 2], in1=RS3[64:96, :],
                                       op=ALU.subtract).then_inc(split_ready.sem, 1)

            with pool.Fori(0, PAIRS - 1) as pair:
                pair_of_images(Here("loop", pair))
            pair_of_images(Here("last", PAIRS - 1))
            pool.wait_ge(*Here("last").emptied("pool"))
            pool.memset(OD, 0.0).then_inc(od_zeroed.sem, 1)

        @block.scalar
        def _(act):
            act.wait_ge(*zeroed.first(1))
            act.wait_ge(*loaded.first(1))

            def group_norm(here):
                act.wait_ge(*here.filled("gvar"))
                act.activation(MV[:, 6:7], here.area("gvar")[:, 0:1], ACT.Sqrt, bias=EPS[:, 0:1])\
                    .then_inc(*here.empty("gvar"))

            def front(here):
                for n in range(NPIX):
                    key = ("t2", n)
                    act.wait_ge(*here.filled(key))
                    act.activation(T2[:, 3 + n * ROWS:3 + (n + 1) * ROWS, 2:2 + W],
                                   here.area(key)[:, 0:PIX].rearrange("p (h w) -> p h w", w=W),
                                   ACT.Copy).then_inc(*here.empty(key))

            def tokens(here, which, g):
                key, (t, m) = ({1: "yt", 2: "yt2"}[which], g), GROUPS[g]
                act.wait_ge(*here.filled(key))
                src = here.area(key)[:, 0:m * P].rearrange("p (t c) -> p t c", c=P)
                full = m if g < NG - 1 else m - 1
                ins = act.activation(UT[which][:, t:t + full, :], src[:, 0:full], ACT.Copy)
                if full < m:
                    ins = act.activation(UT[which][0:LAST, t + full, :], src[0:LAST, full], ACT.Copy)
                ins.then_inc(*here.empty(key))

            def deviations(sums, std, pair, g):
                act.wait_ge(*sums.at(pair, g + 1))
                act.activation(ST[:, 2, :], ST[:, 1, :], ACT.Sqrt, scale=1.0 / C, bias=EPS[:, 0:1])\
                    .then_inc(std.sem, 1)

            def norm1(here, pair, g):
                t, m = GROUPS[g]
                tokens(here, 1, g)
                deviations(ln1_sums, ln1_std, pair, g)
                act.wait_ge(*un1_ready.at(pair, g + 1))
                act.activation(UHL[:, 0:2 * m, 0, :], UN[1][:, 2 * t:2 * t + 2 * m, :], ACT.Copy)\
                    .then_inc(u_high.sem, 1)

            def split_tokens(here, g):
                for i in range(2):
                    key, (t, m) = ("uts", i, g), GROUPS[g]
                    n = min(S - t * P, m * P)
                    act.wait_ge(*here.filled(key))
                    act.activation(UTS[i][:, t * P:t * P + n], here.area(key)[:, 0:512].bitcast(F16)[:, 0:n],
                                   ACT.Copy).then_inc(*here.empty(key))

            def routing_weights(here):
                for g in range(2):
                    key, m = ("wt", g), (16 if g == 0 else TILES - 16)
                    act.wait_ge(*here.filled(key))
                    src = here.area(key)[:, 0:m * C].rearrange("p (t e) -> p t e", e=C)
                    full = m if g == 0 else m - 1
                    ins = act.activation(WT[:, 16 * g:16 * g + full, :], src[:, 0:full], ACT.Copy)
                    if full < m:
                        ins = act.activation(WT[0:LAST, 16 * g + full, :], src[0:LAST, full], ACT.Copy)
                    ins.then_inc(*here.empty(key))

            def back(here, pair, routing):
                for g, (j, m) in enumerate(COLGROUPS):
                    key = ("ucol", g)
                    act.wait_ge(*here.filled(key))
                    act.activation(UCOL[0:HALFP, j:j + m, :],
                                   here.area(key)[0:HALFP, 0:m * P].rearrange("p (j c) -> p j c", c=P),
                                   ACT.Copy).then_inc(*here.empty(key))
                if routing:
                    shares(here)
                    routing_weights(here)
                norm1(here, pair, 0)
                split_tokens(here, 0)
                norm1(here, pair, 1)
                split_tokens(here, 1)
                norm1(here, pair, 2)
                split_tokens(here, 2)
                norm1(here, pair, 3)

            def shares(here):
                act.wait_ge(*lmax_ready.at(here.pair, 1))
                act.activation(EW, LG, ACT.Exp, bias=MX[:, 8:9], accum_out=MX[:, 9:10])\
                    .then_inc(exp_ready.sem, 1)
                act.wait_ge(*l2_ready.at(here.pair, 1))
                act.activation(L2, L2, ACT.Exp, bias=MX[:, 8:9]).then_inc(exp_ready.sem, 1)

            def pair_of_images(here):
                pair = here.pair
                for i in range(2):
                    for t in range(TILES):
                        k, r = i * TILES + t, tile_rows(t)
                        act.wait_ge(*here.filled(("kp", i, t)))
                        if k >= 2:
                            act.wait_ge(*here.emptied(("kp", *divmod(k - 2, TILES))))
                        act.activation(E[0:r, k % 2], here.area(("kp", i, t))[0:r, :], ACT.Exp,
                                       bias=NEG1[0:r, 0:1]).then_inc(e_ready.sem, 1)
                        if (i, t) == (0, LATE):
                            split_tokens(here, 3)
                    if i == 0:
                        act.wait_ge(*w_stored.at(pair, 0))
                    for b in range(1 + i):
                        key = ("kv", i, b)
                        wide = FEAT // (1 + i)
                        act.wait_ge(*here.filled(key))
                        act.activation(AT[i][:, b * wide:(b + 1) * wide], here.area(key)[:, 0:wide], ACT.Copy)\
                            .then_inc(*here.empty(key))
                for s in range(STEPS + 3):
                    for cc in range(4):
                        if s < STEPS:
                            n, key = 4 * s + cc, ("qp", s, cc)
                            act.wait_ge(*here.filled(key))
                            if n >= 1:
                                act.wait_ge(*here.emptied(("qp", *divmod(n - 1, 4))))
                            act.activation(EQ[:, :, :], here.area(key)[:, :]
                                           .rearrange("p (c n) -> p c n", c=2)[:, :, 0:PIX],
                                           ACT.Exp, bias=NEG1[:, 0:1]).then_inc(eq_ready.sem, 1)
                        if cc == 0 and s - 1 in LN2_STEPS:
                            deviations(ln2_sums, ln2_std, pair, LN2_STEPS.index(s - 1))
                    if s == GN_STEP and here.span == "loop":
                        group_norm(here)
                    if s in LN2_STEPS:
                        tokens(here, 2, LN2_STEPS.index(s))
                if here.span == "loop":
                    front(here)
                deviations(ln2_sums, ln2_std, pair, NG - 1)
                for g, (t, m) in enumerate(GROUPS):
                    key, n = ("u2", g), min(S - t * P, m * P)
                    act.wait_ge(*here.filled(key))
                    act.activation(U2[:, t * P:t * P + n], here.area(key)[:, 0:n], ACT.Copy)\
                        .then_inc(*here.empty(key))
                for n in range(NPIX):
                    key = ("lg", n)
                    act.wait_ge(*here.filled(key))
                    act.activation(LG[:, n * PIX:(n + 1) * PIX], here.area(key)[0:C, 0:PIX], ACT.Identity,
                                   bias=GBC[:, 0:1]).then_inc(*here.empty(key))
                if here.span == "loop":
                    back(here, pair + 1, True)
                else:
                    shares(here)
                    routing_weights(here)

            start = Here("setup")
            group_norm(start)
            front(start)
            back(start, 0, False)
            with act.Fori(0, PAIRS - 1) as pair:
                pair_of_images(Here("loop", pair))
            pair_of_images(Here("last", PAIRS - 1))
            end = Here("final")
            act.wait_ge(*end.filled("hid"))
            act.activation(HID, end.area("hid")[:, :].rearrange("p (a e b) -> p a e b", a=2, b=IMAGES),
                           ACT.Gelu).then_inc(*end.empty("hid"))

        @block.vector
        def _(dve):
            links = [0]
            now = [vstep.first]

            def link(ins):
                links[0] += 1
                ins.then_inc(vstep.sem, 1)
                dve.wait_ge(*now[0](links[0]))

            for a in "DE":
                dve.sem_inc(emptied_s[a].sem, 1)
            dve.wait_ge(*zeroed.first(1))
            dve.wait_ge(*loaded.first(1))
            for n, one in (("k", 1.0), ("q", 1.0), ("v", 0.0)):
                w = WNAT[n]
                link(dve.tensor_copy(ST[:, 0, 0:NCHUNK], w[:, :, 0, C - 1]))
                link(dve.tensor_tensor(out=w[:, :, 0, :], in0=w[:, :, 0, :], op=ALU.subtract,
                                       in1=ST[:, 0, 0:NCHUNK].unsqueeze(2).broadcast_to([P, NCHUNK, C])))
                link(dve.tensor_scalar(w[:, :, 0, C - 1], WB[n], one, None, ALU.add))
                dve.tensor_copy(w[:, :, 1, :], w[:, :, 0, :]).then_inc(prepared.sem, 1)
            for k in range(3):
                for i in range(2):
                    half = slice(i * C, (i + 1) * C)
                    link(dve.tensor_copy(W2B[half, k, i, :], W2N[half, :, k]))
            dve.tensor_copy(IDH[:, :], IDN[:, :]).then_inc(prepared.sem, 1)
            for d, w, m in ((D8, W8C, 25), (D7, W7C, 5)):
                link(dve.tensor_tensor(out=d[:, :, :], op=ALU.mult,
                                       in0=IDN[:, :].unsqueeze(1).broadcast_to([P, m, P]),
                                       in1=w[:, :].unsqueeze(2).broadcast_to([P, m, P])))
            for k in range(7):
                link(dve.tensor_tensor(out=P9T[:, k, :].rearrange("p (s b) -> p s b", s=2), op=ALU.mult,
                                       in0=MASK.rearrange("p (s b) -> p s b", s=2),
                                       in1=P9N[:, k, :].unsqueeze(1).broadcast_to([P, 2, C])))
            for m in range(3):
                rows = slice(32 * m, 32 * m + 32)
                for j in range(2):
                    at = 32 * m + HEADS * j
                    link(dve.tensor_copy(SELB[rows, j], IDN[rows, at:at + HEADS].unsqueeze(2)
                                         .broadcast_to([32, HEADS, C])))
                    link(dve.tensor_tensor(out=SEL[:, j, m, j, :], in0=IDN[:, 0:HEADS],
                                           in1=IDN[:, C:C + HEADS], op=ALU.add))
            link(dve.tensor_tensor(out=FOLD[:, :], in0=IDN[:, 0:C], in1=IDN[:, C:P], op=ALU.add))
            link(dve.tensor_copy(BD[:, :, P], IDN[:, C - 1:C].broadcast_to([P, HEADS])))
            link(dve.tensor_copy(BD[:, :, P + 1], IDN[:, P - 1:P].broadcast_to([P, HEADS])))
            start = Here("setup")
            for n, hi, lo in (("wk", WKH, WKL), ("wq", WQH, WQL)):
                dve.wait_ge(*start.filled(n))
                link(dve.tensor_copy(hi[:, :], start.area(n)[:, :]))
                dve.tensor_tensor(out=lo[:, :], in0=start.area(n)[:, :], in1=hi[:, :], op=ALU.subtract)\
                    .then_inc(*start.empty(n))
            dve.wait_ge(*start.filled("wd"))
            dve.tensor_copy(WDT, start.area("wd")[:, 0:NCHUNK * C].rearrange("p (c o) -> p c o", o=C))\
                .then_inc(*start.empty("wd"))
            dve.wait_ge(*start.filled("vd"))
            for s in range(2):
                vd = start.area("vd")[:, s * 512:(s + 1) * 512].rearrange("p (h o) -> p h o", o=C)
                link(dve.tensor_copy(BD[0:C, s:HEADS:2, 0:C], vd[0:C]))
                ins = dve.tensor_copy(BD[C:P, s:HEADS:2, C:P], vd[C:P])
            ins.then_inc(*start.empty("vd"))
            dve.wait_ge(*start.filled("w2"))
            dve.tensor_copy(W2T[:, :, :], start.area("w2")[:, 0:3 * P].rearrange("p (k o) -> p k o", k=3))\
                .then_inc(*start.empty("w2"))
            dve.wait_ge(*start.filled("gw"))
            link(dve.tensor_copy(GWT[:, :], start.area("gw")[:, 0:C]))
            for which in (1, 2):
                dve.memset(UN[which], 0.0)
            dve.memset(ST[:, :, :], 1.0).then_inc(*start.empty("gw"))

            def group_norm(here, pair):
                dve.wait_ge(*x_loaded.at(pair, 1))
                for n in range(NPIX):
                    dve.bn_stats(out=BS[:, n, :], in_=X[:, n * PIX:(n + 1) * PIX]).then_inc(stats.sem, 1)
                dve.wait_ge(*stats.at(pair, NPIX))
                passed(dve)
                dve.bn_aggr(out=MV[:, 0:2], in_=BS[:, :, :]).then_inc(gn_mean.sem, 1)

            def group_norm_variance(here):
                dve.wait_ge(*here.filled("gmean"))
                link(dve.tensor_copy(MV[:, 2:3], here.area("gmean")[:, 0:1]))
                link(dve.tensor_tensor(out=MV[:, 3:4], in0=MV[:, 0:1], in1=MV[:, 2:3], op=ALU.subtract))
                link(dve.tensor_tensor(out=MV[:, 4:5], in0=MV[:, 3:4], in1=MV[:, 3:4], op=ALU.mult))
                dve.tensor_tensor(out=MV[:, 5:6], in0=MV[:, 4:5], in1=MV[:, 1:2], op=ALU.add)\
                    .then_inc(*here.empty("gmean"))

            def group_norm_apply(here):
                dve.wait_ge(*here.emptied("gvar"))
                link(dve.reciprocal(MV[:, 7:8], MV[:, 6:7]))
                dve.tensor_scalar(g_window(4, 0, H), X.rearrange("p (h w) -> p h w", w=W),
                                  MV[:, 2:3], MV[:, 7:8], ALU.subtract, ALU.mult).then_inc(g_ready.sem, 1)

            def taps(here):
                dve.wait_ge(*here.filled("t3"))
                t3 = here.area("t3")[:, :].rearrange("p (i c) -> p i c", i=4)
                link(dve.tensor_copy(OS[:, 0:3 * P], here.area("t3")[:, P:4 * P]))
                for i in range(4):
                    k = 3 - i
                    ins = dve.scalar_tensor_tensor(out=L10[:, k, :], in0=t3[:, i, :], scalar=P6[:, k:k + 1],
                                                   in1=P9T[:, k, :], op0=ALU.mult, op1=ALU.mult)
                link(ins)
                dve.tensor_tensor(out=L10[:, 3, :], in0=L10[:, 3, :], in1=D7[:, 2, :], op=ALU.add)\
                    .then_inc(*here.empty("t3"))
                dve.wait_ge(*here.filled("t3t"))
                for i in range(1, 4):
                    k = 3 + i
                    ins = dve.scalar_tensor_tensor(
                        out=L10[:, k, :], in0=here.area("t3t")[:, (i - 1) * P:i * P], scalar=P6[:, k:k + 1],
                        in1=P9T[:, k, :], op0=ALU.mult, op1=ALU.mult)
                ins.then_inc(*here.empty("t3t"))

            def conv_residual(here, n):
                dve.wait_ge(*here.filled(("conv", n)))
                cut = slice(n * PIX, (n + 1) * PIX)
                dve.tensor_tensor(out=Y[:, cut], in0=here.area(("conv", n))[:, 0:PIX], in1=X[:, cut],
                                  op=ALU.add).then_inc(*here.empty(("conv", n)))

            def norm_sums(here, which, sums, g):
                t, m = GROUPS[g]
                u = UN[which][:, 2 * t:2 * t + 2 * m, :]
                st = ST[:, :, 0:2 * m]
                dve.wait_ge(*here.emptied(({1: "yt", 2: "yt2"}[which], g)))
                link(dve.tensor_reduce(out=st[:, 0], in_=u, axis=AX.X, op=ALU.add))
                link(dve.tensor_scalar(st[:, 3], st[:, 0], 1.0 / C, None, ALU.mult))
                link(dve.tensor_tensor(out=u, in0=u, in1=st[:, 3].unsqueeze(2).broadcast_to([P, 2 * m, C]),
                                       op=ALU.subtract))
                link(dve.tensor_tensor(out=SQ[:, 0:2 * m, :], in0=u, in1=u, op=ALU.mult))
                dve.tensor_reduce(out=st[:, 1], in_=SQ[:, 0:2 * m, :], axis=AX.X, op=ALU.add)\
                    .then_inc(sums.sem, 1)

            def norm_scale(which, std, pair, g):
                t, m = GROUPS[g]
                u = UN[which][:, 2 * t:2 * t + 2 * m, :]
                st = ST[:, :, 0:2 * m]
                dve.wait_ge(*std.at(pair, g + 1))
                link(dve.reciprocal(st[:, 3], st[:, 2]))
                return dve.tensor_tensor(out=u, in0=u, op=ALU.mult,
                                         in1=st[:, 3].unsqueeze(2).broadcast_to([P, 2 * m, C]))

            def norm1(here, pair, g):
                t, m = GROUPS[g]
                u = UN[1][:, 2 * t:2 * t + 2 * m, :]
                norm_sums(here, 1, ln1_sums, g)
                link(norm_scale(1, ln1_std, pair, g))
                dve.memset(u[:, :, C - 1:C], 1.0).then_inc(un1_ready.sem, 1)
                dve.wait_ge(*u_high.at(pair, g + 1))
                dve.tensor_tensor(out=UHL[:, 0:2 * m, 1, :], in0=u, in1=UHL[:, 0:2 * m, 0, :],
                                  op=ALU.subtract).then_inc(u_split.sem, 1)

            def routing(here):
                for w in here.all_emptied([("lg", n) for n in range(NPIX)]):
                    dve.wait_ge(*w)
                passed(dve)
                link(dve.max(out=MX[:, 0:8], in_=LG))
                dve.tensor_scalar(MX[:, 8:9], MX[:, 0:1], -1.0, None, ALU.mult).then_inc(lmax_ready.sem, 1)
                dve.match_replace(out=L2, in_to_replace=MX[:, 0:8], in_values=LG, imm_value=LOW)\
                    .then_inc(l2_ready.sem, 1)

            def shares(here):
                dve.wait_ge(*exp_ready.at(here.pair, 2))
                link(dve.tensor_tensor(out=EW, in0=EW, in1=L2, op=ALU.subtract))
                link(dve.reciprocal(MX[:, 10:11], MX[:, 9:10]))
                dve.tensor_scalar(EW, EW, MX[:, 10:11], None, ALU.mult).then_inc(w_ready.sem, 1)

            def pooled(here):
                dve.wait_ge(*here.filled("pool"))
                for i in range(2):
                    ins = dve.tensor_copy(
                        PT[0:C, :, bass.ds(2 * here.pair + i, 1)].rearrange("p e a -> p (e a)"),
                        here.area("pool")[i * C:(i + 1) * C, i * EXPERTS:(i + 1) * EXPERTS])
                ins.then_inc(*here.empty("pool"))

            def back(here, pair, before):
                if before is not None:
                    routing(here)
                taps(here)
                if before is not None:
                    dve.wait_ge(*t_stored.at(before, 1))
                conv_residual(here, 0)
                if before is not None:
                    shares(here)
                conv_residual(here, 1)
                conv_residual(here, 2)
                if before is not None:
                    pooled(here)
                norm1(here, pair, 0)
                conv_residual(here, 3)
                conv_residual(here, 4)
                norm1(here, pair, 1)
                conv_residual(here, 5)
                norm1(here, pair, 2)
                conv_residual(here, 6)
                norm1(here, pair, 3)

            def k_features(here, i, t):
                k, r = i * TILES + t, tile_rows(t)
                key = ("kp", i, t)
                dve.wait_ge(*e_ready.at(here.pair, k + 1))
                if k >= 2:
                    dve.wait_ge(*products_done(k - 2, here))
                dve.scalar_tensor_tensor(out=KT[0:r, k % 2], in0=E[0:r, k % 2], scalar=1.0,
                                         in1=here.area(key)[0:r, :], op0=ALU.min, op1=ALU.max)\
                    .then_inc(*here.empty(key))

            def head_matrices(here, i):
                for g in range(2):
                    key = ("m", i, g)
                    dve.wait_ge(*here.filled(key))
                    m = here.area(key)[:, :].rearrange("p (c n) -> p c n", n=256)
                    dve.tensor_copy(MW[i][:, 4 * g:4 * g + 4, :], m[:, :, 0:P])
                    for hh in range(2):
                        for cs in range(2):
                            half = slice(hh * C, (hh + 1) * C)
                            first = 4 * g * (DROWS + 2) + cs * C + hh
                            ins = dve.tensor_copy(
                                KKF[i][half, first:first + 3 * (DROWS + 2) + 1:DROWS + 2], m[half, :, P + cs])
                    ins.then_inc(*here.empty(key))

            def q_features(here, s, cc):
                n, key = 4 * s + cc, ("qp", s, cc)
                dve.wait_ge(*eq_ready.at(here.pair, n + 1))
                if s >= 3 and cc == 0:
                    dve.wait_ge(*here.filled(("out", s - 3)))
                dve.scalar_tensor_tensor(
                    out=Q[s % 3][:, 2 * cc:2 * cc + 2, :], in0=EQ[:, :, :], scalar=1.0,
                    in1=here.area(key)[:, :].rearrange("p (c n) -> p c n", c=2)[:, :, 0:PIX],
                    op0=ALU.min, op1=ALU.max).then_inc(*here.empty(key))

            def q_scale(here, s, cc):
                key = ("rb", s, cc)
                q = Q[s % 3][:, 2 * cc:2 * cc + 2, :]
                dve.wait_ge(*here.filled(key))
                dve.tensor_tensor(out=q, in0=q, op=ALU.mult,
                                  in1=here.area(key)[:, :].rearrange("p (c n) -> p c n", c=2)[:, :, 0:PIX])\
                    .then_inc(*here.empty(key))

            def den_parts(here, s):
                n = s % NPIX
                dve.wait_ge(*here.filled(("den", s)))
                dve.tensor_tensor(out=DS[:, :], in0=here.area(("den", s))[0:DROWS, 0:PIX],
                                  in1=CST[0:DROWS, n * PIX:(n + 1) * PIX], op=ALU.mult)\
                    .then_inc(*here.empty(("den", s)))

            def den_guard(here, s):
                dve.wait_ge(*here.filled(("dsum", s)))
                dve.tensor_scalar(RR[:, 0], here.area(("dsum", s))[0:96, 0:SUB], DEN_EPS, None, ALU.add)\
                    .then_inc(*here.empty(("dsum", s)))

            def den_reciprocal(here, s):
                dve.wait_ge(*here.emptied(("dsum", s)))
                if s >= 1:
                    dve.wait_ge(*split_ready.at(here.pair, s))
                dve.reciprocal(RR[:, 1], RR[:, 0]).then_inc(recip_ready.sem, 1)

            def out_parts(here, s):
                n = s % NPIX
                dve.wait_ge(*here.filled(("out", s)))
                dve.tensor_tensor(out=OS[:, :], in0=here.area(("out", s))[:, 0:PIX],
                                  in1=CST[:, n * PIX:(n + 1) * PIX], op=ALU.mult)\
                    .then_inc(*here.empty(("out", s)))

            def out_residual(here, s):
                i, n = divmod(s, NPIX)
                cut, half = slice(n * PIX, (n + 1) * PIX), slice(i * C, (i + 1) * C)
                dve.wait_ge(*here.filled(("fold", s)))
                dve.scalar_tensor_tensor(out=Y[half, cut], in0=here.area(("fold", s))[half, 0:PIX],
                                         scalar=DBC[half, 0:1], in1=Y[half, cut], op0=ALU.add, op1=ALU.add)\
                    .then_inc(*here.empty(("fold", s)))

            def pair_of_images(here):
                pair = here.pair
                for i in range(2):
                    for t in range(TILES):
                        k_features(here, i, t)
                for i in range(2):
                    head_matrices(here, i)
                for s in range(STEPS + 3):
                    feature, scaled = s < STEPS, 2 <= s < STEPS + 2
                    if 1 <= s <= STEPS:
                        den_parts(here, s - 1)
                    if s >= 3:
                        out_parts(here, s - 3)
                    for cc in range(4):
                        if feature:
                            q_features(here, s, cc)
                        if cc == 1 and s >= 3:
                            out_residual(here, s - 3)
                        if scaled:
                            q_scale(here, s - 2, cc)
                        if cc == 0 and 1 <= s <= STEPS:
                            den_guard(here, s - 1)
                        if cc == 1 and 1 <= s <= STEPS:
                            den_reciprocal(here, s - 1)
                        if cc == 0 and s - 1 in LN2_STEPS:
                            norm_sums(here, 2, ln2_sums, LN2_STEPS.index(s - 1))
                        if cc == 2 and s - 1 in LN2_STEPS:
                            norm_scale(2, ln2_std, pair, LN2_STEPS.index(s - 1)).then_inc(un2_ready.sem, 1)
                    if here.span == "loop" and s == GN_STEP - 1:
                        group_norm(here, pair + 1)
                    if here.span == "loop" and s == GN_STEP:
                        group_norm_variance(here)
                    if here.span == "loop" and s == GN_STEP + 1:
                        group_norm_apply(here)
                norm_sums(here, 2, ln2_sums, NG - 1)
                norm_scale(2, ln2_std, pair, NG - 1).then_inc(un2_ready.sem, 1)
                if here.span == "loop":
                    back(here, pair + 1, pair)
                else:
                    routing(here)
                    shares(here)
                    pooled(here)

            group_norm(start, 0)
            group_norm_variance(start)
            group_norm_apply(start)
            back(start, 0, None)
            assert links[0] == VSETUP, links[0]
            with dve.Fori(0, PAIRS - 1) as pair:
                links[0] = 0
                now[0] = lambda n: vstep.at(pair, n)
                pair_of_images(Here("loop", pair))
                assert links[0] == VLOOP, links[0]
            links[0] = 0
            now[0] = lambda n: vstep.at(PAIRS - 1, n)
            pair_of_images(Here("last", PAIRS - 1))

            end = Here("final")
            dve.memset(ONES, 1.0).then_inc(ones_ready.sem, 1)
            for g in range(2):
                dve.wait_ge(*end.filled(("eo", g)))
                dve.tensor_copy(EO[:, 16 * g:16 * g + 16, :],
                                end.area(("eo", g))[0:IMAGES, :].rearrange("p (e o) -> p e o", o=C))\
                    .then_inc(*end.empty(("eo", g)))
            for k in range(PAIRS):
                b, turns = last_buffer(k)
                if k >= 1:
                    dve.wait_ge(*last_t[b - 1].after(turns))
                for n in range(NPIX):
                    key, cut = ("add", k, n), slice(n * PIX, (n + 1) * PIX)
                    dve.wait_ge(*end.filled(key))
                    dve.tensor_tensor(out=LT[b][:, cut], in0=end.area(key)[:, 0:PIX], in1=LT[b][:, cut],
                                      op=ALU.add).then_inc(*end.empty(key))

        @block.tensor
        def _(pe):
            pe.wait_ge(*zeroed.first(1))
            pe.wait_ge(*loaded.first(1))
            start = Here("setup")
            for m, (n, w) in enumerate((("wk", "k"), ("wq", "q"))):
                pe.wait_ge(*prepared.first(m + 1))
                for c in range(NCHUNK):
                    ins = pe.transpose(start.area(n)[:, c * P:(c + 1) * P],
                                       WNAT[w][:, c].rearrange("p s d -> p (s d)"), IDN[:, :])
                ins.then_inc(*start.fill(n))
            for c in range(NCHUNK):
                ins = pe.transpose(start.area("wd")[:, c * C:(c + 1) * C], DN[:, c * P:(c + 1) * P], IDN[0:C, 0:C])
            ins.then_inc(*start.fill("wd"))
            pe.wait_ge(*prepared.first(4))
            pe.wait_ge(*start.emptied("wd"))
            pe.wait_ge(*start.room("vd"))
            for h in range(HEADS):
                c, half = h // 2, slice(h % 2 * C, (h % 2 + 1) * C)
                at = h % 2 * 512 + c * C
                ins = pe.matmul(start.area("vd")[:, at:at + C],
                                WNAT["v"][half, c].rearrange("p s d -> p (s d)"), WDT[half, c, :],
                                start=True, stop=True)
            ins.then_inc(*start.fill("vd"))
            pe.wait_ge(*start.room("w2"))
            for k in range(3):
                ins = pe.transpose(start.area("w2")[:, k * P:(k + 1) * P],
                                   W2B[:, k].rearrange("p s i -> p (s i)"), IDN[:, :])
            ins.then_inc(*start.fill("w2"))
            pe.wait_ge(*start.room("gw"))
            pe.transpose(start.area("gw")[:, 0:C], GWB, IDN[0:C, 0:C]).then_inc(*start.fill("gw"))
            pe.wait_ge(*start.emptied("gw"))


            def group_norm(here, pair):
                for m, key in enumerate(("gmean", "gvar")):
                    pe.wait_ge(*(gn_mean.at(pair, 1) if m == 0 else here.emptied("gmean")))
                    pe.wait_ge(*here.room(key))
                    pe.matmul(here.area(key)[:, 0:1], AVG[:, :], MV[:, 5 * m:5 * m + 1], start=True, stop=True)\
                        .then_inc(*here.fill(key))

            def front(here, pair):
                pe.wait_ge(*g_ready.at(pair, 1))
                for n in range(NPIX):
                    key = ("t2", n)
                    pe.wait_ge(*here.room(key))
                    for k in range(3):
                        ins = pe.matmul(here.area(key)[:, 0:PIX], W2T[:, k, :],
                                        g_window(4 + n * ROWS, k - 1, ROWS), start=k == 0, stop=k == 2)
                    ins.then_inc(*here.fill(key))

            def correlations(here):
                for g, (j, m) in enumerate(COLGROUPS):
                    key = ("ucol", g)
                    pe.wait_ge(*here.room(key))
                    for a in range(m):
                        at = 4 + 4 * PITCH + j + a
                        ins = pe.transpose(here.area(key)[0:HALFP, a * P:(a + 1) * P],
                                           G[:, at:at + (HALFP - 1) * SPLIT + 1:SPLIT], IDN[:, :])
                    ins.then_inc(*here.fill(key))
                for w in here.all_emptied([("ucol", g) for g in range(len(COLGROUPS))]):
                    pe.wait_ge(*w)
                pe.wait_ge(*here.room("t3"))
                for j in range(SPLIT):
                    ins = pe.matmul(here.area("t3")[:, :], UCOL[0:HALFP, j, :], UCOL[0:HALFP, j:j + 7:2, :],
                                    start=j == 0, stop=j == SPLIT - 1)
                ins.then_inc(*here.fill("t3"))
                pe.wait_ge(*here.emptied("t3"))
                pe.wait_ge(*here.room("t3t"))
                for i in range(3):
                    ins = pe.transpose(here.area("t3t")[:, i * P:(i + 1) * P], OS[:, i * P:(i + 1) * P],
                                       IDN[:, :])
                ins.then_inc(*here.fill("t3t"))

            def conv(here, n):
                key, row = ("conv", n), n * ROWS
                pe.wait_ge(*here.room(key))
                acc = here.area(key)[:, 0:PIX]
                for k in range(25):
                    r, c = row + 2 * (k // 5), 2 * (k % 5) - 4
                    pe.matmul(acc, D8[:, k, :], g_window(r, c, ROWS), start=k == 0, stop=False)
                if n == 0:
                    pe.wait_ge(*here.emptied("t3t"))
                    for w in here.all_emptied([("t2", m) for m in range(NPIX)]):
                        pe.wait_ge(*w)
                for k in (0, 1, 3, 4):
                    pe.matmul(acc, D7[:, k, :], T2[:, row + 3:row + 3 + ROWS, k:k + W],
                              start=False, stop=False)
                for k in range(7):
                    ins = pe.matmul(acc, L10[:, k, :], T2[:, row + k:row + k + ROWS, 2:2 + W],
                                    start=False, stop=k == 6)
                ins.then_inc(*here.fill(key))

            def to_tokens(here, which, g):
                key, (t, m) = ({1: "yt", 2: "yt2"}[which], g), GROUPS[g]
                pe.wait_ge(*here.room(key))
                passed(pe)
                for a in range(m):
                    r, at = tile_rows(t + a), (t + a) * P
                    ins = pe.transpose(here.area(key)[0:r, a * P:(a + 1) * P], Y[:, at:at + r], IDN[:, :])
                ins.then_inc(*here.fill(key))

            def split_tokens(here, pair, g):
                pe.wait_ge(*u_split.at(pair, g + 1))
                for i in range(2):
                    key, (t, m) = ("uts", i, g), GROUPS[g]
                    pe.wait_ge(*here.room(key))
                    passed(pe)
                    half = here.area(key)[:, 0:512].bitcast(F16)
                    for a in range(m):
                        r = tile_rows(t + a)
                        ins = pe.transpose(half[:, a * P:a * P + r],
                                           UHL[0:r, 2 * a + i].rearrange("p s c -> p (s c)"), IDH[0:r, 0:r])
                    ins.then_inc(*here.fill(key))

            def routing_weights(here):
                pe.wait_ge(*w_ready.at(here.pair, 1))
                for g in range(2):
                    key = ("wt", g)
                    pe.wait_ge(*here.room(key))
                    passed(pe)
                    for t in range(16 * g, min(16 * g + 16, TILES)):
                        r = tile_rows(t)
                        ins = pe.transpose(here.area(key)[0:r, t % 16 * C:(t % 16 + 1) * C],
                                           EW[:, t * P:t * P + r], IDN[0:C, 0:C])
                    ins.then_inc(*here.fill(key))

            def pool_tokens(here):
                for w in here.all_emptied([("wt", 0), ("wt", 1)]):
                    pe.wait_ge(*w)
                pe.wait_ge(*here.room("pool"))
                for t in range(TILES):
                    r = tile_rows(t)
                    ins = pe.matmul(here.area("pool")[:, 0:C], UT[2][0:r, t, :], WT[0:r, t, :],
                                    start=t == 0, stop=t == TILES - 1)
                ins.then_inc(*here.fill("pool"))

            def back(here, pair, routing):
                correlations(here)
                for n in range(NPIX):
                    if n == NPIX - 1:
                        pe.wait_ge(*here.emptied(("conv", 5)))
                        passed(pe)
                        to_tokens(here, 1, 2)
                    conv(here, n)
                    if routing and n == 1:
                        routing_weights(here)
                    if routing and n == 2:
                        pool_tokens(here)
                    if n in (2, 4):
                        for w in here.all_emptied([("conv", m) for m in range(n)]):
                            pe.wait_ge(*w)
                        passed(pe)
                        to_tokens(here, 1, n // 2 - 1)
                    if n in (3, 5):
                        split_tokens(here, pair, n // 2 - 1)
                split_tokens(here, pair, 2)
                pe.wait_ge(*here.emptied(("conv", NPIX - 1)))
                passed(pe)
                to_tokens(here, 1, 3)

            def k_project(here, i, t):
                key, r = ("kp", i, t), tile_rows(t)
                pe.wait_ge(*here.room(key))
                for n in range(2):
                    cut = slice(n * 512, (n + 1) * 512)
                    for m, w in enumerate((WKH, WKL)):
                        ins = pe.matmul(here.area(key)[0:r, cut], UTS[i][:, t * P:t * P + r], w[:, cut],
                                        start=m == 0, stop=m == 1)
                ins.then_inc(*here.fill(key))

            def k_products(here, i, t):
                k, r = i * TILES + t, tile_rows(t)
                if t == 0:
                    for b in range(1 + i):
                        pe.wait_ge(*here.room(("kv", i, b)))
                pe.wait_ge(*here.emptied(("kp", i, t)))
                pe.wait_ge(*ua_ready.at(here.pair, k + 1))
                for n in range(2):
                    dst = here.area(("kv", 0, 0))[:, n * 512:(n + 1) * 512] if i == 0 \
                        else here.area(("kv", 1, n))[:, :]
                    ins = pe.matmul(dst, UA[0:r, k % 2].rearrange("p s c -> p (s c)"),
                                    KT[0:r, k % 2, n * 512:(n + 1) * 512],
                                    start=t == 0, stop=t == TILES - 1)
                    if t == TILES - 1 and (i or n):
                        ins.then_inc(*here.fill(("kv", i, n if i else 0)))
                if t < TILES - 1:
                    ins.then_inc(kv_used.sem, 1)

            def head_matrices(here, i):
                for b in range(1 + i):
                    pe.wait_ge(*here.emptied(("kv", i, b)))
                for g in range(2):
                    key = ("m", i, g)
                    pe.wait_ge(*here.room(key))
                    for h in range(8 * g, 8 * g + 8):
                        c = h // 2 % 4
                        half = slice(h % 2 * C, (h % 2 + 1) * C)
                        ins = pe.matmul(here.area(key)[half, c * 256:c * 256 + P + 2],
                                        AT[i][:, h * C:(h + 1) * C], BD[:, h, :], start=True, stop=True)
                    ins.then_inc(*here.fill(key))

            def q_project(here, s, cc):
                i, n = divmod(s, NPIX)
                key = ("qp", s, cc)
                pe.wait_ge(*here.room(key))
                for a in range(2):
                    c = 2 * cc + a
                    for m, w in enumerate((WQH, WQL)):
                        ins = pe.matmul(here.area(key)[:, a * 512:a * 512 + PIX], w[:, c * P:(c + 1) * P],
                                        UTS[i][:, n * PIX:(n + 1) * PIX], start=m == 0, stop=m == 1)
                ins.then_inc(*here.fill(key))

            def q_denominators(here, s, cc):
                key, i = ("den", s), s // NPIX
                if cc == 0:
                    pe.wait_ge(*here.room(key))
                    if s % NPIX == 0:
                        for w in here.all_emptied([("m", i, 0), ("m", i, 1)]):
                            pe.wait_ge(*w)
                pe.wait_ge(*here.emptied(("qp", s, cc)))
                for c in (2 * cc, 2 * cc + 1):
                    ins = pe.matmul(here.area(key)[0:DROWS, 0:PIX], KK[i][:, c, :], Q[s % 3][:, c, :],
                                    start=c == 0, stop=c == NCHUNK - 1)
                if cc == 3:
                    ins.then_inc(*here.fill(key))

            def q_sums(here, s):
                key = ("dsum", s)
                pe.wait_ge(*here.emptied(("den", s)))
                pe.wait_ge(*here.room(key))
                for j in range(2):
                    ins = pe.matmul(here.area(key)[0:96, 0:SUB],
                                    SEL[0:DROWS, j].rearrange("p m d h -> p (m d h)"),
                                    DS[:, j * SUB:(j + 1) * SUB], start=j == 0, stop=j == 1)
                ins.then_inc(*here.fill(key))

            def q_broadcast(here, s, cc):
                key = ("rb", s, cc)
                pe.wait_ge(*split_ready.at(here.pair, s + 1))
                pe.wait_ge(*here.room(key))
                for a in range(2):
                    c = 2 * cc + a
                    for j in range(2):
                        at = a * 512 + j * SUB
                        ins = pe.matmul(here.area(key)[:, at:at + SUB],
                                        SELB[:, j, 2 * c:2 * c + 2, :].rearrange("p h c -> p (h c)"),
                                        RS3[:, :], start=True, stop=True)
                ins.then_inc(*here.fill(key))

            def q_output(here, s, cc):
                key, i = ("out", s), s // NPIX
                if cc == 0:
                    pe.wait_ge(*here.room(key))
                pe.wait_ge(*here.emptied(("rb", s, cc)))
                for c in (2 * cc, 2 * cc + 1):
                    ins = pe.matmul(here.area(key)[:, 0:PIX], MW[i][:, c, :], Q[s % 3][:, c, :],
                                    start=c == 0, stop=c == NCHUNK - 1)
                if cc == 3:
                    ins.then_inc(*here.fill(key))

            def q_fold(here, s):
                key, i = ("fold", s), s // NPIX
                pe.wait_ge(*here.emptied(("out", s)))
                pe.wait_ge(*here.room(key))
                pe.matmul(here.area(key)[i * C:(i + 1) * C, 0:PIX], FOLD[:, :], OS[:, :],
                          start=True, stop=True).then_inc(*here.fill(key))

            def pair_of_images(here):
                pair = here.pair
                for w in here.all_before():
                    pe.wait_ge(*w)
                for i in range(2):
                    for t in range(TILES + 1):
                        if t < TILES:
                            k_project(here, i, t)
                        if t >= 1:
                            k_products(here, i, t - 1)
                        if (i, t) == (0, LATE):
                            split_tokens(here, pair, 3)
                        if (i, t) == (0, GROUPS[3][0] - 1):
                            for w in here.all_emptied([("uts", 0, 3), ("uts", 1, 3)]):
                                pe.wait_ge(*w)
                for i in range(2):
                    head_matrices(here, i)
                for s in range(STEPS + 3):
                    feature, scaled = s < STEPS, 2 <= s < STEPS + 2
                    for cc in range(5):
                        if feature and cc < 4:
                            q_project(here, s, cc)
                        if scaled and cc == 0:
                            q_broadcast(here, s - 2, 0)
                        if cc == 1 and 1 <= s <= STEPS:
                            q_sums(here, s - 1)
                        if feature and cc >= 1:
                            q_denominators(here, s, cc - 1)
                        if cc == 1 and s >= 3:
                            q_fold(here, s - 3)
                        if scaled and cc >= 1:
                            q_output(here, s - 2, cc - 1)
                        if scaled and 1 <= cc < 4:
                            q_broadcast(here, s - 2, cc)
                    if s == GN_STEP and here.span == "loop":
                        group_norm(here, pair + 1)
                    if s in LN2_STEPS:
                        to_tokens(here, 2, LN2_STEPS.index(s))
                if here.span == "loop":
                    front(here, pair + 1)
                for g, (t, m) in enumerate(GROUPS):
                    key = ("u2", g)
                    pe.wait_ge(*un2_ready.at(pair, g + 1))
                    pe.wait_ge(*here.room(key))
                    passed(pe)
                    for a in range(m):
                        r = tile_rows(t + a)
                        ins = pe.transpose(here.area(key)[:, a * P:a * P + r], UT[2][0:r, t + a, :],
                                           IDN[0:r, 0:r])
                    ins.then_inc(*here.fill(key))
                for w in here.all_emptied([("u2", g) for g in range(NG)]):
                    pe.wait_ge(*w)
                for n in range(NPIX):
                    key = ("lg", n)
                    pe.wait_ge(*here.room(key))
                    pe.matmul(here.area(key)[0:C, 0:PIX], GWT[:, :], U2[:, n * PIX:(n + 1) * PIX],
                              start=True, stop=True).then_inc(*here.fill(key))
                if here.span == "loop":
                    back(here, pair + 1, True)
                else:
                    routing_weights(here)
                    pool_tokens(here)

            group_norm(start, 0)
            front(start, 0)
            back(start, 0, False)
            with pe.Fori(0, PAIRS - 1) as pair:
                pair_of_images(Here("loop", pair))
            pair_of_images(Here("last", PAIRS - 1))

            end = Here("final")
            pe.wait_ge(*w1_loaded.after(1))
            pe.wait_ge(*end.room("hid"))
            pe.wait_ge(*Here("last").emptied("pool"))
            for e in range(EXPERTS):
                for a in range(2):
                    col = (a * EXPERTS + e) * IMAGES
                    ins = pe.matmul(end.area("hid")[:, col:col + IMAGES], W1S[:, e, a * P:(a + 1) * P],
                                    PT[:, e, :], start=True, stop=True)
            ins.then_inc(*end.fill("hid"))
            pe.wait_ge(*end.emptied("hid"))
            pe.wait_ge(*ones_ready.after(1))
            pe.wait_ge(*w2_loaded.after(1))
            for g in range(2):
                key = ("eo", g)
                pe.wait_ge(*end.room(key))
                for e in range(16 * g, 16 * g + 16):
                    dst = end.area(key)[0:IMAGES, e % 16 * C:(e % 16 + 1) * C]
                    for a in range(2):
                        pe.matmul(dst, HID[:, a, e, :], W2S[:, a, e, :], start=a == 0, stop=False)
                    ins = pe.matmul(dst, ONES, B2S[:, e, :], start=False, stop=True)
                ins.then_inc(*end.fill(key))
            pe.wait_ge(*od_loaded.after(1))
            for k in range(PAIRS):
                b, turns = last_buffer(k)
                if k >= 1:
                    pe.wait_ge(*last_w[b - 1].after(turns))
                for n in range(NPIX):
                    key = ("add", k, n)
                    pe.wait_ge(*end.room(key))
                    pe.matmul(end.area(key)[:, 0:PIX], OD[:, LAST_ORDER[k], :],
                              LW[b][:, n * PIX:(n + 1) * PIX], start=True, stop=True)\
                        .then_inc(*end.fill(key))


VSETUP = 74
VLOOP = 53
LOW = -3.0e38

_INS = ["x", "L0_conv_w2", "L0_conv_p6w", "L0_conv_w7", "L0_conv_w8", "L0_conv_p9w", "L1_attn_wq_w",
        "L1_attn_wq_b", "L1_attn_wk_w", "L1_attn_wk_b", "L1_attn_wv_w", "L1_attn_wv_b", "L1_attn_dense_w",
        "L1_attn_dense_b", "L1_ffn_gate_w", "L1_ffn_gate_b", "L1_ffn_weight1", "L1_ffn_weight2"]


def shape_constants():
    import numpy as np

    ident = np.eye(P, dtype=np.float32)
    channel = np.arange(P)
    avg = np.where(channel[:, None] // 2 == channel[None, :] // 2, 0.5, 0.0).astype(np.float32)
    mask = np.where(channel[:, None] // C == channel[None, :] // C,
                    -1.0 / (np.sqrt(S) * np.sqrt(7 * C)), 0.0).astype(np.float32)
    pos = (np.float32(1.57) * np.arange(S, dtype=np.float32) / np.float32(S)).astype(np.float32)
    cos, sin = np.cos(pos).astype(np.float32), np.sin(pos).astype(np.float32)
    cst = np.concatenate([np.tile(cos, (C, 1)), np.tile(sin, (C, 1))]).astype(np.float32)
    padded = np.zeros((2, TILES * P), np.float32)
    padded[0, :S], padded[1, :S] = cos, sin
    cs = np.ascontiguousarray(padded.reshape(2, TILES, P).transpose(2, 1, 0))
    return {"ident": ident, "avg": avg, "mask": mask, "cst": cst, "cs": cs}


def kernel(**inputs):
    import numpy as np
    import concourse.bacc as bacc
    from concourse.bass_utils import run_bass_kernel_spmd

    nc = bacc.Bacc("TRN2", target_bir_lowering=False, num_devices=1,
                   dynamic_dma_scratch_size=2048)
    arrays, args = {}, []
    for name in _INS:
        arrays[name] = np.ascontiguousarray(inputs[name])
    arrays.update(shape_constants())
    for name, a in arrays.items():
        args.append(nc.dram_tensor(name, a.shape, mybir.dt.from_np(a.dtype), kind="ExternalInput").ap())
    args.append(nc.dram_tensor("out", (IMAGES, C, H, W), F32, kind="ExternalOutput").ap())
    args.append(nc.dram_tensor("t_keep", (IMAGES * C, S), F32, kind="Internal").ap())
    args.append(nc.dram_tensor("w_keep", (IMAGES * EXPERTS, S), F32, kind="Internal").ap())
    args.append(nc.dram_tensor("o_keep", (IMAGES, EXPERTS, C), F32, kind="Internal").ap())
    program(nc, *args)
    r = run_bass_kernel_spmd(nc, [arrays], core_ids=[0])
    return r.results[0]["out"]
```

```python
import concourse.bass as bass
from concourse import mybir
from contextlib import ExitStack

F32, F16, BF16 = mybir.dt.float32, mybir.dt.float16, mybir.dt.bfloat16
ALU = mybir.AluOpType
ACT = mybir.ActivationFunctionType
AX = mybir.AxisListType

P = 128
IMAGES, C, H, W = 16, 64, 56, 56
S = H * W
PAIRS = IMAGES // 2
HEADS = 16
FEAT = HEADS * C
NCHUNK = FEAT // P
ROWS = 8
PIX = ROWS * W
NPIX = S // PIX
TILES = (S + P - 1) // P
LAST = S - (TILES - 1) * P
GROUP = 2 * PIX // P
GROUPS = [(g, min(GROUP, TILES - g)) for g in range(0, TILES, GROUP)]
NG = len(GROUPS)
SUB = PIX // 2
COLGROUP = 8
STEPS = 2 * NPIX
EXPERTS, HIDDEN = 32, 256
PADH, PITCH = H + 8, W + 6
GSIZE = 4 + PADH * PITCH + 8
PADH2, PADW2 = H + 6, W + 4
SPLIT = PITCH // 2
COLS = SPLIT + 6
HALFP = 2 * H
COLGROUPS = [(g, min(COLGROUP, COLS - g)) for g in range(0, COLS, COLGROUP)]
DROWS = C + HEADS
KTILES = 2 * TILES
TAPS = [(8, k) for k in range(25)] + [(7, k) for k in (0, 1, 3, 4)]
PIECES = len(TAPS) * NPIX
YT_TILES = [None, None, 0, 1]
SUM_TILES = [None, None, 0, 4]
STD_TILE = 8
SCALE_TILES = [None, None, 9, 10]
SPLIT_TILES = [None, None, 11, 12]
UTS_TILES = [None, 2, 13, 15]
DIAGONALS = 8
FIRST_TAPS = TAPS[:25 - DIAGONALS] + TAPS[25:]
FIRST_PIECES = len(FIRST_TAPS) * NPIX
STATS_TILE, MEAN_TILE, CENTRE_TILE, VAR_TILE, NORM_TILE = 8, 17, 18, 20, 21
K_PIECES, FRONT_PIECES, Q_PIECES = 2, 18, (1, 1, 1, 2, 2)
FRONT_STEPS = {STEPS: (0, 1, 2), STEPS + 1: (3,), STEPS + 2: (4,)}
FRONT_REST = 5
LN2_STEPS = [11, 13, 15, 16]
BACK = 4
LN_EPS, GN_EPS, DEN_EPS = 1e-5, 1e-5, 1e-5


def tile_rows(t):
    return LAST if t == TILES - 1 else P


class Signal:

    def __init__(self, sem, per_pair, setup=0, unit=1):
        self.sem, self.per, self.setup, self.unit = sem, per_pair, setup, unit

    def first(self, n):
        return self.sem, n * self.unit

    def at(self, pair, n):
        return self.sem, pair * (self.per * self.unit) + (self.setup + n) * self.unit

    def after(self, n):
        return self.sem, (self.setup + PAIRS * self.per + n) * self.unit


def program(nc, x, w2, p6w, w7, w8, p9w, wq_w, wq_b, wk_w, wk_b, wv_w, wv_b, dense_w, dense_b,
            gate_w, gate_b, weight1, weight2, ident_c, avg_c, mask_c, cst_c, cs_c,
            out, t_keep, w_keep, o_keep):
    ctx = ExitStack()
    with ctx:
        ctx.enter_context(nc.allow_non_contiguous_dma(reason="small weights"))

        def sb(name, shape, dtype=F32):
            return ctx.enter_context(nc.sbuf_tensor(name, shape, dtype))

        def signal(name, per_pair=0, setup=0, unit=1):
            return Signal(ctx.enter_context(nc.semaphore(name)), per_pair, setup, unit)

        arena = sb("arena", [P, S + GSIZE + PADH2 * PADW2])
        X = arena[:, 0:S]
        G = arena[:, S:S + GSIZE]
        def g_window(row, col, rows):
            at = 4 + row * PITCH + col
            return G[:, at:at + rows * PITCH].rearrange("p (h w) -> p h w", w=PITCH)[:, :, 0:W]

        T2 = arena[:, S + GSIZE:].rearrange("p (h w) -> p h w", w=PADW2)

        QSIZE = NCHUNK * PIX
        region = sb("region", [P, COLS * P + 2 * S])
        Q = [region[:, i * QSIZE:(i + 1) * QSIZE].rearrange("p (c n) -> p c n", n=PIX) for i in range(3)]
        UCOL = region[:, 0:COLS * P].rearrange("p (j c) -> p j c", c=P)
        un1 = region[:, 0:TILES * P]
        E = region[:, QSIZE:QSIZE + 2 * FEAT].rearrange("p (b f) -> p b f", b=2)
        AT = [region[:, QSIZE + (2 + i) * FEAT:QSIZE + (3 + i) * FEAT] for i in range(2)]
        KT = region[:, QSIZE + 4 * FEAT:QSIZE + 7 * FEAT].rearrange("p (b f) -> p b f", b=3)
        LG = region[0:C, COLS * P:COLS * P + S]
        WT = region[:, COLS * P:COLS * P + TILES * C].rearrange("p (t e) -> p t e", e=C)
        EW = region[0:C, COLS * P + S:COLS * P + 2 * S]

        Y = sb("Y", [P, S])
        un2 = sb("un2", [P, TILES * P])
        UN = {1: un1.rearrange("p (g c) -> p g c", c=C),
              2: un2[:, :].rearrange("p (g c) -> p g c", c=C)}
        UT = {1: un1.rearrange("p (t c) -> p t c", c=P), 2: un2[:, :].rearrange("p (t c) -> p t c", c=P)}
        SQ = sb("SQ", [P, 2 * GROUP, C])
        UHL = sb("UHL", [P, 2 * TILES, 2, C], F16)
        plane = sb("plane", [P, S])
        UTS = [plane[:, i * S // 2:(i + 1) * S // 2].bitcast(F16) for i in range(2)]
        U2 = plane[:, :]
        small = sb("small", [P, 2 * FEAT + 2 * NCHUNK * DROWS])
        MW = [small[:, i * FEAT:(1 + i) * FEAT].rearrange("p (c o) -> p c o", o=P) for i in range(2)]
        KKF = [small[:, 2 * FEAT + i * NCHUNK * DROWS:2 * FEAT + (i + 1) * NCHUNK * DROWS] for i in range(2)]
        KK = [k.rearrange("p (c m) -> p c m", m=DROWS) for k in KKF]
        uhl = UHL[:, :, :, :].rearrange("p g s c -> p (g s c)")
        L2 = uhl.bitcast(F32)[0:C, 0:S]
        EQ = sb("EQ", [P, 2, 2, PIX])

        WKH, WKL, WQH, WQL = (sb(n, [P, FEAT], F16) for n in ("WKH", "WKL", "WQH", "WQL"))
        BD = sb("BD", [P, HEADS, P + 2])
        D7 = sb("D7", [P, P])
        W2T = sb("W2T", [P, 3, P])
        P9T = sb("P9T", [P, 7, P])
        L10 = sb("L10", [P, 7, P])
        SELB = sb("SELB", [96, 2, HEADS, C], BF16)
        CST = sb("CST", [P, S])
        CS = sb("CS", [P, TILES, 2])
        IDN = sb("IDN", [P, P])
        IDH = sb("IDH", [P, P], F16)
        AVG = sb("AVG", [P, P])
        SEL = sb("SEL", [P, 2, 3, 2, HEADS])
        FOLD = sb("FOLD", [P, C])
        GWT = sb("GWT", [P, C])
        UA = sb("UA", [P, 3, 2, C])
        DS = sb("DS", [DROWS, PIX])
        OS = sb("OS", [P, PIX])
        RR = sb("RR", [96, 3, SUB])
        RS3 = sb("RS3", [96, 2, SUB], BF16)
        PT = sb("PT", [C + 1, EXPERTS, IMAGES])
        P6 = sb("P6", [P, 7])
        W8C = sb("W8C", [P, 25])
        W7C = sb("W7C", [P, 5])
        DBC = sb("DBC", [P, 1])
        GBC = sb("GBC", [C, 1])
        EPS = sb("EPS", [P, 1])
        NEG1 = sb("NEG1", [P, 1])
        BS = sb("BS", [P, NPIX, 6])
        MV = sb("MV", [P, 8])
        ST = sb("ST", [P, 2, 4, 2 * GROUP])
        MX = sb("MX", [C, 12])

        ps = {a: ctx.enter_context(nc.psum_tensor(f"ps_{a}", [P, 512 * (2 if a in "ABC" else 1)], F32))
              for a in "ABCDE"}

        turn = [0]

        def misc():
            turn[0] += 1
            return "ABC"[turn[0] % 3]

        def front_uses(first=0):
            return [(("t2", n), misc()) for n in range(first, NPIX)]

        def back_uses(routing):
            uses = [(("ucol", g), misc()) for g in range(len(COLGROUPS))]
            uses += [("t3", "D")]
            uses += [(("wt", g), misc()) for g in range(2)] if routing else []
            uses += [("t3t", misc())] + ([("pool", "E")] if routing else [])
            for n in range(NPIX):
                uses += [(("conv", n), misc())]
                uses += [(("yt", n // 2 - 1), misc())] if n in (2, 4) else []
                uses += [(("uts", i, 0), misc()) for i in range(2)] if n == 4 else []
            return uses

        def pair_uses(last):
            uses = []
            for k in range(KTILES):
                uses += [(("kp", k), "AB"[k % 2])]
                uses += [(("yt", YT_TILES.index(k)), "C")] if k in YT_TILES else []
                uses += [(("kv", 0, 0), "C")] if k == 2 else []
                if k in UTS_TILES:
                    uses += [(("uts", i, UTS_TILES.index(k)), "DE"[i]) for i in range(2)]
                uses += [("gmean", "D")] if k == MEAN_TILE and not last else []
                uses += [("gvar", "E")] if k == VAR_TILE and not last else []
                uses += [(("kv", 1, 0), "D"), (("kv", 1, 1), "E")] if k == TILES else []
            uses += [(("m", i, g), misc()) for i in range(2) for g in range(2)]
            for s in range(STEPS + 3):
                uses += [(("qp", s, cc), "AB"[cc % 2]) for cc in range(4)] if s < STEPS else []
                rb = 2 <= s < STEPS + 2
                uses += [(("rb", s - 2, 0), "C")] if rb else []
                drain = s >= STEPS
                uses += [(("rb", s - 2, cc), "CABA"[cc]) for cc in (1, 2, 3)] if rb and drain else []
                uses += [(("dsum", s - 1), "C")] if 1 <= s <= STEPS else []
                uses += [(("den", s), "E")] if s < STEPS else []
                uses += [(("fold", s - 3), "C")] if s >= 3 else []
                uses += [(("out", s - 2), "D")] if rb else []
                uses += [(("t2", n), "E") for n in FRONT_STEPS.get(s, ())] if not last else []
                uses += [(("rb", s - 2, cc), "C") for cc in (1, 2, 3)] if rb and not drain else []
                uses += [(("yt2", LN2_STEPS.index(s)), "C")] if s in LN2_STEPS else []
            uses += [] if last else front_uses(FRONT_REST)
            uses += [(("u2", g), misc()) for g in range(NG)]
            uses += [(("lg", n), misc()) for n in range(NPIX)]
            return uses + ([(("wt", g), misc()) for g in range(2)] + [("pool", "D")] if last
                           else back_uses(True))

        final_uses = [("hid", "A")] + [(("eo", g), "BC"[g % 2]) for g in range(2)]
        final_uses += [(("add", q, n), "ABC"[(q * NPIX + n) % 3]) for q in range(PAIRS) for n in range(NPIX)]
        spans = {
            "setup": [(k, misc()) for k in ("wk", "wq", "wd", "vd", "w2", "gw")]
            + [("gmean", misc()), ("gvar", misc())] + front_uses() + back_uses(False),
            "loop": pair_uses(False), "last": pair_uses(True), "final": final_uses}
        order, base = {}, {}
        count = dict.fromkeys("ABCDE", 0)
        for span, uses in spans.items():
            base[span] = dict(count)
            for key, a in uses:
                count[a] += 1
                order[span, key] = (a, count[a] - base[span][a])
            if span == "loop":
                per_pair = {a: count[a] - base[span][a] for a in "ABCDE"}
                count = {a: base[span][a] + (PAIRS - 1) * per_pair[a] for a in "ABCDE"}
        filled_s = {a: signal(f"ps_{a}_filled") for a in "ABCDE"}
        emptied_s = {a: signal(f"ps_{a}_emptied") for a in "ABCDE"}
        spare = {a: int(a in "DE") for a in "ABCDE"}

        class Here:

            def __init__(self, span, pair=0):
                self.span, self.pair = span, pair

            def value(self, a, n):
                if self.span == "loop":
                    return self.pair * per_pair[a] + (base["loop"][a] + n)
                return base[self.span][a] + n

            def area(self, key):
                return ps[order[self.span, key][0]]

            def room(self, key):
                a, n = order[self.span, key]
                return emptied_s[a].sem, self.value(a, n - 1 + spare[a])

            def filled(self, key):
                a, n = order[self.span, key]
                return filled_s[a].sem, self.value(a, n)

            def emptied(self, key):
                a, n = order[self.span, key]
                return emptied_s[a].sem, self.value(a, n + spare[a])

            def all_emptied(self, keys):
                return list({order[self.span, k][0]: self.emptied(k) for k in keys}.values())

            def all_before(self, which="ABC"):
                return [(emptied_s[a].sem, self.value(a, spare[a])) for a in which]

            def fill(self, key):
                return filled_s[order[self.span, key][0]].sem, 1

            def empty(self, key):
                return emptied_s[order[self.span, key][0]].sem, 1

        def products_done(k, here):
            if k % TILES == TILES - 1:
                return here.filled(("kv", k // TILES, k // TILES))
            return kv_used.at(here.pair, k + 1 - k // TILES)

        def passed(eng):
            eng.sem_inc(waits_passed.sem, 1)

        loaded = signal("loaded", setup=1, unit=16 * 27)
        zeroed = signal("zeroed", setup=1)
        vstep = signal("vstep", per_pair=VLOOP, setup=VSETUP)
        prepared = signal("prepared", setup=4)
        x_loaded = signal("x_loaded", 1, unit=16)
        stats = signal("stats", NPIX)
        gn_mean = signal("gn_mean", 1)
        g_ready = signal("g_ready", 1)
        taps_done = signal("taps_done", PIECES, setup=FIRST_PIECES - PIECES)
        ln1_sums = signal("ln1_sums", NG)
        ln1_std = signal("ln1_std", NG)
        ln2_sums = signal("ln2_sums", NG)
        ln2_std = signal("ln2_std", NG)
        un1_ready = signal("un1_ready", NG)
        un2_ready = signal("un2_ready", NG)
        u_high = signal("u_high", NG)
        u_split = signal("u_split", NG)
        ua_ready = signal("ua_ready", 2 * TILES)
        e_ready = signal("e_ready", 2 * TILES)
        kv_used = signal("kv_used", 2 * (TILES - 1))
        eq_ready = signal("eq_ready", 4 * STEPS)
        recip_ready = signal("recip_ready", STEPS)
        gstep = signal("gstep", 3 * STEPS)
        split_ready = signal("split_ready", STEPS)
        t_stored = signal("t_stored", 1, unit=16)
        lmax_ready = signal("lmax_ready", 1)
        l2_ready = signal("l2_ready", 1)
        exp_ready = signal("exp_ready", 2)
        w_ready = signal("w_ready", 1)
        w_stored = signal("w_stored", 1, setup=1, unit=16)
        w1_loaded = signal("w1_loaded", unit=16)
        w2_loaded = signal("w2_loaded", unit=16 * 3)
        o_stored = signal("o_stored", unit=16)
        waits_passed = signal("waits_passed")
        ones_ready = signal("ones_ready")
        od_zeroed = signal("od_zeroed")
        od_loaded = signal("od_loaded", unit=16 * 8)
        last_t = [signal(f"last_t{b}", unit=16) for b in range(BACK)]
        last_w = [signal(f"last_w{b}", unit=16) for b in range(BACK)]
        last_out = [signal(f"last_out{b}", unit=16) for b in range(1 + BACK)]

        x_v = x.rearrange("n c h w -> (n c) (h w)")
        out_v = out.rearrange("n c h w -> (n c) (h w)")

        WNAT = {n: v[:, 0:NCHUNK * P].rearrange("p (c s d) -> p c s d", s=2, d=C)
                for n, v in (("k", un2), ("q", region), ("v", plane))}
        WB = {n: v[:, NCHUNK * P:NCHUNK * P + NCHUNK] for n, v in (("k", un2), ("q", region), ("v", plane))}
        DN = Y[0:C, 0:FEAT]
        W2N = Y[:, FEAT:FEAT + 3 * C].rearrange("p (i k) -> p i k", k=3)
        W2B = Y[:, 1216:1216 + 3 * P].rearrange("p (k s i) -> p k s i", k=3, s=2)
        GWB = Y[0:C, 1600:1600 + P]
        P9N = Y[:, 1728:1728 + 7 * C].rearrange("p (k b) -> p k b", k=7)
        MASK = Y[:, 2176:2176 + P]
        DIAG = region[:, COLS * P:(COLS + DIAGONALS) * P].rearrange("p (k c) -> p k c", c=P)
        WDT = Y[:, 2304:2304 + NCHUNK * C].rearrange("p (c o) -> p c o", o=C)

        n2 = 2 * EXPERTS * C
        bd = BD[:, :, :].rearrange("p k c -> p (k c)")
        W1S = arena[0:C + 1, 0:EXPERTS * HIDDEN].rearrange("p (e h) -> p e h", h=HIDDEN)
        W2S = region[:, 0:n2].rearrange("p (a e o) -> p a e o", a=2, o=C)
        B2S = region[0:1, n2:n2 + EXPERTS * C].rearrange("p (e o) -> p e o", o=C)
        HID = bd[:, 0:2 * EXPERTS * IMAGES].rearrange("p (a e b) -> p a e b", a=2, b=IMAGES)
        ONES = bd[0:1, 2 * EXPERTS * IMAGES:2 * EXPERTS * IMAGES + IMAGES]
        EO = arena[0:IMAGES, EXPERTS * HIDDEN:EXPERTS * (HIDDEN + C)].rearrange("p (e o) -> p e o", o=C)
        OD = EQ[:, :, :, :].rearrange("p b c n -> p (b c n)")[:, 0:PAIRS * P].rearrange("p (q o) -> p q o", o=P)
        LAST_ORDER = [PAIRS - 1] + list(range(PAIRS - 1))
        lower, upper = slice(0, C), slice(C, P)
        ew = slice(COLS * P + S, COLS * P + 2 * S)
        LT = [Y[:, :], CST[:, :], small[:, 0:S], uhl.bitcast(F32)[:, 0:S], un2[:, 0:S]]
        LW = [EW, region[upper, ew], plane[upper, :], plane[lower, :], arena[lower, 0:S]]
        LFULL = [region[:, ew], region[:, ew], plane[:, :], plane[:, :], arena[:, 0:S]]
        LDUE = [[1], [1], [2, 3], [3], [4], [5], [6, 7], [7]]

        def last_buffer(k):
            return (0, 0) if k == 0 else (1 + (k - 1) % BACK, (k - 1) // BACK + 1)

        block = ctx.enter_context(nc.Block())

        @block.sync
        def _(sp):
            loads = [(IDN[:], ident_c), (AVG[:], avg_c), (MASK, mask_c), (CST[:], cst_c), (CS[:], cs_c)]
            for n, w, b in (("k", wk_w, wk_b), ("q", wq_w, wq_b), ("v", wv_w, wv_b)):
                loads += [(WNAT[n][:, :, 0, :], w.rearrange("(c p) d -> p c d", p=P)),
                          (WB[n], b.rearrange("(c p) -> p c", p=P))]
            loads += [(DN, dense_w)]
            for i in range(2):
                half = slice(i * C, (i + 1) * C)
                loads += [(W2N[half], w2.rearrange("o i a k -> o i (a k)")),
                          (P6[half], p6w.rearrange("a c k b -> c (a k b)")),
                          (W8C[half], w8.rearrange("c a k l -> c (a k l)")),
                          (W7C[half], w7.rearrange("c a b k -> c (a b k)")),
                          (DBC[half], dense_b.rearrange("(c a) -> c a", a=1)),
                          (GBC[i * EXPERTS:(i + 1) * EXPERTS], gate_b.rearrange("(e a) -> e a", a=1))]
            loads += [(P9N, bass.AP(p9w.tensor, p9w.offset, [[0, P], [C, 7], [1, C]]))]
            sp.sem_inc(w_stored.sem, 16)
            for dst, src in loads:
                sp.dma_start(dst, src).then_inc(loaded.sem, 16)
            sp.dma_start(X, x_v[0:P, :]).then_inc(x_loaded.sem, 16)
            sp.wait_ge(*zeroed.first(1))
            for i in range(2):
                sp.dma_start(GWB[i * EXPERTS:(i + 1) * EXPERTS, i * C:(i + 1) * C],
                             gate_w).then_inc(loaded.sem, 16)
            assert len(loads) + 2 == loaded.unit // 16, len(loads)

            def pair_of_images(here):
                pair = here.pair
                for w in here.all_before():
                    sp.wait_ge(*w)
                    passed(sp)
                if here.span == "loop":
                    sp.dma_start(X, x_v[bass.ds((pair + 1) * P, P), :]).then_inc(x_loaded.sem, 16)
                else:
                    sp.dma_start(W1S, weight1.rearrange("e d h -> d e h")).then_inc(w1_loaded.sem, 16)
                sp.wait_ge(*here.emptied(("fold", STEPS - 1)))
                passed(sp)
                if here.span == "loop":
                    sp.dma_start(t_keep[bass.ds(pair * P, P), :], Y[:, :]).then_inc(t_stored.sem, 16)
                    sp.wait_ge(*w_ready.at(pair, 1))
                    sp.dma_start(w_keep[bass.ds(pair * C, C), :], EW).then_inc(w_stored.sem, 16)

            with sp.Fori(0, PAIRS - 1) as pair:
                pair_of_images(Here("loop", pair))
            pair_of_images(Here("last", PAIRS - 1))

            end = Here("final")

            def last_load(k):
                b, n = last_buffer(k)
                q = LAST_ORDER[k]
                sp.dma_start(LT[b], t_keep[q * P:(q + 1) * P, :]).then_inc(last_t[b - 1].sem, 16)
                if k == BACK:
                    sp.wait_ge(*end.emptied("hid"))
                sp.dma_start(LW[b], w_keep[q * C:(q + 1) * C, :]).then_inc(last_w[b - 1].sem, 16)

            sp.wait_ge(*t_stored.at(PAIRS - 1, 0))
            sp.wait_ge(*w_stored.at(PAIRS - 1, 0))
            last_load(1)
            for w in Here("last").all_emptied([("lg", n) for n in range(NPIX)]):
                sp.wait_ge(*w)
            last_load(2)
            sp.wait_ge(*w_ready.at(PAIRS - 1, 1))
            last_load(3)
            sp.wait_ge(*Here("last").emptied("pool"))
            for a in range(2):
                sp.dma_start(W2S[:, a], weight2[:, a * P:(a + 1) * P, :].rearrange("e h o -> h e o"))\
                    .then_inc(w2_loaded.sem, 16)
            sp.dma_start(B2S, weight2[:, HIDDEN:HIDDEN + 1, :].rearrange("e a o -> a e o"))\
                .then_inc(w2_loaded.sem, 16)
            last_load(4)
            for w in end.all_emptied([("eo", 0), ("eo", 1)]):
                sp.wait_ge(*w)
            sp.dma_start(o_keep, EO).then_inc(o_stored.sem, 16)
            sp.wait_ge(*o_stored.after(1))
            sp.wait_ge(*od_zeroed.after(1))
            o_v = o_keep.rearrange("(q i) e o -> i e q o", i=2)
            for first, half in ((0, C), (2, 0), (4, C), (6, 0)):
                for i in range(2):
                    at, qs = half + i * EXPERTS, slice(first, first + 2)
                    sp.dma_start(OD[at:at + EXPERTS, qs, i * C:(i + 1) * C],
                                 o_v[i][:, qs]).then_inc(od_loaded.sem, 16)
            for k in range(PAIRS):
                b, n = last_buffer(k)
                q = LAST_ORDER[k]
                for w in end.all_emptied([("add", k, n) for n in range(NPIX)]):
                    sp.wait_ge(*w)
                sp.dma_start(out_v[q * P:(q + 1) * P, :], LT[b]).then_inc(last_out[b].sem, 16)
                if 2 <= k < PAIRS - BACK + 1:
                    last, turns = last_buffer(k - 1)
                    sp.wait_ge(*last_out[last].after(turns))
                    last_load(k - 1 + BACK)
            for b in range(1 + BACK):
                sp.wait_ge(*last_out[b].after(sum(last_buffer(k)[0] == b for k in range(PAIRS))))

        @block.gpsimd
        def _(pool):
            pool.memset(W2B, 0.0)
            pool.memset(GWB, 0.0)
            pool.memset(SEL[:, :, :, :, :], 0.0)
            pool.memset(EPS[:, :], GN_EPS)
            pool.memset(NEG1[:, :], -1.0)
            pool.memset(BD[:, :, :], 0.0)
            pool.memset(ST[:, :, :, :], 1.0).then_inc(zeroed.sem, 1)
            pool.memset(arena[:, S:], 0.0)
            pool.memset(small[:, 2 * FEAT:], 0.0)
            for u in (region, un2):
                pool.memset(u[:, (TILES - 1) * P:TILES * P], 0.0)
            pool.memset(PT[:, :, :], 1.0).then_inc(zeroed.sem, 1)
            pool.wait_ge(*loaded.first(1))

            def pair_of_images(here):
                pair = here.pair
                for k in range(KTILES):
                    i, t = divmod(k, TILES)
                    if i == 0 and t % GROUP == 0:
                        pool.wait_ge(*un1_ready.at(pair, t // GROUP + 1))
                    if k >= 3:
                        pool.wait_ge(*products_done(k - 3, here))
                    r = tile_rows(t)
                    pool.tensor_tensor(
                        out=UA[0:r, k % 3], op=ALU.mult,
                        in0=UN[1][0:r, 2 * t + i:2 * t + i + 1, :].broadcast_to([r, 2, C]),
                        in1=CS[0:r, t, :].unsqueeze(2).broadcast_to([r, 2, C]),
                    ).then_inc(ua_ready.sem, 1)
                for s in range(STEPS):
                    pool.wait_ge(*recip_ready.at(pair, s + 1))
                    if s >= 2:
                        pool.wait_ge(*here.filled(("rb", s - 2, 3)))
                    passed(pool)
                    parts = RS3[:, s % 2]
                    pool.tensor_copy(parts, RR[:, 1]).then_inc(gstep.sem, 1)
                    pool.wait_ge(*gstep.at(pair, 3 * s + 1))
                    pool.tensor_tensor(out=RR[:, 2], in0=RR[:, 1], in1=parts,
                                       op=ALU.subtract).then_inc(gstep.sem, 1)
                    pool.wait_ge(*gstep.at(pair, 3 * s + 2))
                    passed(pool)
                    pool.tensor_copy(parts[32:64], RR[32:64, 2])
                    pool.tensor_copy(parts[64:96], RR[64:96, 2]).then_inc(gstep.sem, 1)
                    pool.wait_ge(*gstep.at(pair, 3 * s + 3))
                    pool.tensor_tensor(out=parts[64:96], in0=RR[64:96, 2], in1=parts[64:96],
                                       op=ALU.subtract).then_inc(split_ready.sem, 1)

            with pool.Fori(0, PAIRS - 1) as pair:
                pair_of_images(Here("loop", pair))
            pair_of_images(Here("last", PAIRS - 1))
            pool.wait_ge(*Here("last").emptied("pool"))
            pool.memset(OD, 0.0).then_inc(od_zeroed.sem, 1)

        @block.scalar
        def _(act):
            act.wait_ge(*zeroed.first(1))
            act.wait_ge(*loaded.first(1))

            def group_norm(here):
                act.wait_ge(*here.filled("gvar"))
                act.activation(MV[:, 6:7], here.area("gvar")[:, 0:1], ACT.Sqrt, bias=EPS[:, 0:1])\
                    .then_inc(*here.empty("gvar"))

            def front(here, chunks):
                for n in chunks:
                    key = ("t2", n)
                    act.wait_ge(*here.filled(key))
                    act.activation(T2[:, 3 + n * ROWS:3 + (n + 1) * ROWS, 2:2 + W],
                                   here.area(key)[:, 0:PIX].rearrange("p (h w) -> p h w", w=W),
                                   ACT.Copy).then_inc(*here.empty(key))

            def tokens(here, which, g):
                key, (t, m) = ({1: "yt", 2: "yt2"}[which], g), GROUPS[g]
                act.wait_ge(*here.filled(key))
                src = here.area(key)[:, 0:m * P].rearrange("p (t c) -> p t c", c=P)
                full = m if g < NG - 1 else m - 1
                ins = act.activation(UT[which][:, t:t + full, :], src[:, 0:full], ACT.Copy)
                if full < m:
                    ins = act.activation(UT[which][0:LAST, t + full, :], src[0:LAST, full], ACT.Copy)
                ins.then_inc(*here.empty(key))

            def deviations(sums, std, pair, g):
                act.wait_ge(*sums.at(pair, g + 1))
                act.activation(ST[:, g % 2, 2, :], ST[:, g % 2, 1, :], ACT.Sqrt, scale=1.0 / C,
                               bias=EPS[:, 0:1])\
                    .then_inc(std.sem, 1)

            def high_part(pair, g):
                t, m = GROUPS[g]
                act.wait_ge(*un1_ready.at(pair, g + 1))
                act.activation(UHL[:, 2 * t:2 * t + 2 * m, 0, :], UN[1][:, 2 * t:2 * t + 2 * m, :], ACT.Copy)\
                    .then_inc(u_high.sem, 1)

            def split_tokens(here, g):
                for i in range(2):
                    key, (t, m) = ("uts", i, g), GROUPS[g]
                    n = min(S - t * P, m * P)
                    act.wait_ge(*here.filled(key))
                    act.activation(UTS[i][:, t * P:t * P + n], here.area(key)[:, 0:512].bitcast(F16)[:, 0:n],
                                   ACT.Copy).then_inc(*here.empty(key))

            def routing_weights(here):
                for g in range(2):
                    key, m = ("wt", g), (16 if g == 0 else TILES - 16)
                    act.wait_ge(*here.filled(key))
                    src = here.area(key)[:, 0:m * C].rearrange("p (t e) -> p t e", e=C)
                    full = m if g == 0 else m - 1
                    ins = act.activation(WT[:, 16 * g:16 * g + full, :], src[:, 0:full], ACT.Copy)
                    if full < m:
                        ins = act.activation(WT[0:LAST, 16 * g + full, :], src[0:LAST, full], ACT.Copy)
                    ins.then_inc(*here.empty(key))

            def back(here, pair, routing):
                for g, (j, m) in enumerate(COLGROUPS):
                    key = ("ucol", g)
                    act.wait_ge(*here.filled(key))
                    act.activation(UCOL[0:HALFP, j:j + m, :],
                                   here.area(key)[0:HALFP, 0:m * P].rearrange("p (j c) -> p j c", c=P),
                                   ACT.Copy).then_inc(*here.empty(key))
                if routing:
                    shares(here)
                    routing_weights(here)
                for g in range(2):
                    tokens(here, 1, g)
                    if g == 1:
                        split_tokens(here, 0)
                    deviations(ln1_sums, ln1_std, pair, g)
                    high_part(pair, g)

            def shares(here):
                act.wait_ge(*lmax_ready.at(here.pair, 1))
                act.activation(EW, LG, ACT.Exp, bias=MX[:, 8:9], accum_out=MX[:, 9:10])\
                    .then_inc(exp_ready.sem, 1)
                act.wait_ge(*l2_ready.at(here.pair, 1))
                act.activation(L2, L2, ACT.Exp, bias=MX[:, 8:9]).then_inc(exp_ready.sem, 1)

            def products_out(here, i):
                for b in range(1 + i):
                    key = ("kv", i, b)
                    wide = FEAT // (1 + i)
                    act.wait_ge(*here.filled(key))
                    act.activation(AT[i][:, b * wide:(b + 1) * wide], here.area(key)[:, 0:wide], ACT.Copy)\
                        .then_inc(*here.empty(key))

            def pair_of_images(here):
                pair = here.pair
                for k in range(KTILES):
                    r = tile_rows(k % TILES)
                    act.wait_ge(*here.filled(("kp", k)))
                    act.activation(E[0:r, k % 2], here.area(("kp", k))[0:r, :], ACT.Exp,
                                   bias=NEG1[0:r, 0:1]).then_inc(e_ready.sem, 1)
                    if k in YT_TILES:
                        tokens(here, 1, YT_TILES.index(k))
                    if k == STD_TILE:
                        for g in (2, 3):
                            deviations(ln1_sums, ln1_std, pair, g)
                    if k in SPLIT_TILES:
                        high_part(pair, SPLIT_TILES.index(k))
                    if k in UTS_TILES:
                        split_tokens(here, UTS_TILES.index(k))
                    if k == VAR_TILE and here.span == "loop":
                        group_norm(here)
                    if k == TILES + 2:
                        products_out(here, 0)
                products_out(here, 1)
                for s in range(STEPS + 3):
                    for cc in range(4):
                        if s < STEPS:
                            key = ("qp", s, cc)
                            act.wait_ge(*here.filled(key))
                            act.activation(EQ[:, cc % 2], here.area(key)[:, :]
                                           .rearrange("p (c n) -> p c n", c=2)[:, :, 0:PIX],
                                           ACT.Exp, bias=NEG1[:, 0:1]).then_inc(eq_ready.sem, 1)
                        if cc == 0 and s - 2 in LN2_STEPS[:2]:
                            deviations(ln2_sums, ln2_std, pair, LN2_STEPS.index(s - 2))
                    if here.span == "loop":
                        front(here, FRONT_STEPS.get(s, ()))
                    if s in LN2_STEPS:
                        tokens(here, 2, LN2_STEPS.index(s))
                deviations(ln2_sums, ln2_std, pair, NG - 2)
                deviations(ln2_sums, ln2_std, pair, NG - 1)
                if here.span == "loop":
                    front(here, range(FRONT_REST, NPIX))
                for g, (t, m) in enumerate(GROUPS):
                    key, n = ("u2", g), min(S - t * P, m * P)
                    act.wait_ge(*here.filled(key))
                    act.activation(U2[:, t * P:t * P + n], here.area(key)[:, 0:n], ACT.Copy)\
                        .then_inc(*here.empty(key))
                for n in range(NPIX):
                    key = ("lg", n)
                    act.wait_ge(*here.filled(key))
                    act.activation(LG[:, n * PIX:(n + 1) * PIX], here.area(key)[0:C, 0:PIX], ACT.Identity,
                                   bias=GBC[:, 0:1]).then_inc(*here.empty(key))
                if here.span == "loop":
                    back(here, pair + 1, True)
                else:
                    shares(here)
                    routing_weights(here)

            start = Here("setup")
            act.wait_ge(*zeroed.first(2))
            group_norm(start)
            front(start, range(NPIX))
            back(start, 0, False)
            with act.Fori(0, PAIRS - 1) as pair:
                pair_of_images(Here("loop", pair))
            pair_of_images(Here("last", PAIRS - 1))
            end = Here("final")
            act.wait_ge(*end.filled("hid"))
            act.activation(HID, end.area("hid")[:, :].rearrange("p (a e b) -> p a e b", a=2, b=IMAGES),
                           ACT.Gelu).then_inc(*end.empty("hid"))

        @block.vector
        def _(dve):
            links = [0]
            now = [vstep.first]

            def link(ins):
                links[0] += 1
                ins.then_inc(vstep.sem, 1)
                dve.wait_ge(*now[0](links[0]))

            for a in "DE":
                dve.sem_inc(emptied_s[a].sem, 1)
            dve.wait_ge(*zeroed.first(1))
            dve.wait_ge(*loaded.first(1))
            for n, one in (("k", 1.0), ("q", 1.0), ("v", 0.0)):
                w = WNAT[n]
                link(dve.tensor_copy(ST[:, 0, 0, 0:NCHUNK], w[:, :, 0, C - 1]))
                link(dve.tensor_tensor(out=w[:, :, 0, :], in0=w[:, :, 0, :], op=ALU.subtract,
                                       in1=ST[:, 0, 0, 0:NCHUNK].unsqueeze(2).broadcast_to([P, NCHUNK, C])))
                link(dve.tensor_scalar(w[:, :, 0, C - 1], WB[n], one, None, ALU.add))
                dve.tensor_copy(w[:, :, 1, :], w[:, :, 0, :]).then_inc(prepared.sem, 1)
            for k in range(3):
                for i in range(2):
                    half = slice(i * C, (i + 1) * C)
                    link(dve.tensor_copy(W2B[half, k, i, :], W2N[half, :, k]))
            dve.tensor_copy(IDH[:, :], IDN[:, :]).then_inc(prepared.sem, 1)
            link(dve.tensor_scalar(D7[:, :], IDN[:, :], W7C[:, 2:3], None, ALU.mult))
            for k in range(7):
                link(dve.tensor_tensor(out=P9T[:, k, :].rearrange("p (s b) -> p s b", s=2), op=ALU.mult,
                                       in0=MASK.rearrange("p (s b) -> p s b", s=2),
                                       in1=P9N[:, k, :].unsqueeze(1).broadcast_to([P, 2, C])))
            link(dve.tensor_tensor(out=DIAG, op=ALU.mult, in0=IDN[:, :].unsqueeze(1).broadcast_to([P, DIAGONALS, P]),
                                   in1=W8C[:, 25 - DIAGONALS:].unsqueeze(2).broadcast_to([P, DIAGONALS, P])))
            for m in range(3):
                rows = slice(32 * m, 32 * m + 32)
                for j in range(2):
                    at = 32 * m + HEADS * j
                    link(dve.tensor_copy(SELB[rows, j], IDN[rows, at:at + HEADS].unsqueeze(2)
                                         .broadcast_to([32, HEADS, C])))
                    link(dve.tensor_tensor(out=SEL[:, j, m, j, :], in0=IDN[:, 0:HEADS],
                                           in1=IDN[:, C:C + HEADS], op=ALU.add))
            link(dve.tensor_tensor(out=FOLD[:, :], in0=IDN[:, 0:C], in1=IDN[:, C:P], op=ALU.add))
            link(dve.tensor_copy(BD[:, :, P], IDN[:, C - 1:C].broadcast_to([P, HEADS])))
            link(dve.tensor_copy(BD[:, :, P + 1], IDN[:, P - 1:P].broadcast_to([P, HEADS])))
            start = Here("setup")
            for n, hi, lo in (("wk", WKH, WKL), ("wq", WQH, WQL)):
                dve.wait_ge(*start.filled(n))
                link(dve.tensor_copy(hi[:, :], start.area(n)[:, :]))
                dve.tensor_tensor(out=lo[:, :], in0=start.area(n)[:, :], in1=hi[:, :], op=ALU.subtract)\
                    .then_inc(*start.empty(n))
            dve.wait_ge(*start.filled("wd"))
            dve.tensor_copy(WDT, start.area("wd")[:, 0:NCHUNK * C].rearrange("p (c o) -> p c o", o=C))\
                .then_inc(*start.empty("wd"))
            dve.wait_ge(*start.filled("vd"))
            for s in range(2):
                vd = start.area("vd")[:, s * 512:(s + 1) * 512].rearrange("p (h o) -> p h o", o=C)
                link(dve.tensor_copy(BD[0:C, s:HEADS:2, 0:C], vd[0:C]))
                ins = dve.tensor_copy(BD[C:P, s:HEADS:2, C:P], vd[C:P])
            ins.then_inc(*start.empty("vd"))
            dve.wait_ge(*start.filled("w2"))
            dve.tensor_copy(W2T[:, :, :], start.area("w2")[:, 0:3 * P].rearrange("p (k o) -> p k o", k=3))\
                .then_inc(*start.empty("w2"))
            dve.wait_ge(*start.filled("gw"))
            dve.tensor_copy(GWT[:, :], start.area("gw")[:, 0:C]).then_inc(*start.empty("gw"))
            dve.wait_ge(*zeroed.first(2))

            def group_norm(pair, n):
                if n == 0:
                    dve.wait_ge(*x_loaded.at(pair, 1))
                dve.bn_stats(out=BS[:, n, :], in_=X[:, n * PIX:(n + 1) * PIX]).then_inc(stats.sem, 1)
                if n == NPIX - 1:
                    dve.wait_ge(*stats.at(pair, NPIX))
                    passed(dve)
                    dve.bn_aggr(out=MV[:, 0:2], in_=BS[:, :, :]).then_inc(gn_mean.sem, 1)

            def group_norm_variance(here):
                dve.wait_ge(*here.filled("gmean"))
                link(dve.tensor_copy(MV[:, 2:3], here.area("gmean")[:, 0:1]))
                link(dve.tensor_tensor(out=MV[:, 3:4], in0=MV[:, 0:1], in1=MV[:, 2:3], op=ALU.subtract))
                link(dve.tensor_tensor(out=MV[:, 4:5], in0=MV[:, 3:4], in1=MV[:, 3:4], op=ALU.mult))
                dve.tensor_tensor(out=MV[:, 5:6], in0=MV[:, 4:5], in1=MV[:, 1:2], op=ALU.add)\
                    .then_inc(*here.empty("gmean"))

            def group_norm_apply(here):
                dve.wait_ge(*here.emptied("gvar"))
                link(dve.reciprocal(MV[:, 7:8], MV[:, 6:7]))
                dve.tensor_scalar(g_window(4, 0, H), X.rearrange("p (h w) -> p h w", w=W),
                                  MV[:, 2:3], MV[:, 7:8], ALU.subtract, ALU.mult).then_inc(g_ready.sem, 1)

            piece = [0]

            def depthwise(here, pair, count):
                first = here.span == "setup"
                taps = FIRST_TAPS if first else TAPS
                end = min(piece[0] + count, len(taps) * NPIX)
                for m in range(piece[0], end):
                    (which, k), n = taps[m // NPIX], m % NPIX
                    if m >= NPIX:
                        dve.wait_ge(*(taps_done.first(m - NPIX + 1) if first
                                      else taps_done.at(pair, m - NPIX + 1)))
                    elif m == 0:
                        dve.wait_ge(*g_ready.at(pair, 1))
                    if which == 8:
                        window, w = g_window(n * ROWS + 2 * (k // 5), 2 * (k % 5) - 4, ROWS), W8C
                    else:
                        window, w = T2[:, n * ROWS + 3:(n + 1) * ROWS + 3, k:k + W], W7C
                        if k == 0:
                            dve.wait_ge(*here.emptied(("t2", n)))
                    chunk = X[:, n * PIX:(n + 1) * PIX].rearrange("p (h w) -> p h w", w=W)
                    dve.scalar_tensor_tensor(out=chunk, in0=window, scalar=w[:, k:k + 1], in1=chunk,
                                             op0=ALU.mult, op1=ALU.add).then_inc(taps_done.sem, 1)
                piece[0] = end

            def taps(here):
                dve.wait_ge(*here.filled("t3"))
                t3 = here.area("t3")[:, :].rearrange("p (i c) -> p i c", i=4)
                link(dve.tensor_copy(OS[:, 0:3 * P], here.area("t3")[:, P:4 * P]))
                for i in range(4):
                    k = 3 - i
                    ins = dve.scalar_tensor_tensor(out=L10[:, k, :], in0=t3[:, i, :], scalar=P6[:, k:k + 1],
                                                   in1=P9T[:, k, :], op0=ALU.mult, op1=ALU.mult)
                link(ins)
                dve.tensor_tensor(out=L10[:, 3, :], in0=L10[:, 3, :], in1=D7[:, :], op=ALU.add)\
                    .then_inc(*here.empty("t3"))
                dve.wait_ge(*here.filled("t3t"))
                for i in range(1, 4):
                    k = 3 + i
                    ins = dve.scalar_tensor_tensor(
                        out=L10[:, k, :], in0=here.area("t3t")[:, (i - 1) * P:i * P], scalar=P6[:, k:k + 1],
                        in1=P9T[:, k, :], op0=ALU.mult, op1=ALU.mult)
                ins.then_inc(*here.empty("t3t"))

            def conv_residual(here, pair, n):
                dve.wait_ge(*here.filled(("conv", n)))
                if n == 0:
                    dve.wait_ge(*(taps_done.first(FIRST_PIECES) if here.span == "setup"
                                  else taps_done.at(pair, PIECES)))
                cut = slice(n * PIX, (n + 1) * PIX)
                dve.tensor_tensor(out=Y[:, cut], in0=here.area(("conv", n))[:, 0:PIX], in1=X[:, cut],
                                  op=ALU.add).then_inc(*here.empty(("conv", n)))

            def norm_part(here, which, sums, g, part):
                t, m = GROUPS[g]
                u = UN[which][:, 2 * t:2 * t + 2 * m, :]
                st = ST[:, g % 2, :, 0:2 * m]
                if part == 0:
                    dve.wait_ge(*here.emptied(({1: "yt", 2: "yt2"}[which], g)))
                    link(dve.tensor_reduce(out=st[:, 0], in_=u, axis=AX.X, op=ALU.add))
                    link(dve.tensor_scalar(st[:, 3], st[:, 0], 1.0 / C, None, ALU.mult))
                elif part == 1:
                    link(dve.tensor_tensor(out=u, in0=u, in1=st[:, 3].unsqueeze(2).broadcast_to([P, 2 * m, C]),
                                           op=ALU.subtract))
                elif part == 2:
                    link(dve.tensor_tensor(out=SQ[:, 0:2 * m, :], in0=u, in1=u, op=ALU.mult))
                else:
                    dve.tensor_reduce(out=st[:, 1], in_=SQ[:, 0:2 * m, :], axis=AX.X, op=ALU.add)\
                        .then_inc(sums.sem, 1)

            def norm_sums(here, which, sums, g):
                for part in range(4):
                    norm_part(here, which, sums, g, part)

            def norm_scale(which, std, pair, g):
                t, m = GROUPS[g]
                u = UN[which][:, 2 * t:2 * t + 2 * m, :]
                st = ST[:, g % 2, :, 0:2 * m]
                dve.wait_ge(*std.at(pair, g + 1))
                link(dve.reciprocal(st[:, 3], st[:, 2]))
                return dve.tensor_tensor(out=u, in0=u, op=ALU.mult,
                                         in1=st[:, 3].unsqueeze(2).broadcast_to([P, 2 * m, C]))

            def norm1_scale(pair, g):
                t, m = GROUPS[g]
                link(norm_scale(1, ln1_std, pair, g))
                dve.memset(UN[1][:, 2 * t:2 * t + 2 * m, C - 1:C], 1.0).then_inc(un1_ready.sem, 1)

            def low_part(pair, g):
                t, m = GROUPS[g]
                dve.wait_ge(*u_high.at(pair, g + 1))
                dve.tensor_tensor(out=UHL[:, 2 * t:2 * t + 2 * m, 1, :], op=ALU.subtract,
                                  in0=UN[1][:, 2 * t:2 * t + 2 * m, :],
                                  in1=UHL[:, 2 * t:2 * t + 2 * m, 0, :]).then_inc(u_split.sem, 1)

            def routing(here):
                for w in here.all_emptied([("lg", n) for n in range(NPIX)]):
                    dve.wait_ge(*w)
                passed(dve)
                link(dve.max(out=MX[:, 0:8], in_=LG))
                dve.tensor_scalar(MX[:, 8:9], MX[:, 0:1], -1.0, None, ALU.mult).then_inc(lmax_ready.sem, 1)
                dve.match_replace(out=L2, in_to_replace=MX[:, 0:8], in_values=LG, imm_value=LOW)\
                    .then_inc(l2_ready.sem, 1)

            def shares(here):
                dve.wait_ge(*exp_ready.at(here.pair, 2))
                link(dve.tensor_tensor(out=EW, in0=EW, in1=L2, op=ALU.subtract))
                link(dve.reciprocal(MX[:, 10:11], MX[:, 9:10]))
                dve.tensor_scalar(EW, EW, MX[:, 10:11], None, ALU.mult).then_inc(w_ready.sem, 1)

            def pooled(here):
                dve.wait_ge(*here.filled("pool"))
                for i in range(2):
                    ins = dve.tensor_copy(
                        PT[0:C, :, bass.ds(2 * here.pair + i, 1)].rearrange("p e a -> p (e a)"),
                        here.area("pool")[i * C:(i + 1) * C, i * EXPERTS:(i + 1) * EXPERTS])
                ins.then_inc(*here.empty("pool"))

            def back(here, pair, before):
                if before is not None:
                    routing(here)
                    depthwise(here, pair, 12)
                    shares(here)
                if before is not None:
                    depthwise(here, pair, PIECES)
                else:
                    depthwise(here, pair, 90)
                taps(here)
                if before is None:
                    depthwise(here, pair, PIECES)
                if before is not None:
                    dve.wait_ge(*t_stored.at(before, 1))
                    pooled(here)
                for n in range(NPIX):
                    conv_residual(here, pair, n)
                    if n in (2, 4):
                        norm_sums(here, 1, ln1_sums, n // 2 - 1)
                        norm1_scale(pair, n // 2 - 1)
                        low_part(pair, n // 2 - 1)

            def k_features(here, k):
                r, key = tile_rows(k % TILES), ("kp", k)
                dve.wait_ge(*e_ready.at(here.pair, k + 1))
                if k == 0:
                    dve.wait_ge(*w_stored.at(here.pair, 0))
                if k >= 3:
                    dve.wait_ge(*products_done(k - 3, here))
                dve.scalar_tensor_tensor(out=KT[0:r, k % 3], in0=E[0:r, k % 2], scalar=1.0,
                                         in1=here.area(key)[0:r, :], op0=ALU.min, op1=ALU.max)\
                    .then_inc(*here.empty(key))

            def head_matrices(here, i):
                for g in range(2):
                    key = ("m", i, g)
                    dve.wait_ge(*here.filled(key))
                    m = here.area(key)[:, :].rearrange("p (c n) -> p c n", n=256)
                    dve.tensor_copy(MW[i][:, 4 * g:4 * g + 4, :], m[:, :, 0:P])
                    for hh in range(2):
                        for cs in range(2):
                            half = slice(hh * C, (hh + 1) * C)
                            first = 4 * g * (DROWS + 2) + cs * C + hh
                            ins = dve.tensor_copy(
                                KKF[i][half, first:first + 3 * (DROWS + 2) + 1:DROWS + 2], m[half, :, P + cs])
                    ins.then_inc(*here.empty(key))

            def q_features(here, s, cc):
                n, key = 4 * s + cc, ("qp", s, cc)
                dve.wait_ge(*eq_ready.at(here.pair, n + 1))
                if s >= 3 and cc == 0:
                    dve.wait_ge(*here.filled(("out", s - 3)))
                dve.scalar_tensor_tensor(
                    out=Q[s % 3][:, 2 * cc:2 * cc + 2, :], in0=EQ[:, cc % 2], scalar=1.0,
                    in1=here.area(key)[:, :].rearrange("p (c n) -> p c n", c=2)[:, :, 0:PIX],
                    op0=ALU.min, op1=ALU.max).then_inc(*here.empty(key))

            def q_scale(here, s, cc):
                key = ("rb", s, cc)
                q = Q[s % 3][:, 2 * cc:2 * cc + 2, :]
                dve.wait_ge(*here.filled(key))
                dve.tensor_tensor(out=q, in0=q, op=ALU.mult,
                                  in1=here.area(key)[:, :].rearrange("p (c n) -> p c n", c=2)[:, :, 0:PIX])\
                    .then_inc(*here.empty(key))

            def den_parts(here, s):
                n = s % NPIX
                dve.wait_ge(*here.filled(("den", s)))
                dve.tensor_tensor(out=DS[:, :], in0=here.area(("den", s))[0:DROWS, 0:PIX],
                                  in1=CST[0:DROWS, n * PIX:(n + 1) * PIX], op=ALU.mult)\
                    .then_inc(*here.empty(("den", s)))

            def den_guard(here, s):
                dve.wait_ge(*here.filled(("dsum", s)))
                dve.tensor_scalar(RR[:, 0], here.area(("dsum", s))[0:96, 0:SUB], DEN_EPS, None, ALU.add)\
                    .then_inc(*here.empty(("dsum", s)))

            def den_reciprocal(here, s):
                dve.wait_ge(*here.emptied(("dsum", s)))
                if s >= 1:
                    dve.wait_ge(*split_ready.at(here.pair, s))
                dve.reciprocal(RR[:, 1], RR[:, 0]).then_inc(recip_ready.sem, 1)

            def out_parts(here, s):
                n = s % NPIX
                dve.wait_ge(*here.filled(("out", s)))
                dve.tensor_tensor(out=OS[:, :], in0=here.area(("out", s))[:, 0:PIX],
                                  in1=CST[:, n * PIX:(n + 1) * PIX], op=ALU.mult)\
                    .then_inc(*here.empty(("out", s)))

            def out_residual(here, s):
                i, n = divmod(s, NPIX)
                cut, half = slice(n * PIX, (n + 1) * PIX), slice(i * C, (i + 1) * C)
                dve.wait_ge(*here.filled(("fold", s)))
                dve.scalar_tensor_tensor(out=Y[half, cut], in0=here.area(("fold", s))[half, 0:PIX],
                                         scalar=DBC[half, 0:1], in1=Y[half, cut], op0=ALU.add, op1=ALU.add)\
                    .then_inc(*here.empty(("fold", s)))

            def pair_of_images(here):
                pair = here.pair
                conv = here.span == "loop"
                for k in range(KTILES):
                    k_features(here, k)
                    for g in (2, 3):
                        if 0 <= k - SUM_TILES[g] < 4:
                            norm_part(here, 1, ln1_sums, g, k - SUM_TILES[g])
                    if k in SCALE_TILES:
                        norm1_scale(pair, SCALE_TILES.index(k))
                    if k in SPLIT_TILES:
                        low_part(pair, SPLIT_TILES.index(k))
                    if conv and STATS_TILE <= k < STATS_TILE + NPIX:
                        group_norm(pair + 1, k - STATS_TILE)
                    if conv and k == CENTRE_TILE:
                        group_norm_variance(here)
                    if conv and k == NORM_TILE:
                        group_norm_apply(here)
                    if conv and k > NORM_TILE:
                        depthwise(here, pair + 1, K_PIECES)
                for i in range(2):
                    head_matrices(here, i)
                for s in range(STEPS + 3):
                    feature, scaled = s < STEPS, 2 <= s < STEPS + 2
                    drain = s >= STEPS
                    if 1 <= s <= STEPS:
                        den_parts(here, s - 1)
                    if s >= 3 and drain:
                        out_parts(here, s - 3)
                    for cc in range(5):
                        if scaled and cc >= 2 and not drain:
                            q_scale(here, s - 2, cc - 1)
                        if feature and cc < 4:
                            q_features(here, s, cc)
                        if cc == 0 and s >= 3 and not drain:
                            out_parts(here, s - 3)
                        if scaled and cc == 0:
                            q_scale(here, s - 2, 0)
                        if scaled and drain and cc in (0, 2, 3):
                            q_scale(here, s - 2, max(cc, 1))
                        if cc == 1 and 1 <= s <= STEPS:
                            den_guard(here, s - 1)
                        if cc == 1 and s >= 3 and not drain:
                            out_residual(here, s - 3)
                        if cc == (1 if drain else 2) and 1 <= s <= STEPS:
                            den_reciprocal(here, s - 1)
                        if cc == 1 and drain:
                            out_residual(here, s - 3)
                        if cc < 4 and s - 1 in LN2_STEPS:
                            norm_part(here, 2, ln2_sums, LN2_STEPS.index(s - 1), cc)
                        elif conv:
                            depthwise(here, pair + 1, Q_PIECES[cc])
                        if cc == 2 and s - 2 in LN2_STEPS[:2]:
                            norm_scale(2, ln2_std, pair, LN2_STEPS.index(s - 2)).then_inc(un2_ready.sem, 1)
                norm_sums(here, 2, ln2_sums, NG - 1)
                for g in (NG - 2, NG - 1):
                    norm_scale(2, ln2_std, pair, g).then_inc(un2_ready.sem, 1)
                if conv:
                    depthwise(here, pair + 1, FRONT_PIECES)
                if here.span == "loop":
                    back(here, pair + 1, pair)
                else:
                    routing(here)
                    shares(here)
                    pooled(here)

            for n in range(NPIX):
                group_norm(0, n)
            group_norm_variance(start)
            group_norm_apply(start)
            back(start, 0, None)
            assert links[0] == VSETUP, links[0]
            with dve.Fori(0, PAIRS - 1) as pair:
                links[0] = piece[0] = 0
                now[0] = lambda n: vstep.at(pair, n)
                pair_of_images(Here("loop", pair))
                assert links[0] == VLOOP, links[0]
            links[0] = 0
            now[0] = lambda n: vstep.at(PAIRS - 1, n)
            pair_of_images(Here("last", PAIRS - 1))

            end = Here("final")
            dve.memset(ONES, 1.0).then_inc(ones_ready.sem, 1)
            for g in range(2):
                dve.wait_ge(*end.filled(("eo", g)))
                dve.tensor_copy(EO[:, 16 * g:16 * g + 16, :],
                                end.area(("eo", g))[0:IMAGES, :].rearrange("p (e o) -> p e o", o=C))\
                    .then_inc(*end.empty(("eo", g)))
            for k in range(PAIRS):
                b, turns = last_buffer(k)
                if k >= 1:
                    dve.wait_ge(*last_t[b - 1].after(turns))
                for n in range(NPIX):
                    key, cut = ("add", k, n), slice(n * PIX, (n + 1) * PIX)
                    dve.wait_ge(*end.filled(key))
                    dve.tensor_tensor(out=LT[b][:, cut], in0=end.area(key)[:, 0:PIX], in1=LT[b][:, cut],
                                      op=ALU.add).then_inc(*end.empty(key))

        @block.tensor
        def _(pe):
            pe.wait_ge(*zeroed.first(1))
            pe.wait_ge(*loaded.first(1))
            start = Here("setup")
            for m, (n, w) in enumerate((("wk", "k"), ("wq", "q"))):
                pe.wait_ge(*prepared.first(m + 1))
                for c in range(NCHUNK):
                    ins = pe.transpose(start.area(n)[:, c * P:(c + 1) * P],
                                       WNAT[w][:, c].rearrange("p s d -> p (s d)"), IDN[:, :])
                ins.then_inc(*start.fill(n))
            for c in range(NCHUNK):
                ins = pe.transpose(start.area("wd")[:, c * C:(c + 1) * C], DN[:, c * P:(c + 1) * P], IDN[0:C, 0:C])
            ins.then_inc(*start.fill("wd"))
            pe.wait_ge(*prepared.first(4))
            pe.wait_ge(*start.emptied("wd"))
            pe.wait_ge(*start.room("vd"))
            for h in range(HEADS):
                c, half = h // 2, slice(h % 2 * C, (h % 2 + 1) * C)
                at = h % 2 * 512 + c * C
                ins = pe.matmul(start.area("vd")[:, at:at + C],
                                WNAT["v"][half, c].rearrange("p s d -> p (s d)"), WDT[half, c, :],
                                start=True, stop=True)
            ins.then_inc(*start.fill("vd"))
            pe.wait_ge(*start.room("w2"))
            for k in range(3):
                ins = pe.transpose(start.area("w2")[:, k * P:(k + 1) * P],
                                   W2B[:, k].rearrange("p s i -> p (s i)"), IDN[:, :])
            ins.then_inc(*start.fill("w2"))
            pe.wait_ge(*start.room("gw"))
            pe.transpose(start.area("gw")[:, 0:C], GWB, IDN[0:C, 0:C]).then_inc(*start.fill("gw"))
            pe.wait_ge(*start.emptied("gw"))

            def group_norm(here, pair, key):
                pe.wait_ge(*(gn_mean.at(pair, 1) if key == "gmean" else here.emptied("gmean")))
                pe.wait_ge(*here.room(key))
                column = MV[:, 0:1] if key == "gmean" else MV[:, 5:6]
                pe.matmul(here.area(key)[:, 0:1], AVG[:, :], column, start=True, stop=True)\
                    .then_inc(*here.fill(key))

            def front(here, pair, chunks):
                for n in chunks:
                    if n == 0:
                        pe.wait_ge(*g_ready.at(pair, 1))
                    key = ("t2", n)
                    pe.wait_ge(*here.room(key))
                    for k in range(3):
                        ins = pe.matmul(here.area(key)[:, 0:PIX], W2T[:, k, :],
                                        g_window(4 + n * ROWS, k - 1, ROWS), start=k == 0, stop=k == 2)
                    ins.then_inc(*here.fill(key))

            def correlations(here):
                for g, (j, m) in enumerate(COLGROUPS):
                    key = ("ucol", g)
                    pe.wait_ge(*here.room(key))
                    for a in range(m):
                        at = 4 + 4 * PITCH + j + a
                        ins = pe.transpose(here.area(key)[0:HALFP, a * P:(a + 1) * P],
                                           G[:, at:at + (HALFP - 1) * SPLIT + 1:SPLIT], IDN[:, :])
                    ins.then_inc(*here.fill(key))
                for w in here.all_emptied([("ucol", g) for g in range(len(COLGROUPS))]):
                    pe.wait_ge(*w)
                pe.wait_ge(*here.room("t3"))
                for j in range(SPLIT):
                    ins = pe.matmul(here.area("t3")[:, :], UCOL[0:HALFP, j, :], UCOL[0:HALFP, j:j + 7:2, :],
                                    start=j == 0, stop=j == SPLIT - 1)
                ins.then_inc(*here.fill("t3"))

            def turned_correlations(here):
                pe.wait_ge(*here.emptied("t3"))
                pe.wait_ge(*here.room("t3t"))
                for i in range(3):
                    ins = pe.transpose(here.area("t3t")[:, i * P:(i + 1) * P], OS[:, i * P:(i + 1) * P],
                                       IDN[:, :])
                ins.then_inc(*here.fill("t3t"))

            def conv(here, n):
                key, row = ("conv", n), n * ROWS
                pe.wait_ge(*here.room(key))
                acc, first = here.area(key)[:, 0:PIX], here.span == "setup"
                for j in range(DIAGONALS if first else 0):
                    k = 25 - DIAGONALS + j
                    pe.matmul(acc, DIAG[:, j, :], g_window(row + 2 * (k // 5), 2 * (k % 5) - 4, ROWS),
                              start=j == 0, stop=False)
                if n == 0:
                    pe.wait_ge(*here.emptied("t3t"))
                    for w in here.all_emptied([("t2", m) for m in range(NPIX)]):
                        pe.wait_ge(*w)
                for k in range(7):
                    ins = pe.matmul(acc, L10[:, k, :], T2[:, row + k:row + k + ROWS, 2:2 + W],
                                    start=k == 0 and not first, stop=k == 6)
                ins.then_inc(*here.fill(key))

            def to_tokens(here, which, g):
                key, (t, m) = ({1: "yt", 2: "yt2"}[which], g), GROUPS[g]
                pe.wait_ge(*here.room(key))
                passed(pe)
                for a in range(m):
                    r, at = tile_rows(t + a), (t + a) * P
                    ins = pe.transpose(here.area(key)[0:r, a * P:(a + 1) * P], Y[:, at:at + r], IDN[:, :])
                ins.then_inc(*here.fill(key))

            def split_tokens(here, pair, g):
                pe.wait_ge(*u_split.at(pair, g + 1))
                for i in range(2):
                    key, (t, m) = ("uts", i, g), GROUPS[g]
                    pe.wait_ge(*here.room(key))
                    passed(pe)
                    half = here.area(key)[:, 0:512].bitcast(F16)
                    for a in range(m):
                        r = tile_rows(t + a)
                        ins = pe.transpose(half[:, a * P:a * P + r],
                                           UHL[0:r, 2 * (t + a) + i].rearrange("p s c -> p (s c)"), IDH[0:r, 0:r])
                    ins.then_inc(*here.fill(key))

            def routing_weights(here):
                pe.wait_ge(*w_ready.at(here.pair, 1))
                for g in range(2):
                    key = ("wt", g)
                    pe.wait_ge(*here.room(key))
                    passed(pe)
                    for t in range(16 * g, min(16 * g + 16, TILES)):
                        r = tile_rows(t)
                        ins = pe.transpose(here.area(key)[0:r, t % 16 * C:(t % 16 + 1) * C],
                                           EW[:, t * P:t * P + r], IDN[0:C, 0:C])
                    ins.then_inc(*here.fill(key))

            def pool_tokens(here):
                for w in here.all_emptied([("wt", 0), ("wt", 1)]):
                    pe.wait_ge(*w)
                pe.wait_ge(*here.room("pool"))
                for t in range(TILES):
                    r = tile_rows(t)
                    ins = pe.matmul(here.area("pool")[:, 0:C], UT[2][0:r, t, :], WT[0:r, t, :],
                                    start=t == 0, stop=t == TILES - 1)
                ins.then_inc(*here.fill("pool"))

            def back(here, pair, routing):
                correlations(here)
                if routing:
                    routing_weights(here)
                turned_correlations(here)
                if routing:
                    pool_tokens(here)
                for n in range(NPIX):
                    conv(here, n)
                    if n in (2, 4):
                        for w in here.all_emptied([("conv", m) for m in range(n)]):
                            pe.wait_ge(*w)
                        passed(pe)
                        to_tokens(here, 1, n // 2 - 1)
                    if n == 4:
                        split_tokens(here, pair, 0)

            def k_project(here, k):
                key, (i, t) = ("kp", k), divmod(k, TILES)
                r = tile_rows(t)
                if i == 0 and t in [g for g, _ in GROUPS[1:]]:
                    for w in here.all_emptied([("uts", j, t // GROUP) for j in range(2)]):
                        pe.wait_ge(*w)
                pe.wait_ge(*here.room(key))
                for n in range(2):
                    cut = slice(n * 512, (n + 1) * 512)
                    for m, w in enumerate((WKH, WKL)):
                        ins = pe.matmul(here.area(key)[0:r, cut], UTS[i][:, t * P:t * P + r], w[:, cut],
                                        start=m == 0, stop=m == 1)
                ins.then_inc(*here.fill(key))

            def k_products(here, k):
                i, t = divmod(k, TILES)
                r = tile_rows(t)
                if t == 0:
                    for b in range(1 + i):
                        pe.wait_ge(*here.room(("kv", i, b)))
                pe.wait_ge(*here.emptied(("kp", k)))
                pe.wait_ge(*ua_ready.at(here.pair, k + 1))
                for n in range(2):
                    dst = here.area(("kv", 0, 0))[:, n * 512:(n + 1) * 512] if i == 0 \
                        else here.area(("kv", 1, n))[:, :]
                    ins = pe.matmul(dst, UA[0:r, k % 3].rearrange("p s c -> p (s c)"),
                                    KT[0:r, k % 3, n * 512:(n + 1) * 512],
                                    start=t == 0, stop=t == TILES - 1)
                    if t == TILES - 1 and (i or n):
                        ins.then_inc(*here.fill(("kv", i, n if i else 0)))
                if t < TILES - 1:
                    ins.then_inc(kv_used.sem, 1)

            def head_matrices(here, i):
                for b in range(1 + i):
                    pe.wait_ge(*here.emptied(("kv", i, b)))
                for g in range(2):
                    key = ("m", i, g)
                    pe.wait_ge(*here.room(key))
                    for h in range(8 * g, 8 * g + 8):
                        c = h // 2 % 4
                        half = slice(h % 2 * C, (h % 2 + 1) * C)
                        ins = pe.matmul(here.area(key)[half, c * 256:c * 256 + P + 2],
                                        AT[i][:, h * C:(h + 1) * C], BD[:, h, :], start=True, stop=True)
                    ins.then_inc(*here.fill(key))

            def q_project(here, s, cc):
                i, n = divmod(s, NPIX)
                key = ("qp", s, cc)
                pe.wait_ge(*here.room(key))
                for a in range(2):
                    c = 2 * cc + a
                    for m, w in enumerate((WQH, WQL)):
                        ins = pe.matmul(here.area(key)[:, a * 512:a * 512 + PIX], w[:, c * P:(c + 1) * P],
                                        UTS[i][:, n * PIX:(n + 1) * PIX], start=m == 0, stop=m == 1)
                ins.then_inc(*here.fill(key))

            def q_denominators(here, s, cc):
                key, i = ("den", s), s // NPIX
                if cc == 0:
                    pe.wait_ge(*here.room(key))
                    if s % NPIX == 0:
                        for w in here.all_emptied([("m", i, 0), ("m", i, 1)]):
                            pe.wait_ge(*w)
                pe.wait_ge(*here.emptied(("qp", s, cc)))
                for c in (2 * cc, 2 * cc + 1):
                    ins = pe.matmul(here.area(key)[0:DROWS, 0:PIX], KK[i][:, c, :], Q[s % 3][:, c, :],
                                    start=c == 0, stop=c == NCHUNK - 1)
                if cc == 3:
                    ins.then_inc(*here.fill(key))

            def q_sums(here, s):
                key = ("dsum", s)
                pe.wait_ge(*here.emptied(("den", s)))
                pe.wait_ge(*here.room(key))
                for j in range(2):
                    ins = pe.matmul(here.area(key)[0:96, 0:SUB],
                                    SEL[0:DROWS, j].rearrange("p m d h -> p (m d h)"),
                                    DS[:, j * SUB:(j + 1) * SUB], start=j == 0, stop=j == 1)
                ins.then_inc(*here.fill(key))

            def q_broadcast(here, s, cc):
                key = ("rb", s, cc)
                pe.wait_ge(*split_ready.at(here.pair, s + 1))
                pe.wait_ge(*here.room(key))
                for a in range(2):
                    c = 2 * cc + a
                    for j in range(2):
                        at = a * 512 + j * SUB
                        ins = pe.matmul(here.area(key)[:, at:at + SUB],
                                        SELB[:, j, 2 * c:2 * c + 2, :].rearrange("p h c -> p (h c)"),
                                        RS3[:, s % 2], start=True, stop=True)
                ins.then_inc(*here.fill(key))

            def q_output(here, s, cc):
                key, i = ("out", s), s // NPIX
                if cc == 0:
                    pe.wait_ge(*here.room(key))
                pe.wait_ge(*here.emptied(("rb", s, cc)))
                for c in (2 * cc, 2 * cc + 1):
                    ins = pe.matmul(here.area(key)[:, 0:PIX], MW[i][:, c, :], Q[s % 3][:, c, :],
                                    start=c == 0, stop=c == NCHUNK - 1)
                if cc == 3:
                    ins.then_inc(*here.fill(key))

            def q_fold(here, s):
                key, i = ("fold", s), s // NPIX
                pe.wait_ge(*here.emptied(("out", s)))
                pe.wait_ge(*here.room(key))
                pe.matmul(here.area(key)[i * C:(i + 1) * C, 0:PIX], FOLD[:, :], OS[:, :],
                          start=True, stop=True).then_inc(*here.fill(key))

            def pair_of_images(here):
                pair = here.pair
                for w in here.all_before():
                    pe.wait_ge(*w)
                for k in range(KTILES + 2):
                    if k < KTILES:
                        k_project(here, k)
                    if k in YT_TILES:
                        to_tokens(here, 1, YT_TILES.index(k))
                    if k >= 2:
                        k_products(here, k - 2)
                    if k in UTS_TILES:
                        split_tokens(here, pair, UTS_TILES.index(k))
                    if here.span == "loop" and k == MEAN_TILE:
                        group_norm(here, pair + 1, "gmean")
                    if here.span == "loop" and k == VAR_TILE:
                        group_norm(here, pair + 1, "gvar")
                for i in range(2):
                    head_matrices(here, i)
                for s in range(STEPS + 3):
                    feature, scaled, drain = s < STEPS, 2 <= s < STEPS + 2, s >= STEPS
                    for cc in range(5):
                        if feature and (cc in (1, 2, 3) or s == 0 and cc == 0):
                            q_project(here, s, cc)
                        if scaled and not drain and cc != 1:
                            q_broadcast(here, s - 2, max(cc - 1, 0))
                        if scaled and drain and cc == 0:
                            for c in range(3):
                                q_broadcast(here, s - 2, c)
                        if cc == 4 and s + 1 < STEPS:
                            q_project(here, s + 1, 0)
                        if feature and cc >= 1:
                            q_denominators(here, s, cc - 1)
                        if cc == 1 and 1 <= s <= STEPS:
                            q_sums(here, s - 1)
                        if scaled and cc >= 1:
                            q_output(here, s - 2, cc - 1)
                        if cc == 1 and s >= 3:
                            q_fold(here, s - 3)
                        if here.span == "loop":
                            front(here, pair + 1, FRONT_STEPS.get(s, ())[max(cc - 1, 0):cc])
                        if scaled and drain and cc == 2:
                            q_broadcast(here, s - 2, 3)
                    if s in LN2_STEPS:
                        to_tokens(here, 2, LN2_STEPS.index(s))
                if here.span == "loop":
                    front(here, pair + 1, range(FRONT_REST, NPIX))
                for g, (t, m) in enumerate(GROUPS):
                    key = ("u2", g)
                    pe.wait_ge(*un2_ready.at(pair, g + 1))
                    pe.wait_ge(*here.room(key))
                    passed(pe)
                    for a in range(m):
                        r = tile_rows(t + a)
                        ins = pe.transpose(here.area(key)[:, a * P:a * P + r], UT[2][0:r, t + a, :],
                                           IDN[0:r, 0:r])
                    ins.then_inc(*here.fill(key))
                for w in here.all_emptied([("u2", g) for g in range(NG)]):
                    pe.wait_ge(*w)
                for n in range(NPIX):
                    key = ("lg", n)
                    pe.wait_ge(*here.room(key))
                    pe.matmul(here.area(key)[0:C, 0:PIX], GWT[:, :], U2[:, n * PIX:(n + 1) * PIX],
                              start=True, stop=True).then_inc(*here.fill(key))
                if here.span == "loop":
                    back(here, pair + 1, True)
                else:
                    routing_weights(here)
                    pool_tokens(here)

            group_norm(start, 0, "gmean")
            group_norm(start, 0, "gvar")
            front(start, 0, range(NPIX))
            back(start, 0, False)
            with pe.Fori(0, PAIRS - 1) as pair:
                pair_of_images(Here("loop", pair))
            pair_of_images(Here("last", PAIRS - 1))

            end = Here("final")
            pe.wait_ge(*w1_loaded.after(1))
            pe.wait_ge(*end.room("hid"))
            pe.wait_ge(*Here("last").emptied("pool"))
            for e in range(EXPERTS):
                for a in range(2):
                    col = (a * EXPERTS + e) * IMAGES
                    ins = pe.matmul(end.area("hid")[:, col:col + IMAGES], W1S[:, e, a * P:(a + 1) * P],
                                    PT[:, e, :], start=True, stop=True)
            ins.then_inc(*end.fill("hid"))
            pe.wait_ge(*end.emptied("hid"))
            pe.wait_ge(*ones_ready.after(1))
            pe.wait_ge(*w2_loaded.after(1))
            for g in range(2):
                key = ("eo", g)
                pe.wait_ge(*end.room(key))
                for e in range(16 * g, 16 * g + 16):
                    dst = end.area(key)[0:IMAGES, e % 16 * C:(e % 16 + 1) * C]
                    for a in range(2):
                        pe.matmul(dst, HID[:, a, e, :], W2S[:, a, e, :], start=a == 0, stop=False)
                    ins = pe.matmul(dst, ONES, B2S[:, e, :], start=False, stop=True)
                ins.then_inc(*end.fill(key))
            pe.wait_ge(*od_loaded.after(1))
            for k in range(PAIRS):
                b = last_buffer(k)[0]
                for due in LDUE[k]:
                    source, turns = last_buffer(due)
                    pe.wait_ge(*last_w[source - 1].after(turns))
                for n in range(NPIX):
                    key = ("add", k, n)
                    pe.wait_ge(*end.room(key))
                    pe.matmul(end.area(key)[:, 0:PIX], OD[:, LAST_ORDER[k], :],
                              LFULL[b][:, n * PIX:(n + 1) * PIX], start=True, stop=True)\
                        .then_inc(*end.fill(key))


VSETUP = 61
VLOOP = 53
LOW = -3.0e38

_INS = ["x", "L0_conv_w2", "L0_conv_p6w", "L0_conv_w7", "L0_conv_w8", "L0_conv_p9w", "L1_attn_wq_w",
        "L1_attn_wq_b", "L1_attn_wk_w", "L1_attn_wk_b", "L1_attn_wv_w", "L1_attn_wv_b", "L1_attn_dense_w",
        "L1_attn_dense_b", "L1_ffn_gate_w", "L1_ffn_gate_b", "L1_ffn_weight1", "L1_ffn_weight2"]


def shape_constants():
    import numpy as np

    ident = np.eye(P, dtype=np.float32)
    channel = np.arange(P)
    avg = np.where(channel[:, None] // 2 == channel[None, :] // 2, 0.5, 0.0).astype(np.float32)
    mask = np.where(channel[:, None] // C == channel[None, :] // C,
                    -1.0 / (np.sqrt(S) * np.sqrt(7 * C)), 0.0).astype(np.float32)
    pos = (np.float32(1.57) * np.arange(S, dtype=np.float32) / np.float32(S)).astype(np.float32)
    cos, sin = np.cos(pos).astype(np.float32), np.sin(pos).astype(np.float32)
    cst = np.concatenate([np.tile(cos, (C, 1)), np.tile(sin, (C, 1))]).astype(np.float32)
    padded = np.zeros((2, TILES * P), np.float32)
    padded[0, :S], padded[1, :S] = cos, sin
    cs = np.ascontiguousarray(padded.reshape(2, TILES, P).transpose(2, 1, 0))
    return {"ident": ident, "avg": avg, "mask": mask, "cst": cst, "cs": cs}


def kernel(**inputs):
    import numpy as np
    import concourse.bacc as bacc
    from concourse.bass_utils import run_bass_kernel_spmd

    nc = bacc.Bacc("TRN2", target_bir_lowering=False, num_devices=1,
                   dynamic_dma_scratch_size=2048)
    arrays, args = {}, []
    for name in _INS:
        arrays[name] = np.ascontiguousarray(inputs[name])
    arrays.update(shape_constants())
    for name, a in arrays.items():
        args.append(nc.dram_tensor(name, a.shape, mybir.dt.from_np(a.dtype), kind="ExternalInput").ap())
    args.append(nc.dram_tensor("out", (IMAGES, C, H, W), F32, kind="ExternalOutput").ap())
    args.append(nc.dram_tensor("t_keep", (IMAGES * C, S), F32, kind="Internal").ap())
    args.append(nc.dram_tensor("w_keep", (IMAGES * EXPERTS, S), F32, kind="Internal").ap())
    args.append(nc.dram_tensor("o_keep", (IMAGES, EXPERTS, C), F32, kind="Internal").ap())
    program(nc, *args)
    r = run_bass_kernel_spmd(nc, [arrays], core_ids=[0])
    return r.results[0]["out"]
```
